# Optimizing a Trainium2 kernel written in Bass

```python
import numpy as np
import jax
import jax.numpy as jnp

def _softmax(x, axis=-1):
    return jax.nn.softmax(x, axis=axis)

def _gelu(x):
    return jax.nn.gelu(x, approximate=True)

def _silu(x):
    return jax.nn.silu(x)

def _sigmoid(x):
    return jax.nn.sigmoid(x)

def _layernorm(x, axis=-1, eps=1e-05):
    m = jnp.mean(x, axis=axis, keepdims=True)
    v = jnp.var(x, axis=axis, keepdims=True)
    return (x - m) / jnp.sqrt(v + eps)

def _scatter_add(tgt, idx, src, axis=0):
    return tgt.at[idx].add(src)

def _segment_sum(src, seg, n):
    return jax.ops.segment_sum(src, seg, n)
kernel_name = 'mk_adj_preln_d4_adj_r2_cf9ea5'

def setup_inputs(seed: int=0):
    np.random.seed(seed)
    _w = jnp.asarray

    def _rec_inputs():
        import jax
        import jax.numpy as jnp
        _gk = jax.random.key(seed)
        x = -0.000929 + 1 * jax.random.normal(jax.random.fold_in(_gk, 1), (8, 2048, 64), jnp.float32)
        _a = jax.random.bernoulli(jax.random.fold_in(_gk, 2), 0.00195312, (8, 2048, 2048))
        _a = jnp.logical_or(_a, jnp.swapaxes(_a, -1, -2))
        _a = jnp.logical_or(_a, jnp.eye(2048, dtype=bool))
        _af = _a.astype(jnp.float32)
        _af = _af * jax.random.uniform(jax.random.fold_in(_gk, 3), (8, 2048, 2048), jnp.float32, 0.05, 1)
        adj = _af
        return (x, adj)
    x, adj = _rec_inputs()

    def _L0_gnn_setup():
        import jax, jax.numpy as jnp
        import numpy as np
        B, N, C, R = (4, 2048, 64, 16)
        EPS = 1e-12
        key = jax.random.key(seed)
        k_x, k_w, k_u = jax.random.split(key, 3)
        x = jax.random.normal(k_x, (B, N, C), dtype=jnp.float32)
        W = jax.random.uniform(k_w, (B, N, N), dtype=jnp.float32)
        U = 0.01 * jax.random.normal(k_u, (N, R), dtype=jnp.float32)
        w_scale = jnp.asarray(1.0, dtype=jnp.float32)
        return {'x': x, 'W': W, 'U': U, 'w_scale': w_scale}
    _L0_gnn_all = _L0_gnn_setup()
    _L0_gnn_in = {k: v for k, v in _L0_gnn_all.items() if k in ('U', 'w_scale')}
    del _L0_gnn_all

    def _L1_gnn_setup():
        import jax, jax.numpy as jnp
        import numpy as np
        ALPHA = 0.2
        NEG_INF = -9000000000000000.0
        key = jax.random.key(seed)
        k1, k2, k3, k4 = jax.random.split(key, 4)
        B, N, F_in, F_out = (32, 512, 64, 64)
        h = jax.random.normal(k1, (B, N, F_in), dtype=jnp.float32)
        adj = (jax.random.uniform(k2, (B, N, N)) < 0.05).astype(jnp.float32)
        adj = jnp.maximum(adj, jnp.eye(N, dtype=jnp.float32)[None])
        W = jax.random.normal(k3, (F_in, F_out), dtype=jnp.float32) * 0.1
        a = jax.random.normal(k4, (2 * F_out, 1), dtype=jnp.float32) * 0.1
        return {'h': h, 'adj': adj, 'W': W, 'a': a}
    _L1_gnn_all = _L1_gnn_setup()
    _L1_gnn_in = {k: v for k, v in _L1_gnn_all.items() if k in ('W', 'a')}
    del _L1_gnn_all

    def _L2_gnn_setup():
        import jax, jax.numpy as jnp
        import numpy as np
        B, N, H = (4, 2048, 64)
        key = jax.random.key(seed)
        ks = jax.random.split(key, 12)
        s = 1.0 / np.sqrt(H)
        h = jax.random.normal(ks[0], (B, N, H), dtype=jnp.float32)
        A = jax.random.uniform(ks[1], (B, N, N), dtype=jnp.float32)
        W1 = jax.random.normal(ks[2], (H, H), dtype=jnp.float32) * s
        b1 = jnp.zeros((H,), dtype=jnp.float32)
        W2 = jax.random.normal(ks[3], (H, H), dtype=jnp.float32) * s
        b2 = jnp.zeros((H,), dtype=jnp.float32)
        W_ih = jax.random.normal(ks[4], (3 * H, H), dtype=jnp.float32) * s
        b_ih = jnp.zeros((3 * H,), dtype=jnp.float32)
        W_hh = jax.random.normal(ks[5], (3 * H, H), dtype=jnp.float32) * s
        b_hh = jnp.zeros((3 * H,), dtype=jnp.float32)
        return {'h': h, 'A': A, 'W1': W1, 'b1': b1, 'W2': W2, 'b2': b2, 'W_ih': W_ih, 'b_ih': b_ih, 'W_hh': W_hh, 'b_hh': b_hh}
    _L2_gnn_all = _L2_gnn_setup()
    _L2_gnn_in = {k: v for k, v in _L2_gnn_all.items() if k in ('W1', 'b1', 'W2', 'b2', 'W_ih', 'b_ih', 'W_hh', 'b_hh')}
    del _L2_gnn_all

    def _L3_gnn_setup():
        import jax, jax.numpy as jnp
        import numpy as np
        B, L, C, OUT = (32, 512, 64, 64)
        BN_EPS = 1e-05
        key = jax.random.key(seed)
        kH, kA, kW = jax.random.split(key, 3)
        H = jax.random.normal(kH, (B, L, C), dtype=jnp.float32)
        A = jax.random.uniform(kA, (B, L, L), dtype=jnp.float32)
        gamma = jnp.ones((C,), jnp.float32)
        beta = jnp.zeros((C,), jnp.float32)
        W = jax.random.normal(kW, (C, OUT), dtype=jnp.float32) * 0.05
        b = jnp.zeros((OUT,), jnp.float32)
        return {'H': H, 'A': A, 'gamma': gamma, 'beta': beta, 'W': W, 'b': b}
    _L3_gnn_all = _L3_gnn_setup()
    _L3_gnn_in = {k: v for k, v in _L3_gnn_all.items() if k in ('gamma', 'beta', 'W', 'b')}
    del _L3_gnn_all
    return {'x': x, 'adj': adj, 'L0_gnn_U': _L0_gnn_in['U'], 'L0_gnn_w_scale': _L0_gnn_in['w_scale'], 'L1_gnn_W': _L1_gnn_in['W'], 'L1_gnn_a': _L1_gnn_in['a'], 'L2_gnn_W1': _L2_gnn_in['W1'], 'L2_gnn_b1': _L2_gnn_in['b1'], 'L2_gnn_W2': _L2_gnn_in['W2'], 'L2_gnn_b2': _L2_gnn_in['b2'], 'L2_gnn_W_ih': _L2_gnn_in['W_ih'], 'L2_gnn_b_ih': _L2_gnn_in['b_ih'], 'L2_gnn_W_hh': _L2_gnn_in['W_hh'], 'L2_gnn_b_hh': _L2_gnn_in['b_hh'], 'L3_gnn_gamma': _L3_gnn_in['gamma'], 'L3_gnn_beta': _L3_gnn_in['beta'], 'L3_gnn_W': _L3_gnn_in['W'], 'L3_gnn_b': _L3_gnn_in['b']}

def reference(x, adj, L0_gnn_U, L0_gnn_w_scale, L1_gnn_W, L1_gnn_a, L2_gnn_W1, L2_gnn_b1, L2_gnn_W2, L2_gnn_b2, L2_gnn_W_ih, L2_gnn_b_ih, L2_gnn_W_hh, L2_gnn_b_hh, L3_gnn_gamma, L3_gnn_beta, L3_gnn_W, L3_gnn_b):
    import jax
    import jax.numpy as jnp

    def _L0_gnn_ref(x, W, U, w_scale):
        import jax, jax.numpy as jnp
        import numpy as np
        B, N, C, R = (4, 2048, 64, 16)
        EPS = 1e-12
        Ws = 0.5 * (W + jnp.swapaxes(W, -1, -2))
        A = jax.nn.sigmoid(U @ U.T)
        K = Ws * A[None, :, :]
        deg = jnp.maximum(K.sum(axis=-1), EPS)
        d = jax.lax.rsqrt(deg)
        K = K * d[:, :, None] * d[:, None, :]
        return w_scale * jnp.einsum('bnm,bmc->bnc', K, x)

    def _L1_gnn_ref(h, adj, W, a):
        import jax, jax.numpy as jnp
        import numpy as np
        ALPHA = 0.2
        NEG_INF = -9000000000000000.0
        F_out = W.shape[1]
        Wh = jnp.matmul(h, W)
        a1, a2 = (a[:F_out, 0], a[F_out:, 0])
        s1 = Wh @ a1
        s2 = Wh @ a2
        e = s1[:, :, None] + s2[:, None, :]
        e = jnp.where(e > 0, e, ALPHA * e)
        attn_logits = jnp.where(adj > 0, e, NEG_INF)
        attention = jax.nn.softmax(attn_logits, axis=-1)
        h_out = jnp.matmul(attention, Wh)
        return jax.nn.elu(h_out)

    def _L2_gnn_ref(h, A, W1, b1, W2, b2, W_ih, b_ih, W_hh, b_hh):
        import jax, jax.numpy as jnp
        import numpy as np
        B, N, H = (4, 2048, 64)
        m = jax.nn.relu(jnp.einsum('bnh,hk->bnk', h, W1) + b1)
        m = jax.nn.relu(jnp.einsum('bnh,hk->bnk', m, W2) + b2)
        msg = jax.nn.relu(jnp.einsum('bij,bjh->bih', A, m))
        gi = jnp.einsum('bnh,gh->bng', msg, W_ih) + b_ih
        gh = jnp.einsum('bnh,gh->bng', h, W_hh) + b_hh
        i_r, i_z, i_n = jnp.split(gi, 3, axis=-1)
        h_r, h_z, h_n = jnp.split(gh, 3, axis=-1)
        r = jax.nn.sigmoid(i_r + h_r)
        z = jax.nn.sigmoid(i_z + h_z)
        n = jnp.tanh(i_n + r * h_n)
        return (1.0 - z) * n + z * h

    def _L3_gnn_ref(H, A, gamma, beta, W, b):
        import jax, jax.numpy as jnp
        import numpy as np
        B, L, C, OUT = (32, 512, 64, 64)
        BN_EPS = 1e-05
        batch, l, c = H.shape
        Hf = H.reshape(batch * l, c)
        mean = Hf.mean(axis=0)
        var = jnp.mean((Hf - mean) ** 2, axis=0)
        Hn = ((Hf - mean) * jax.lax.rsqrt(var + BN_EPS) * gamma + beta).reshape(batch, l, c)
        d = A.sum(axis=2)
        A_norm = jnp.sqrt(d)[:, :, None] * A * jax.lax.rsqrt(d)[:, None, :]
        A_hat = jnp.eye(l, dtype=A.dtype) - A_norm
        X = Hn @ W + b
        out = jnp.einsum('bij,bjo->bio', A_hat, X)
        return jax.nn.leaky_relu(out, negative_slope=0.01)
    h = jnp.maximum(_layernorm(x, axis=-1), 0.0)
    x = x + _L0_gnn_ref(h, adj, L0_gnn_U, L0_gnn_w_scale)
    h = jnp.maximum(_layernorm(x, axis=-1), 0.0)
    x = x + _L1_gnn_ref(h, adj, L1_gnn_W, L1_gnn_a)
    h = jnp.maximum(_layernorm(x, axis=-1), 0.0)
    x = x + _L2_gnn_ref(h, adj, L2_gnn_W1, L2_gnn_b1, L2_gnn_W2, L2_gnn_b2, L2_gnn_W_ih, L2_gnn_b_ih, L2_gnn_W_hh, L2_gnn_b_hh)
    h = jnp.maximum(_layernorm(x, axis=-1), 0.0)
    x = x + _L3_gnn_ref(h, adj, L3_gnn_gamma, L3_gnn_beta, L3_gnn_W, L3_gnn_b)
    return x

_drawn_inputs = setup_inputs


def setup_inputs(seed=0):
    import zlib

    import numpy as np

    out = dict(_drawn_inputs(seed))
    spreads = {'L2_gnn_b1': (0.0, 0.1),
     'L2_gnn_b2': (0.0, 0.1),
     'L2_gnn_b_ih': (0.0, 0.377),
     'L2_gnn_b_hh': (0.0, 0.559),
     'L3_gnn_gamma': (1.0, 0.2),
     'L3_gnn_beta': (0.0, 0.1),
     'L3_gnn_b': (0.0, 0.1)}
    factors = {'L0_gnn_U': 64.0}
    for name, (base, spread) in spreads.items():
        noise = np.random.default_rng([zlib.crc32(name.encode()), seed]).standard_normal(out[name].shape)
        drawn = base * np.exp(spread * noise) if base else spread * noise
        out[name] = jnp.asarray(drawn.astype(out[name].dtype))
    for name, factor in factors.items():
        out[name] = (out[name] * factor).astype(out[name].dtype)
    return out
```

```python
from contextlib import ExitStack

import concourse.bass as bass
from concourse import mybir

ALU = mybir.AluOpType
ACT = mybir.ActivationFunctionType
AX = mybir.AxisListType.X
F32 = mybir.dt.float32
F16 = mybir.dt.float16
BF16 = mybir.dt.bfloat16
I32 = mybir.dt.int32

P = 128
CB = 4
MAT_SCALE = 1024.0
VEC_SCALE = 64.0
UNSCALE = 1.0 / (MAT_SCALE * VEC_SCALE)
ATT_SCALE = 1024.0
RING = 5
LATE = 4
STEEP = float(2 ** 40)
LN_EPS = 1e-5
BN_EPS = 1e-5
DEG_EPS = 1e-12
RSQRT_STEPS = 11
LN_STEPS = 6 + RSQRT_STEPS
U_SCALE = 16.0


class Chain:

    def __init__(self, eng, sem, base):
        self.eng, self.sem, self.base, self.n = eng, sem, base, 0

    def do(self, ins):
        ins.then_inc(self.sem, 1)
        self.n += 1

    def settle(self, back=0):
        self.eng.wait_ge(self.sem, self.base + (self.n - back))

    def link(self, ins):
        self.do(ins)
        self.settle()


def rsqrt(ch, eng, y, x, t):
    yi = y.bitcast(I32)
    ch.link(eng.tensor_scalar(t.bitcast(I32), x.bitcast(I32), 1, None, ALU.logical_shift_right))
    ch.link(eng.tensor_scalar(yi, t.bitcast(I32), -1.0, 1597463007.0, ALU.mult, ALU.add))
    for _ in range(3):
        ch.link(eng.scalar_tensor_tensor(out=t, in0=y, scalar=-0.5, in1=y, op0=ALU.mult, op1=ALU.mult))
        ch.link(eng.tensor_tensor(t, t, x, ALU.mult))
        ch.link(eng.scalar_tensor_tensor(out=y, in0=t, scalar=1.5, in1=y, op0=ALU.add, op1=ALU.mult))


def gnn_kernel(nc, x, adj, U, w_scale, L1W, L1a, W1, b1, W2, b2, W_ih, b_ih, W_hh, b_hh,
               gamma, beta, L3W, L3b, out, xs, vs):
    B, N, C = x.shape
    R = U.shape[1]
    NB = N // P
    NQ = NB // CB
    D = C + 1
    UK = 3 * R
    chunks = [(n, k) for n in range(NB) for k in range(n // CB + 1)]
    NCH = len(chunks)
    first_chunk = [chunks.index((n, 0)) for n in range(NB)]
    off_diag = [min(CB, n - CB * k) for n, k in chunks]
    up_index = [sum(1 for c in off_diag[:i] if c > 0) for i in range(NCH)]
    NUP = sum(1 for c in off_diag if c > 0)
    TCH = NB * NQ

    xv = x.rearrange("b (i p) c -> b p i c", p=P)
    outv = out.rearrange("b (i p) c -> b p i c", p=P)
    adj_rows = adj.rearrange("b (i p) m -> b i p m", p=P)
    adj_cols = adj.rearrange("b (i p) m -> b p i m", p=P)

    ctx = ExitStack()
    with ctx:
        def sb(name, shape, dt):
            return ctx.enter_context(nc.sbuf_tensor(name, shape, dt))

        def sem(name):
            return ctx.enter_context(nc.semaphore(name))

        mat = sb("mat", [P, NB, NB, 2, P], F16)
        rows = sb("rows", [P, 2, N], F32)
        cols = sb("cols", [P, 2, NB, P], F32)
        s1row = cols[:, 0, :, :].rearrange("p i c -> p (i c)")
        m1T = s1row
        hT = cols[:, 1, :, :].rearrange("p i c -> p (i c)")
        u_nat = cols[:, 0, :, :].rearrange("p i c -> p (i c)").bitcast(F16)[:, 0:2 * NB * UK] \
            .rearrange("p (o i c) -> p o i c", o=2, i=NB)
        cat = sb("cat", [P, NB, 2 * C + 1], F32)
        h = cat[:, :, C:2 * C]
        h1 = cat[:, :, C:2 * C + 1]
        xt = sb("xt", [P, NB, C], F32)
        vec = sb("vec", [P, NB, 2 * D], F16)
        vec_d = sb("vec_d", [P, NB, 2 * D], F16)
        u_st = vec_d[:, :, :].rearrange("p i c -> p (i c)")[0:UK, 0:N]
        vout = vec_d[:, :, :].bitcast(F32)
        tmp = sb("tmp", [P, NB, D], F32)
        scr = sb("scr", [P, 6 * 512], F32)
        a_sum_b = scr[:, 0:1024].rearrange("p (s n) -> p s n", s=2)
        s_sig_b = scr[:, 1024:2048].rearrange("p (s n) -> p s n", s=2)
        k_f32_b = scr[:, 2048:3072].rearrange("p (s n) -> p s n", s=2)
        half = scr[:, :].bitcast(F16).rearrange("p (s n) -> p s n", n=512)
        pos_b, neg_b = half[:, 0:RING, :], half[:, RING:2 * RING, :]
        t_rz = scr[:, 0:512].rearrange("p (i c) -> p i c", i=CB)
        t_pre = scr[:, 512:768].rearrange("p (i c) -> p i c", i=CB)
        t_n = scr[:, 768:1024].rearrange("p (i c) -> p i c", i=CB)
        t_w = scr[:, 1024:1280].rearrange("p (i c) -> p i c", i=CB)
        msum = scr[:, 1280:1280 + CB * D].rearrange("p (i c) -> p i c", i=CB)
        catT = scr[:, 1600:1600 + CB * P]
        yred = sb("yred", [P, 2, 8 * D], F32)
        u_mv = yred[:, :, :].rearrange("p a c -> p (a c)").bitcast(F16)[0:UK, 0:N]
        nsum = yred[:, 0, :].rearrange("p (s c) -> p s c", c=D)
        nwt = yred[:, 1, :].rearrange("p (s c) -> p s c", c=D)
        yq = sb("yq", [P, CB, C], F32)
        rsum = sb("rsum", [P, NB, NQ], F32)
        st = sb("st", [P, 8, NB], F32)
        mean, var, rstd, tn, dscale, deg, dinv, sqd = (st[:, i, :] for i in range(8))
        coef = sb("coef", [P, 4, NB], F32)
        s2st = sb("s2st", [P, NB], F32)
        small = sb("small", [P, 4], F32)
        wsc = sb("wsc", [P, 1], F32)
        ident = sb("ident", [P, P], F32)
        ident16 = sb("ident16", [P, P], F16)
        zeros16 = sb("zeros16", [P, P], F16)
        ones16 = sb("ones16", [P, P], F16)
        onesf = sb("onesf", [P, P], F32)
        wa = sb("wa", [C, C + 2], F32)
        wa1 = sb("wa1", [C, P], F32)
        w1s = sb("w1s", [C, C], F32)
        w2s = sb("w2s", [C, C], F32)
        b1s = sb("b1s", [C, 1], F32)
        b2s = sb("b2s", [P, C], F32)
        wcat = sb("wcat", [P, 4 * C], F32)
        bias2 = sb("bias2", [C, 4 * C], F16)
        bn_sum = sb("bn_sum", [P, 2, C], F32)
        bn_part = yred[:, 1, 0:2 * C].rearrange("p (t c) -> p t c", t=2)
        bnv = sb("bnv", [C, 8], F32)
        gb = sb("gb", [C, 2], F32)
        w3s = yred[0:C, 1, 2 * C:3 * C]
        wfin = yred[0:D, 1, 3 * C:4 * C]
        b3row = yred[0:1, 1, 4 * C:5 * C]
        e_last = yred[0:1, 0, 2 * C:2 * C + D]
        a12 = scr[0:C, 0:2]
        g_rz = scr[:, 128:256]
        g_n = scr[:, 256:384]
        bih = scr[0:C, 384:384 + 3 * C]
        bhh = scr[0:C, 576:576 + 3 * C]
        bsum = scr[0:C, 768:1024]
        bhi = scr[0:C, 1024:1152].bitcast(F16)
        blo = scr[0:C, 1152:1280].bitcast(F16)
        waT = scr[0:C, 1280:1344]
        fold = yred[0:C, 0, 0:D]
        fin_v = [vec[:, :, :].bitcast(F32), vout]
        fin_x = [xt[:, :, :], tmp[:, :, 0:C]]
        fin_vt = [scr[:, 0:512], scr[:, 512:1024]]
        fin_r = [scr[:, 1024:1280], scr[:, 1280:1536]]
        fin_y = [scr[:, 1536:1792], scr[:, 1792:2048]]
        t_elu = scr[:, 2816:2816 + CB * C].rearrange("p (i c) -> p i c", c=C)

        tp = ctx.enter_context(nc.psum_tensor("tp", [P, 2, 512], F32))
        acc = [ctx.enter_context(nc.psum_tensor(f"acc{i}", [P, 3, 512], F32)) for i in range(2)]
        s_ps = acc[0][:, 0:2, :]
        y_ps = acc[0][:, 2, :]
        deg_ps = acc[1][:, 2, 0:NB]
        k_ps = [acc[1][:, i, :].bitcast(F16) for i in range(2)]
        wh_ps = acc[0][:, 0:2, :].rearrange("p a (i c) -> p (a i) c", c=C)
        s12_ps = acc[0][:, 2, 0:2 * NB].rearrange("p (i t) -> p i t", t=2)
        m_ps = acc[1][:, 1:3, :].rearrange("p a (i c) -> p (a i) c", c=C)
        gate_ps = [acc[i][:, 2, :].rearrange("p (i c) -> p i c", c=4 * C) for i in range(2)]

        w_in, set_pe, set_dve, set_pool = (sem(n) for n in ("w_in", "set_pe", "set_dve", "set_pool"))
        row_in = [sem(f"row_in{i}") for i in range(2)]
        col_in = [sem(f"col_in{i}") for i in range(2)]
        arow_in = [sem(f"arow_in{i}") for i in range(2)]
        x0_in, xr_in, x1_out, x1_in = (sem(n) for n in ("x0_in", "xr_in", "x1_out", "x1_in"))
        x3_out, v3_out = sem("x3_out"), sem("v3_out")
        w3_in, e_set = sem("w3_in"), sem("e_set")
        fin_in = [sem(f"fin_in{i}") for i in range(2)]
        fin_out = [sem(f"fin_out{i}") for i in range(2)]
        at_done, slog_done, sig_done, asum_done, kf_done, khi_done, klo_done, kup_t, kup_done = (
            sem(n) for n in ("at_done", "slog_done", "sig_done", "asum_done", "kf_done", "khi_done",
                             "klo_done", "kup_t", "kup_done"))
        deg_done, deg_read, dh_done, v0_hi, v0_done, y_done, y_read, x1_done = (
            sem(n) for n in ("deg_done", "deg_read", "dh_done", "v0_hi", "v0_done", "y_done", "y_read", "x1_done"))
        ln0_step, h0_ready, deg_step, y_step, v_step, f_step = (
            sem(n) for n in ("ln0_step", "h0_ready", "deg_step", "y_step", "v_step", "f_step"))
        a2t_done, ahi_done, alo_done = (sem(n) for n in ("a2t_done", "ahi_done", "alo_done"))
        h_ready, ht_t, ht_cp, wh_mm, s1_mm, s1_cp, mx_in, mx_t, mx_r, mx_b = (sem(n) for n in (
            "h_ready", "ht_t", "ht_cp", "wh_mm", "s1_mm", "s1_cp", "mx_in", "mx_t", "mx_r", "mx_b"))
        nb_done = sem("nb_done")
        coef_in, coef_done, bw_ready, bw_hi, b_ready, g1_done, g2_pool, g2_dve, pos_done, g_used = (sem(n) for n in (
            "coef_in", "coef_done", "bw_ready", "bw_hi", "b_ready", "g1_done", "g2_pool", "g2_dve", "pos_done", "g_used"))
        acc_done, acc_read, elu_in, elu_exp, m1_mm, m1_cp, m_mm, m_sum, v_hi, v_ready = (sem(n) for n in (
            "acc_done", "acc_read", "elu_in", "elu_exp", "m1_mm", "m1_cp", "m_mm", "m_sum", "v_hi", "v_ready"))
        msg_in, msg_done, cat_t, cat_cp, gate_mm, rz_done, pre_done, n_done, gru_done = (sem(n) for n in (
            "msg_in", "msg_done", "cat_t", "cat_cp", "gate_mm", "rz_done", "pre_done", "n_done", "gru_done"))
        x3_ready, m3_in, v3_done = sem("x3_ready"), sem("m3_in"), sem("v3_done")
        f_mm, f_vt, f_vtcp, f_out, f_relu, f_y, f_add = (sem(n) for n in (
            "f_mm", "f_vt", "f_vtcp", "f_out", "f_relu", "f_y", "f_add"))

        def known(b, k):
            return isinstance(b, int) and b * NCH + k <= 0

        def pool_g2(g):
            return g - g // 3

        POOL_G2 = pool_g2(TCH)

        block = ctx.enter_context(nc.Block())

        W_DMAS = 17
        SET_POOL, SET_IDENT, SET_WAT, SET_WA, SET_DVE = 10, 1, 16, 20, 22
        DEG_STEPS, V_STEPS = 3 + RSQRT_STEPS, 138
        F_SUMS, F_FOLD, F_ALL = 1, 21, 22

        @block.sync
        def _(sp):
            sp.dma_start(tmp[:, :, 0:R], U.rearrange("(i p) r -> p i r", p=P)).then_inc(w_in, 16)
            sp.dma_start(wsc[:, :], w_scale.partition_broadcast(P)).then_inc(w_in, 16)
            sp.dma_start(wa[:, 0:C], L1W).then_inc(w_in, 16)
            for t in range(2):
                sp.dma_start(a12[:, t:t + 1], L1a[C * t:C * t + C, :]).then_inc(w_in, 16)
            sp.dma_start(w1s[:, :], W1).then_inc(w_in, 16)
            sp.dma_start(w2s[:, :], W2).then_inc(w_in, 16)
            sp.dma_start(b1s[:, :], b1.rearrange("(c o) -> c o", o=1)).then_inc(w_in, 16)
            sp.dma_start(b2s[:, :], b2.partition_broadcast(P)).then_inc(w_in, 16)
            sp.dma_start(g_rz[:, 0:C], W_ih[0:2 * C, :]).then_inc(w_in, 16)
            sp.dma_start(g_rz[:, C:2 * C], W_hh[0:2 * C, :]).then_inc(w_in, 16)
            sp.wait_ge(set_pool, 1)
            sp.dma_start(g_n[0:C, 0:C], W_ih[2 * C:3 * C, :]).then_inc(w_in, 16)
            sp.dma_start(g_n[C:2 * C, C:2 * C], W_hh[2 * C:3 * C, :]).then_inc(w_in, 16)
            sp.dma_start(bih, b_ih.partition_broadcast(C)).then_inc(w_in, 16)
            sp.dma_start(bhh, b_hh.partition_broadcast(C)).then_inc(w_in, 16)
            sp.dma_start(gb[:, 0:1], gamma.rearrange("(c o) -> c o", o=1)).then_inc(w_in, 16)
            sp.dma_start(gb[:, 1:2], beta.rearrange("(c o) -> c o", o=1)).then_inc(w_in, 16)

            def load_step(b, n, first):
                s = n % 2
                if not (first and n < 2):
                    back = first_chunk[n - 1] if n >= 2 else first_chunk[NB - 1] - NCH if n == 0 else 0
                    sp.wait_ge(asum_done, b * NCH + back)
                sp.dma_start(rows[:, s, 0:(n + 1) * P], adj_rows[b, n, :, 0:(n + 1) * P]).then_inc(row_in[s], 16)
                if n > 0:
                    if first and n == 1:
                        sp.wait_ge(set_dve, SET_DVE)
                    sp.dma_start(cols[:, s, 0:n, :], adj_cols[b, :, 0:n, n * P:(n + 1) * P]).then_inc(col_in[s], 16)

            def load_residual(b):
                sp.dma_start(xt[:, :, :], xv[b]).then_inc(xr_in, 16)

            def store_x1(b):
                sp.wait_ge(x1_done, b * NQ + NQ)
                sp.dma_start(xs[b], xt[:, :, :]).then_inc(x1_out, 16)
                sp.wait_ge(x1_out, b * 16 + 16)

            sp.dma_start(h, xv[0]).then_inc(x0_in, 16)
            for n in range(NB):
                load_step(0, n, True)
            load_residual(0)
            with sp.Fori(1, B) as b:
                sp.wait_ge(v0_done, b)
                sp.dma_start(h, xv[b]).then_inc(x0_in, 16)
                for n in range(NB):
                    load_step(b, n, False)
                store_x1(b - 1)
                load_residual(b)

            def load_row(b, i, first):
                s = i % 2
                if first and i < 2:
                    sp.wait_ge(asum_done, B * NCH)
                else:
                    sp.wait_ge(a2t_done, b * TCH + NQ * (i - 1))
                sp.dma_start(rows[:, s, :], adj_rows[b, i]).then_inc(arow_in[s], 16)

            def store_x3(b):
                sp.wait_ge(x3_ready, b + 1)
                sp.dma_start(xs[b], xt[:, :, :]).then_inc(x3_out, 16)

            def store_v(b):
                sp.wait_ge(v3_done, b + 1)
                sp.dma_start(vs[b], vout).then_inc(v3_out, 16)

            for i in range(NB):
                load_row(0, i, True)
            store_x1(B - 1)
            sp.dma_start(xt[:, :, :], xs[0]).then_inc(x1_in, 16)
            with sp.Fori(0, B - 1) as b:
                store_x3(b)
                load_row(b + 1, 0, False)
                load_row(b + 1, 1, False)
                sp.wait_ge(x3_out, b * 16 + 16)
                sp.dma_start(xt[:, :, :], xs[b + 1]).then_inc(x1_in, 16)
                for i in range(2, NB):
                    load_row(b + 1, i, False)
                store_v(b)
            store_x3(B - 1)
            sp.dma_start(w3s, L3W).then_inc(w3_in, 16)
            sp.dma_start(b3row, L3b.rearrange("(o c) -> o c", o=1)).then_inc(w3_in, 16)
            store_v(B - 1)
            sp.wait_ge(x3_out, B * 16)
            sp.wait_ge(v3_out, B * 16)
            sp.wait_ge(f_step, F_ALL)

            def load_final(t, s):
                sp.dma_start(fin_v[s], vs[t * 2 + s]).then_inc(fin_in[s], 16)
                sp.dma_start(fin_x[s], xs[t * 2 + s]).then_inc(fin_in[s], 16)

            def store_final(t, s):
                sp.wait_ge(f_add, t * (2 * NQ) + (s + 1) * NQ)
                sp.dma_start(outv[t * 2 + s], fin_x[s]).then_inc(fin_out[s], 16)

            for s in range(2):
                load_final(0, s)
            with sp.Fori(0, B // 2 - 1) as t:
                for s in range(2):
                    store_final(t, s)
                for s in range(2):
                    sp.wait_ge(fin_out[s], t * 16 + 16)
                    load_final(t + 1, s)
            for s in range(2):
                store_final(B // 2 - 1, s)
            for s in range(2):
                sp.wait_ge(fin_out[s], 16 * (B // 2))

        USES = NB // 2

        def row_landed(eng, b, n):
            eng.wait_ge(row_in[n % 2], b * (16 * USES) + 16 * (n // 2 + 1))

        def col_landed(eng, b, n):
            uses, use = (USES - 1, n // 2) if n % 2 == 0 else (USES, n // 2 + 1)
            eng.wait_ge(col_in[n % 2], b * (16 * uses) + 16 * use)

        @block.tensor
        def _(pe):
            pe.wait_ge(set_pool, SET_POOL)
            pe.wait_ge(w_in, 16 * W_DMAS)
            pe.wait_ge(set_dve, SET_IDENT)
            pe.transpose(tp[0:C, 0, 0:C], wa[:, 0:C], ident[0:C, 0:C])
            pe.transpose(tp[:, 0, P:2 * P], g_rz, ident[:, :])
            pe.transpose(tp[:, 0, 2 * P:3 * P], g_n, ident[:, :]).then_inc(set_pe, 1)
            pe.wait_ge(set_dve, SET_WAT)
            pe.matmul(tp[0:C, 1, 0:2], waT, a12, start=True, stop=True).then_inc(set_pe, 1)
            pe.wait_ge(set_dve, SET_WA)
            for o in range(2):
                for i in range(NB):
                    ins = pe.transpose(acc[o][0:UK, i // 8, :].bitcast(F16)[:, (i % 8) * P:(i % 8 + 1) * P],
                                       u_nat[:, o, i, :], ident16[:, :])
            ins.then_inc(set_pe, 1)
            pe.wait_ge(set_dve, SET_DVE)

            def k_step(b, n, late):
                for k in range(n // CB + 1):
                    ck = first_chunk[n] + k
                    m0, m1 = CB * k, min(CB * k + CB, n + 1)
                    if k == 0:
                        row_landed(pe, b, n)
                        if n > 0:
                            col_landed(pe, b, n)
                    if not known(b, ck - 1):
                        pe.wait_ge(asum_done, b * NCH + (ck - 1))
                        pe.wait_ge(sig_done, b * NCH + (ck - 1))
                    for m in range(m0, m1):
                        src = cols[:, n % 2, m, :] if m < n else rows[:, n % 2, n * P:(n + 1) * P]
                        ins = pe.transpose(tp[:, ck % 2, (m - m0) * P:(m - m0 + 1) * P], src, ident[:, :])
                    ins.then_inc(at_done, 1)
                    pe.matmul(s_ps[:, ck % 2, 0:(m1 - m0) * P], u_st[:, n * P:(n + 1) * P],
                              u_mv[:, m0 * P:m1 * P], start=True, stop=True).then_inc(slog_done, 1)
                    late.append(ck)
                    if len(late) > LATE:
                        upper(b, late.pop(0))

            def upper(b, ck):
                n, k = chunks[ck]
                off, u = off_diag[ck], up_index[ck]
                if off <= 0:
                    return
                pe.wait_ge(klo_done, b * NCH + (ck + 1))
                if u == 0:
                    if not known(b, 0):
                        pe.wait_ge(deg_read, b)
                    pe.matmul(deg_ps, zeros16[:, :], zeros16[:, 0:NB], start=True, stop=False,
                              skip_group_check=True)
                if not (isinstance(b, int) and b == 0 and u < 2):
                    pe.wait_ge(kup_done, b * NUP + (u - 1))
                for m in range(CB * k, CB * k + off):
                    for part in range(2):
                        pe.matmul(deg_ps[:, m:m + 1], mat[:, n, m, part, :], ones16[:, 0:1],
                                  start=False, stop=False, skip_group_check=True)
                        c = (m - CB * k) * 2 + part
                        ins = pe.transpose(k_ps[u % 2][:, c * P:(c + 1) * P], mat[:, n, m, part, :], ident16[:, :])
                ins.then_inc(kup_t, 1)

            def finish_k(b, late):
                while late:
                    upper(b, late.pop(0))
                pe.matmul(deg_ps, zeros16[:, :], zeros16[:, 0:NB], start=False, stop=True,
                          skip_group_check=True).then_inc(deg_done, 1)

            def y_block(b, i, part=None):
                if part is not None and part > 0:
                    pass
                elif i == 0:
                    pe.wait_ge(v0_done, b + 1)
                    pe.wait_ge(kup_done, b * NUP + NUP)
                elif i % CB == 0:
                    pe.wait_ge(y_read, b * NQ + i // CB)
                o = (i % CB) * P
                for j in range(NB) if part is None else range(CB * part, CB * part + CB):
                    pe.matmul(y_ps[:, o:o + P], mat[:, j, i, 0, :], vec[:, j, 0:2 * C],
                              start=(j == 0), stop=False, skip_group_check=True)
                    ins = pe.matmul(y_ps[:, o:o + C], mat[:, j, i, 1, :], vec[:, j, 0:C],
                                    start=False, stop=(j == NB - 1), skip_group_check=True)
                if i % CB == CB - 1 and part in (None, NQ - 1):
                    ins.then_inc(y_done, 1)

            late = []
            for n in range(NB):
                k_step(0, n, late)
            finish_k(0, late)
            with pe.Fori(1, B) as b:
                for n in range(NB):
                    y_block(b - 1, n)
                    k_step(b, n, late)
                finish_k(b, late)

            def a_step(b, i, beside=None):
                pe.wait_ge(arow_in[i % 2], b * (16 * USES) + 16 * (i // 2 + 1))
                for k in range(NQ):
                    c = i * NQ + k
                    if c >= 2:
                        pe.wait_ge(alo_done, b * TCH + (c - 1))
                    for j in range(CB):
                        ins = pe.transpose(tp[:, c % 2, j * P:(j + 1) * P],
                                           rows[:, i % 2, (CB * k + j) * P:(CB * k + j + 1) * P], ident[:, :])
                    ins.then_inc(a2t_done, 1)
                    if beside is not None:
                        beside(k)

            y_block(B - 1, 0)
            for n in range(NB):
                a_step(0, n, (lambda k: y_block(B - 1, n + 1, k)) if n + 1 < NB else None)

            def vec_part(a, o, i, js):
                for j in js:
                    pe.matmul(a[:, o:o + 2 * D], mat[:, j, i, 0, :], vec[:, j, :],
                              start=(j == 0), stop=False, skip_group_check=True)
                    ins = pe.matmul(a[:, o:o + D], mat[:, j, i, 1, :], vec[:, j, 0:D],
                                    start=False, stop=(j == NB - 1), skip_group_check=True)
                return ins

            def full_array(c):
                pe.matmul(tp[:, c, 0:1], zeros16[:, :], ones16[:, 0:1], start=True, stop=True)

            def h_transposed(b, layer):
                pe.wait_ge(h_ready, b * 2 + layer)
                for c in range(NQ):
                    if c >= 2:
                        pe.wait_ge(ht_cp, b * (2 * NQ) + (layer - 1) * NQ + (c - 1))
                    full_array(c % 2)
                    for i in range(CB):
                        ins = pe.transpose(tp[0:C, c % 2, i * P:(i + 1) * P], h[:, CB * c + i, :], ident[:, :])
                    ins.then_inc(ht_t, 1)
                pe.wait_ge(ht_cp, b * (2 * NQ) + layer * NQ)
                full_array(0)

            def layer1(b):
                h_transposed(b, 1)
                for i in range(NB):
                    pe.matmul(wh_ps[:, i, :], hT[0:C, i * P:(i + 1) * P], wa[:, 0:C], start=True, stop=True)
                    ins = pe.matmul(s12_ps[:, i, :], hT[0:C, i * P:(i + 1) * P], wa[:, C:C + 2],
                                    start=True, stop=True)
                ins.then_inc(wh_mm, 1)
                for c in range(NQ):
                    dst = acc[1][:, c, :] if c < 3 else tp[:, 0, :]
                    pe.matmul(dst, wa1[:, :], hT[0:C, c * 512:(c + 1) * 512], start=True, stop=True) \
                        .then_inc(s1_mm, 1)
                pe.wait_ge(mx_in, b + 1)
                pe.transpose(tp[0:1, 1, 0:P], small[:, 0:1], ident[:, :]).then_inc(mx_t, 1)
                pe.wait_ge(mx_r, b + 1)
                pe.matmul(tp[:, 1, P:P + 1], onesf[0:1, :], small[0:1, 1:2], start=True, stop=True) \
                    .then_inc(mx_b, 1)
                pe.wait_ge(s1_cp, b * NQ + NQ)
                pe.wait_ge(b_ready, b + 1)
                for q in range(NQ):
                    a = acc[q % 2]
                    if q >= 2:
                        pe.wait_ge(acc_read, b * (3 * NQ) + (q - 1))
                    for bank in range(3):
                        pe.matmul(a[:, bank, 0:3 * 2 * D], zeros16[:, :],
                                  vec[:, 0:3, :].rearrange("p i c -> p (i c)"),
                                  start=True, stop=False, skip_group_check=True)
                    for j in range(NB):
                        g = q * NB + j
                        if g % 3 < 2:
                            pe.wait_ge(g2_pool, b * POOL_G2 + pool_g2(g + 1))
                        else:
                            pe.wait_ge(g2_dve, b * (TCH - POOL_G2) + (g + 1 - pool_g2(g + 1)))
                        for s in range(2 * CB):
                            m = (pos_b, neg_b)[s // CB][:, g % RING, (s % CB) * P:(s % CB + 1) * P]
                            ins = pe.matmul(a[:, s // 3, (s % 3) * 2 * D:(s % 3 + 1) * 2 * D], m,
                                            (vec, vec_d)[s // CB][:, j, :], start=False,
                                            stop=(j == NB - 1), skip_group_check=True)
                        ins.then_inc(g_used, 1)
                    pe.matmul(a[:, 2, 2 * 2 * D:3 * 2 * D], zeros16[:, :], vec[:, 0, :], start=False, stop=True,
                              skip_group_check=True).then_inc(acc_done, 1)

            def layer2(b):
                h_transposed(b, 2)
                for c in range(NQ):
                    dst = acc[0][0:C, c, :] if c < 3 else acc[1][0:C, 0, :]
                    pe.matmul(dst, w1s[:, :], hT[0:C, c * 512:(c + 1) * 512], start=True, stop=True) \
                        .then_inc(m1_mm, 1)
                pe.wait_ge(m1_cp, b * NQ + NQ)
                for i in range(NB):
                    ins = pe.matmul(m_ps[:, i, :], m1T[0:C, i * P:(i + 1) * P], w2s[:, :], start=True, stop=True)
                ins.then_inc(m_mm, 1)
                pe.wait_ge(v_ready, b * 2 + 1)
                for q in range(NQ):
                    if q >= 2:
                        pe.wait_ge(acc_read, b * (3 * NQ) + NQ + (q - 1))
                    for i in range(CB):
                        ins = vec_part(acc[q % 2][:, i // 2, :], (i % 2) * 2 * D, CB * q + i, range(NB))
                        if i == CB - 1:
                            ins.then_inc(acc_done, 1)
                        if q >= 1 and i == 1:
                            cat_transposed(b, q - 1)
                        if q >= 1 and i == 2:
                            gates(b, q - 1)
                cat_transposed(b, NQ - 1)
                gates(b, NQ - 1)

            def cat_transposed(b, q):
                pe.wait_ge(msg_done, b * NQ + (q + 1))
                for i in range(CB):
                    ins = pe.transpose(tp[:, q % 2, i * P:(i + 1) * P], cat[:, CB * q + i, 0:2 * C], ident[:, :])
                ins.then_inc(cat_t, 1)

            def gates(b, q):
                pe.wait_ge(cat_cp, b * NQ + (q + 1))
                if q >= 1:
                    pe.wait_ge(pre_done, b * NQ + q)
                for i in range(CB):
                    g = gate_ps[i // 2][:, i % 2, :]
                    pe.matmul(g, catT[:, i * P:(i + 1) * P], wcat[:, :], start=True, stop=False)
                    ins = pe.matmul(g, ones16[0:C, :], bias2[:, :], start=False, stop=True)
                ins.then_inc(gate_mm, 1)

            def layer3(b, follow):
                pe.wait_ge(v_ready, b * 2 + 2)

                def block_part(i, k):
                    q = i // CB
                    if q >= 2 and i % CB == 0 and k == 0:
                        pe.wait_ge(acc_read, b * (3 * NQ) + 2 * NQ + (q - 1))
                    ins = vec_part(acc[q % 2][:, (i % CB) // 2, :], (i % 2) * 2 * D, i, range(CB * k, CB * k + CB))
                    if i % CB == CB - 1 and k == NQ - 1:
                        ins.then_inc(acc_done, 1)

                for k in range(NQ):
                    block_part(0, k)
                for i in range(NB):
                    if follow:
                        a_step(b + 1, i, (lambda k: block_part(i + 1, k)) if i + 1 < NB else None)
                    elif i + 1 < NB:
                        for k in range(NQ):
                            block_part(i + 1, k)

            with pe.Fori(0, B - 1) as b:
                layer1(b)
                layer2(b)
                layer3(b, True)
            layer1(B - 1)
            layer2(B - 1)
            layer3(B - 1, False)

            pe.wait_ge(f_step, F_SUMS)
            pe.matmul(tp[0:C, 0, 0:1], bn_sum[:, 0, :], onesf[:, 0:1], start=True, stop=True)
            pe.matmul(tp[0:C, 0, 1:2], bn_sum[:, 1, :], onesf[:, 0:1], start=True, stop=True).then_inc(f_mm, 1)
            pe.wait_ge(f_step, F_FOLD)
            pe.wait_ge(w3_in, 32)
            pe.wait_ge(e_set, 2)
            pe.matmul(tp[0:D, 1, 0:C], fold, w3s, start=True, stop=False)
            pe.matmul(tp[0:D, 1, 0:C], e_last, b3row, start=False, stop=True).then_inc(f_mm, 1)
            pe.wait_ge(f_step, F_ALL)
            with pe.Fori(0, B // 2) as t:
                for s in range(2):
                    pe.wait_ge(fin_in[s], t * 32 + 32)
                    for q in range(NQ):
                        c = s * NQ + q
                        if c >= 2:
                            pe.wait_ge(f_vtcp, t * (2 * NQ) + (c - 1))
                        for i in range(CB):
                            ins = pe.transpose(tp[0:D, c % 2, i * P:(i + 1) * P], fin_v[s][:, CB * q + i, :], ident[:, :])
                        ins.then_inc(f_vt, 1)
                        pe.wait_ge(f_vtcp, t * (2 * NQ) + (c + 1))
                        if c >= 2:
                            pe.wait_ge(f_y, t * (2 * NQ) + (c - 1))
                        for i in range(CB):
                            ins = pe.matmul(acc[c % 2][:, 0, i * C:(i + 1) * C], fin_vt[c % 2][0:D, i * P:(i + 1) * P],
                                            wfin, start=True, stop=True)
                        ins.then_inc(f_out, 1)
                pe.wait_ge(f_y, t * (2 * NQ) + 2 * NQ)

        @block.scalar
        def _(act):
            def k_sig(b, ck):
                w = (min(CB, chunks[ck][0] + 1 - CB * chunks[ck][1])) * P
                act.wait_ge(slog_done, b * NCH + (ck + 1))
                if not known(b, ck - 1):
                    act.wait_ge(kf_done, b * NCH + (ck - 1))
                act.activation(s_sig_b[:, ck % 2, 0:w], s_ps[:, ck % 2, 0:w], ACT.Sigmoid,
                               scale=1.0 / (U_SCALE * U_SCALE)).then_inc(sig_done, 1)

            def k_hi(b, ck):
                n, k = chunks[ck]
                m0, m1 = CB * k, min(CB * k + CB, n + 1)
                act.wait_ge(kf_done, b * NCH + (ck + 1))
                act.activation(mat[:, n, m0:m1, 0, :],
                               k_f32_b[:, ck % 2, 0:(m1 - m0) * P].rearrange("p (i c) -> p i c", c=P),
                               ACT.Copy).then_inc(khi_done, 1)

            def k_up(b, ck):
                n, k = chunks[ck]
                off, u = off_diag[ck], up_index[ck]
                if off <= 0:
                    return
                act.wait_ge(kup_t, b * NUP + (u + 1))
                act.activation(mat[:, CB * k:CB * k + off, n, :, :],
                               k_ps[u % 2][:, 0:off * 2 * P].rearrange("p (m s c) -> p m s c", s=2, c=P),
                               ACT.Copy).then_inc(kup_done, 1)

            def k_batch(b):
                for ck in range(NCH + LATE + 1):
                    if ck < NCH:
                        k_sig(b, ck)
                    if 1 <= ck <= NCH:
                        k_hi(b, ck - 1)
                    if ck >= LATE + 1:
                        k_up(b, ck - LATE - 1)
                act.wait_ge(dh_done, b + 1)
                act.activation(vec[:, :, 0:C], tmp[:, :, 0:C], ACT.Copy, scale=VEC_SCALE).then_inc(v0_hi, 1)

            k_batch(0)
            with act.Fori(1, B) as b:
                k_batch(b)

            def a_hi(b, c):
                i, k = c // NQ, c % NQ
                act.wait_ge(a2t_done, b * TCH + (c + 1))
                act.activation(mat[:, CB * k:CB * k + CB, i, 0, :],
                               tp[:, c % 2, :].rearrange("p (j c) -> p j c", c=P), ACT.Copy,
                               scale=MAT_SCALE).then_inc(ahi_done, 1)

            for c in range(TCH):
                a_hi(0, c)

            def h_copy(b, layer):
                for c in range(NQ):
                    act.wait_ge(ht_t, b * (2 * NQ) + (layer - 1) * NQ + (c + 1))
                    act.activation(hT[0:C, c * 512:(c + 1) * 512], tp[0:C, c % 2, :], ACT.Copy).then_inc(ht_cp, 1)

            def layer1(b):
                h_copy(b, 1)
                for c in range(NQ):
                    act.wait_ge(s1_mm, b * NQ + (c + 1))
                    src = acc[1][:, c, :] if c < 3 else tp[:, 0, :]
                    act.activation(s1row[:, c * 512:(c + 1) * 512], src, ACT.Copy).then_inc(s1_cp, 1)
                act.wait_ge(coef_in, b + 1)
                act.activation(coef[:, :, :], coef[:, :, :], ACT.Exp).then_inc(coef_done, 1)
                for t in range(2):
                    act.wait_ge(bw_ready, b * 2 + (t + 1))
                    act.activation((vec, vec_d)[t][:, :, 0:D], tmp[:, :, :], ACT.Copy).then_inc(bw_hi, 1)
                for g in range(TCH):
                    q, j = g // NB, g % NB
                    if g >= RING:
                        act.wait_ge(g_used, b * TCH + (g - RING + 1))
                    act.activation(pos_b[:, g % RING, :], s1row[:, q * 512:(q + 1) * 512], ACT.Sigmoid,
                                   bias=s2st[:, j:j + 1], scale=STEEP).then_inc(pos_done, 1)
                    if q >= 1 and j == 5:
                        elu(b, q - 1)
                elu(b, NQ - 1)

            def elu(b, q):
                act.wait_ge(elu_in, b * NQ + (q + 1))
                act.activation(t_elu, t_elu, ACT.Exp).then_inc(elu_exp, 1)

            def layer2(b):
                h_copy(b, 2)
                for c in range(NQ):
                    act.wait_ge(m1_mm, b * NQ + (c + 1))
                    src = acc[0][0:C, c, :] if c < 3 else acc[1][0:C, 0, :]
                    act.activation(m1T[0:C, c * 512:(c + 1) * 512], src, ACT.Relu, bias=b1s[:, 0:1]).then_inc(m1_cp, 1)
                act.wait_ge(m_sum, b + 1)
                act.activation(vec[:, :, 0:C], tmp[:, :, 0:C], ACT.Relu, scale=VEC_SCALE).then_inc(v_hi, 1)

                def gate_copies(q):
                    act.wait_ge(cat_t, b * NQ + (q + 1))
                    if q >= 1:
                        act.wait_ge(gate_mm, b * NQ + q)
                    act.activation(catT, tp[:, q % 2, :], ACT.Copy).then_inc(cat_cp, 1)
                    act.wait_ge(gate_mm, b * NQ + (q + 1))
                    if q >= 1:
                        act.wait_ge(gru_done, b * NQ + q)
                    for i in range(2):
                        ins = act.activation(t_rz[:, 2 * i:2 * i + 2, :], gate_ps[i][:, :, 0:2 * C], ACT.Tanh, scale=0.5)
                    ins.then_inc(rz_done, 1)

                def n_gate(q):
                    act.wait_ge(pre_done, b * NQ + (q + 1))
                    act.activation(t_n, t_pre, ACT.Tanh).then_inc(n_done, 1)

                for q in range(NQ):
                    if q >= 1:
                        gate_copies(q - 1)
                    act.wait_ge(msg_in, b * NQ + (q + 1))
                    act.activation(cat[:, CB * q:CB * q + CB, 0:C], msum[:, :, 0:C], ACT.Relu,
                                   scale=UNSCALE).then_inc(msg_done, 1)
                    if q >= 1:
                        n_gate(q - 1)
                gate_copies(NQ - 1)
                n_gate(NQ - 1)

            def layer3(b, follow):
                act.wait_ge(m3_in, b + 1)
                act.activation(vec[:, :, 0:D], tmp[:, :, :], ACT.Copy, scale=VEC_SCALE).then_inc(v_hi, 1)
                if follow:
                    for c in range(TCH):
                        a_hi(b + 1, c)
                    act.wait_ge(v3_out, b * 16 + 16)

            with act.Fori(0, B - 1) as b:
                layer1(b)
                layer2(b)
                layer3(b, True)
            layer1(B - 1)
            layer2(B - 1)
            layer3(B - 1, False)

            with act.Fori(0, B // 2) as t:
                for c in range(2 * NQ):
                    act.wait_ge(f_vt, t * (2 * NQ) + (c + 1))
                    act.activation(fin_vt[c % 2][0:D, :], tp[0:D, c % 2, :], ACT.Copy).then_inc(f_vtcp, 1)
                    act.wait_ge(f_out, t * (2 * NQ) + (c + 1))
                    if c >= 2:
                        act.wait_ge(f_y, t * (2 * NQ) + (c - 1))
                    act.activation(fin_r[c % 2], acc[c % 2][:, 0, 0:CB * C], ACT.Relu, scale=0.99).then_inc(f_relu, 1)

        @block.gpsimd
        def _(pool):
            pool.memset(g_n, 0.0).then_inc(set_pool, 1)
            pool.memset(ident[:, :], 0.0).then_inc(set_pool, 1)
            pool.wait_ge(set_pool, 2)
            pool.affine_select(out=ident[:, :], in_=ident[:, :], compare_op=ALU.not_equal, fill=1.0, base=0,
                               pattern=[[-1, P]], channel_multiplier=1).then_inc(set_pool, 1)
            pool.memset(onesf[:, :], 1.0).then_inc(set_pool, 1)
            pool.memset(zeros16[:, :], 0.0).then_inc(set_pool, 1)
            pool.memset(ones16[:, :], 1.0).then_inc(set_pool, 1)
            pool.memset(bn_sum[:, :, :], 0.0).then_inc(set_pool, 1)
            pool.memset(bias2[:, :], 0.0).then_inc(set_pool, 1)
            pool.memset(cat[:, :, 2 * C:2 * C + 1], 1.0).then_inc(set_pool, 1)
            pool.memset(rsum[:, :, :], 0.0).then_inc(set_pool, 1)

            with pool.Fori(0, B) as b:
                for ck, (n, k) in enumerate(chunks):
                    m0, m1 = CB * k, min(CB * k + CB, n + 1)
                    pool.wait_ge(khi_done, b * NCH + (ck + 1))
                    pool.tensor_tensor(mat[:, n, m0:m1, 1, :],
                                       k_f32_b[:, ck % 2, 0:(m1 - m0) * P].rearrange("p (i c) -> p i c", c=P),
                                       mat[:, n, m0:m1, 0, :], ALU.subtract).then_inc(klo_done, 1)
            with pool.Fori(0, B) as b:
                for g in range(TCH):
                    if g % 3 < 2:
                        pool.wait_ge(g1_done, b * TCH + (g + 1))
                        pool.tensor_tensor(neg_b[:, g % RING, :], neg_b[:, g % RING, :], pos_b[:, g % RING, :],
                                           ALU.subtract).then_inc(g2_pool, 1)
            pool.wait_ge(x3_ready, B)
            pool.memset(e_last[:, 0:C], 0.0).then_inc(e_set, 1)
            pool.memset(e_last[:, C:D], 1.0).then_inc(e_set, 1)

        @block.vector
        def _(dve):
            def layer_norm(ch, src, ready):
                wide = [P, NB, C]
                sq, xc = h, tmp[:, :, 0:C]
                ch.link(dve.tensor_reduce(mean, src, AX, ALU.add))
                ch.link(dve.tensor_scalar(mean, mean, -1.0 / C, None, ALU.mult))
                ch.link(dve.tensor_tensor(xc, src, mean.unsqueeze(2).to_broadcast(wide), ALU.add))
                ch.link(dve.tensor_tensor(sq, xc, xc, ALU.mult))
                ch.link(dve.tensor_reduce(var, sq, AX, ALU.add))
                ch.link(dve.tensor_scalar(var, var, 1.0 / C, LN_EPS, ALU.mult, ALU.add))
                rsqrt(ch, dve, rstd, var, tn)
                dve.scalar_tensor_tensor(out=h, in0=xc, scalar=0.0, in1=rstd.unsqueeze(2).to_broadcast(wide),
                                         op0=ALU.max, op1=ALU.mult).then_inc(ready, 1)

            dve.wait_ge(set_pool, SET_POOL)
            dve.wait_ge(w_in, 16 * W_DMAS)
            ch = Chain(dve, set_dve, 0)
            u16 = tmp[:, :, R:2 * R]
            ch.link(dve.tensor_copy(ident16[:, :], ident[:, :]))
            assert ch.n == SET_IDENT
            ch.link(dve.tensor_scalar(u16, tmp[:, :, 0:R], U_SCALE, None, ALU.mult))
            ch.link(dve.tensor_copy(u_nat[:, 0, :, 0:R], u16))
            ch.link(dve.tensor_tensor(u_nat[:, 0, :, 2 * R:3 * R], u16, u_nat[:, 0, :, 0:R], ALU.subtract))
            ch.do(dve.tensor_copy(u_nat[:, 0, :, R:2 * R], u_nat[:, 0, :, 0:R]))
            ch.do(dve.tensor_copy(u_nat[:, 1, :, 0:R], u_nat[:, 0, :, 0:R]))
            ch.do(dve.tensor_copy(u_nat[:, 1, :, R:2 * R], u_nat[:, 0, :, 2 * R:3 * R]))
            ch.do(dve.tensor_copy(u_nat[:, 1, :, 2 * R:3 * R], u_nat[:, 0, :, 0:R]))
            ch.do(dve.tensor_tensor(bsum[:, 0:2 * C], bih[:, 0:2 * C], bhh[:, 0:2 * C], ALU.add))
            ch.do(dve.tensor_copy(bsum[:, 2 * C:3 * C], bih[:, 2 * C:3 * C]))
            ch.link(dve.tensor_copy(bsum[:, 3 * C:4 * C], bhh[:, 2 * C:3 * C]))
            ch.link(dve.tensor_copy(bhi, bsum))
            ch.link(dve.tensor_tensor(blo, bsum, bhi, ALU.subtract))
            ch.do(dve.tensor_copy(bias2[0:1, :], bhi[0:1, :]))
            ch.do(dve.tensor_copy(bias2[32:33, :], blo[32:33, :]))
            dve.wait_ge(set_pe, 1)
            ch.do(dve.tensor_copy(waT, tp[0:C, 0, 0:C]))
            assert ch.n == SET_WAT, ch.n
            ch.do(dve.tensor_copy(wcat[:, 0:P], tp[:, 0, P:2 * P]))
            ch.do(dve.tensor_copy(wcat[:, P:2 * P], tp[:, 0, 2 * P:3 * P]))
            dve.wait_ge(set_pe, 2)
            ch.link(dve.tensor_copy(wa[:, C:C + 2], tp[0:C, 1, 0:2]))
            ch.link(dve.tensor_copy(wa1[:, :], wa[:, C:C + 1].to_broadcast([C, P])))
            assert ch.n == SET_WA, ch.n
            dve.wait_ge(set_pe, 3)
            for o, dst in enumerate((u_st, u_mv)):
                ch.do(dve.tensor_copy(dst.rearrange("p (a c) -> p a c", a=2),
                                      acc[o][0:UK, 0:2, :].bitcast(F16)))
            assert ch.n == SET_DVE, ch.n
            ch.settle()

            def k_sum(b, ck):
                n, k = chunks[ck]
                w = min(CB, n + 1 - CB * k) * P
                if k == 0:
                    row_landed(dve, b, n)
                dve.wait_ge(at_done, b * NCH + (ck + 1))
                if not known(b, ck - 1):
                    dve.wait_ge(kf_done, b * NCH + (ck - 1))
                dve.tensor_tensor(a_sum_b[:, ck % 2, 0:w], rows[:, n % 2, CB * k * P:CB * k * P + w],
                                  tp[:, ck % 2, 0:w], ALU.add).then_inc(asum_done, 1)

            def k_mul(b, ck):
                n, k = chunks[ck]
                w = min(CB, n + 1 - CB * k) * P
                dve.wait_ge(sig_done, b * NCH + (ck + 1))
                dve.wait_ge(asum_done, b * NCH + (ck + 1))
                if not known(b, ck - 1):
                    dve.wait_ge(klo_done, b * NCH + (ck - 1))
                dve.scalar_tensor_tensor(out=k_f32_b[:, ck % 2, 0:w], in0=a_sum_b[:, ck % 2, 0:w],
                                         scalar=0.5 * MAT_SCALE, in1=s_sig_b[:, ck % 2, 0:w], op0=ALU.mult,
                                         op1=ALU.mult, accum_out=rsum[:, n, k:k + 1]).then_inc(kf_done, 1)

            def y_post(b, q):
                dve.wait_ge(y_done, b * NQ + (q + 1))
                if q == 0:
                    dve.wait_ge(xr_in, b * 16 + 16)
                dve.tensor_reduce(yq[:, :, :], y_ps.rearrange("p (i s c) -> p i c s", s=2, c=C), AX,
                                  ALU.add).then_inc(y_read, 1)
                dve.wait_ge(y_read, b * NQ + (q + 1))
                dve.tensor_tensor(yq[:, :, :], yq[:, :, :],
                                  dscale[:, CB * q:CB * q + CB].unsqueeze(2).to_broadcast([P, CB, C]),
                                  ALU.mult).then_inc(y_step, 1)
                dve.wait_ge(y_step, b * NQ + (q + 1))
                dve.tensor_tensor(xt[:, CB * q:CB * q + CB, :], xt[:, CB * q:CB * q + CB, :], yq[:, :, :],
                                  ALU.add).then_inc(x1_done, 1)
                dve.wait_ge(x1_done, b * NQ + (q + 1))

            def k_batch(b, last):
                for ck in range(NCH + 1):
                    n = chunks[ck][0] if ck < NCH else NB
                    if last is not None and n % CB == 0 and n > 0 and (n == NB or chunks[ck][1] == 0):
                        y_post(last, n // CB - 1)
                    if ck < NCH:
                        k_sum(b, ck)
                    if ck >= 1:
                        k_mul(b, ck - 1)
                    if ck < NCH and chunks[ck][1] == 0:
                        if n == 11:
                            dve.wait_ge(x0_in, b * 16 + 16)
                            ch = Chain(dve, ln0_step, b * LN_STEPS)
                            layer_norm(ch, h, h0_ready)
                            assert ch.n == LN_STEPS
                ch = Chain(dve, deg_step, b * DEG_STEPS)
                dve.wait_ge(kf_done, b * NCH + NCH)
                ch.link(dve.tensor_reduce(deg, rsum[:, :, :], AX, ALU.add))
                dve.wait_ge(deg_done, b + 1)
                dve.tensor_tensor(deg, deg, deg_ps, ALU.add).then_inc(deg_read, 1)
                dve.wait_ge(deg_read, b + 1)
                dve.wait_ge(h0_ready, b + 1)
                ch.link(dve.tensor_scalar(deg, deg, 1.0 / MAT_SCALE, DEG_EPS, ALU.mult, ALU.max))
                rsqrt(ch, dve, dinv, deg, tn)
                ch.do(dve.tensor_scalar(dscale, dinv, wsc[:, 0:1], UNSCALE, ALU.mult, ALU.mult))
                dve.tensor_tensor(tmp[:, :, 0:C], h, dinv.unsqueeze(2).to_broadcast([P, NB, C]),
                                  ALU.mult).then_inc(dh_done, 1)
                dve.wait_ge(v0_hi, b + 1)
                dve.scalar_tensor_tensor(out=vec[:, :, C:2 * C], in0=tmp[:, :, 0:C], scalar=VEC_SCALE,
                                         in1=vec[:, :, 0:C], op0=ALU.mult, op1=ALU.subtract).then_inc(v0_done, 1)
                assert ch.n == DEG_STEPS, ch.n

            k_batch(0, None)
            with dve.Fori(1, B) as b:
                k_batch(b, b - 1)

            def a_lo(b, c):
                i, k = c // NQ, c % NQ
                dve.wait_ge(ahi_done, b * TCH + (c + 1))
                dve.scalar_tensor_tensor(out=mat[:, CB * k:CB * k + CB, i, 1, :],
                                         in0=tp[:, c % 2, :].rearrange("p (j c) -> p j c", c=P), scalar=MAT_SCALE,
                                         in1=mat[:, CB * k:CB * k + CB, i, 0, :], op0=ALU.mult,
                                         op1=ALU.subtract).then_inc(alo_done, 1)

            for c in range(TCH):
                if c % (NQ * CB) == NQ * (CB - 1):
                    y_post(B - 1, c // (NQ * CB))
                a_lo(0, c)

            def wide(v, q=None):
                if q is None:
                    return v.unsqueeze(2).to_broadcast([P, NB, C])
                return v[:, CB * q:CB * q + CB].unsqueeze(2).to_broadcast([P, CB, C])

            def layer1(b, ch):
                dve.wait_ge(x1_in, b * 16 + 16)
                layer_norm(ch, xt[:, :, :], h_ready)
                s1, s2 = s12_ps[:, :, 0], s12_ps[:, :, 1]
                dve.wait_ge(wh_mm, b + 1)
                dve.tensor_reduce(small[:, 0:1], s2, AX, ALU.max).then_inc(mx_in, 1)
                dve.wait_ge(mx_t, b + 1)
                dve.tensor_reduce(small[0:1, 1:2], tp[0:1, 1, 0:P], AX, ALU.max).then_inc(mx_r, 1)
                dve.wait_ge(mx_b, b + 1)
                ch.link(dve.tensor_copy(small[:, 2:3], tp[:, 1, P:P + 1]))
                top = small[:, 2:3]
                ch.link(dve.tensor_scalar(var, s1, top, None, ALU.add))
                ch.link(dve.scalar_tensor_tensor(out=tn, in0=var, scalar=0.2, in1=var, op0=ALU.mult, op1=ALU.max))
                ch.do(dve.tensor_tensor(coef[:, 0, :], var, tn, ALU.subtract))
                ch.do(dve.scalar_tensor_tensor(out=coef[:, 1, :], in0=var, scalar=0.2, in1=tn, op0=ALU.mult,
                                               op1=ALU.subtract))
                ch.do(dve.tensor_scalar(coef[:, 2, :], s2, top, None, ALU.subtract))
                ch.do(dve.tensor_scalar(s2st[:, :], s2, STEEP, None, ALU.mult))
                ch.settle(1)
                dve.tensor_scalar(coef[:, 3, :], coef[:, 2, :], 0.2, None, ALU.mult).then_inc(coef_in, 1)
                dve.wait_ge(coef_done, b + 1)
                ch.link(dve.tensor_scalar(coef[:, 2:4, :], coef[:, 2:4, :], ATT_SCALE, None, ALU.mult))
                for t in range(2):
                    w = coef[:, 2 + t, :]
                    if t == 1:
                        ch.settle()
                    ch.do(dve.tensor_tensor(tmp[:, :, 0:C], wh_ps, wide(w), ALU.mult))
                    dve.tensor_copy(tmp[:, :, C:D], w.unsqueeze(2)).then_inc(bw_ready, 1)
                    dve.wait_ge(bw_hi, b * 2 + (t + 1))
                    v = (vec, vec_d)[t]
                    ins = dve.tensor_tensor(v[:, :, D:2 * D], tmp[:, :, :], v[:, :, 0:D], ALU.subtract)
                    if t == 0:
                        ch.do(ins)
                    else:
                        ins.then_inc(b_ready, 1)
                dve.wait_ge(s1_cp, b * NQ + NQ)

                def neighbours(g):
                    q, j = g // NB, g % NB
                    if g >= RING:
                        dve.wait_ge(g_used, b * TCH + (g - RING + 1))
                    dve.tensor_scalar(neg_b[:, g % RING, :].rearrange("p (i c) -> p i c", c=P),
                                      mat[:, j, CB * q:CB * q + CB, 0, :], 0.0, None, ALU.is_gt).then_inc(nb_done, 1)

                def positive(g):
                    dve.wait_ge(nb_done, b * TCH + (g + 1))
                    dve.wait_ge(pos_done, b * TCH + (g + 1))
                    dve.tensor_tensor(pos_b[:, g % RING, :], neg_b[:, g % RING, :], pos_b[:, g % RING, :],
                                      ALU.mult).then_inc(g1_done, 1)

                def negative(g):
                    if g % 3 == 2:
                        dve.wait_ge(g1_done, b * TCH + (g + 1))
                        dve.tensor_tensor(neg_b[:, g % RING, :], neg_b[:, g % RING, :], pos_b[:, g % RING, :],
                                          ALU.subtract).then_inc(g2_dve, 1)

                def post(q):
                    a = acc[q % 2]
                    dve.wait_ge(acc_done, b * (3 * NQ) + (q + 1))
                    for bank in range(3):
                        k = min(3, 2 * CB - 3 * bank)
                        ins = dve.tensor_reduce(nsum[:, 3 * bank:3 * bank + k, :],
                                                a[:, bank, 0:k * 2 * D].rearrange("p (i s c) -> p i c s", s=2, c=D),
                                                AX, ALU.add)
                    ins.then_inc(acc_read, 1)
                    dve.wait_ge(acc_read, b * (3 * NQ) + (q + 1))
                    for t in range(2):
                        ch.do(dve.tensor_tensor(nwt[:, CB * t:CB * t + CB, :], nsum[:, CB * t:CB * t + CB, :],
                                                coef[:, t, CB * q:CB * q + CB].unsqueeze(2).to_broadcast([P, CB, D]),
                                                ALU.mult))
                    ch.settle()
                    ch.link(dve.tensor_tensor(nsum[:, 0:CB, :], nwt[:, 0:CB, :], nwt[:, CB:2 * CB, :], ALU.add))
                    den = tn[:, 0:CB]
                    ch.link(dve.reciprocal(den.unsqueeze(2), nsum[:, 0:CB, C:D]))
                    ch.link(dve.tensor_tensor(yq[:, :, :], nsum[:, 0:CB, 0:C],
                                              den.unsqueeze(2).to_broadcast([P, CB, C]), ALU.mult))
                    dve.tensor_scalar(t_elu, yq[:, :, :], 0.0, None, ALU.min).then_inc(elu_in, 1)
                    return q

                def post_end(q):
                    dve.wait_ge(elu_exp, b * NQ + (q + 1))
                    ch.link(dve.scalar_tensor_tensor(out=yq[:, :, :], in0=yq[:, :, :], scalar=0.0, in1=t_elu,
                                                     op0=ALU.max, op1=ALU.add))
                    x_q = xt[:, CB * q:CB * q + CB, :]
                    ch.link(dve.scalar_tensor_tensor(out=x_q, in0=yq[:, :, :], scalar=-1.0, in1=x_q,
                                                     op0=ALU.add, op1=ALU.add))

                for g in range(TCH + 2):
                    if g < TCH:
                        neighbours(g)
                    if 1 <= g <= TCH:
                        positive(g - 1)
                    if g >= 2:
                        negative(g - 2)
                    if NB <= g < TCH and g % NB == 4:
                        post(g // NB - 1)
                    if NB <= g < TCH and g % NB == 8:
                        post_end(g // NB - 1)
                post(NQ - 1)
                post_end(NQ - 1)

            def layer2(b, ch):
                layer_norm(ch, xt[:, :, :], h_ready)
                dve.wait_ge(m_mm, b + 1)
                dve.tensor_tensor(tmp[:, :, 0:C], m_ps, b2s[:, :].unsqueeze(1).to_broadcast([P, NB, C]),
                                  ALU.add).then_inc(m_sum, 1)
                ch.do(dve.memset(vec[:, :, C:D], VEC_SCALE))
                ch.do(dve.memset(vec[:, :, 2 * D - 1:2 * D], 0.0))
                dve.wait_ge(v_hi, b * 2 + 1)
                ch.link(dve.tensor_scalar(tmp[:, :, 0:C], tmp[:, :, 0:C], 0.0, VEC_SCALE, ALU.max, ALU.mult))
                dve.tensor_tensor(vec[:, :, D:D + C], tmp[:, :, 0:C], vec[:, :, 0:C], ALU.subtract).then_inc(v_ready, 1)

                def message(q):
                    dve.wait_ge(acc_done, b * (3 * NQ) + NQ + (q + 1))
                    if q >= 1:
                        dve.wait_ge(msg_done, b * NQ + q)
                    for k in range(2):
                        ins = dve.tensor_reduce(msum[:, 2 * k:2 * k + 2, :],
                                                acc[q % 2][:, k, 0:4 * D].rearrange("p (i s c) -> p i c s", s=2, c=D),
                                                AX, ALU.add)
                    ins.then_inc(acc_read, 1)
                    dve.wait_ge(acc_read, b * (3 * NQ) + NQ + (q + 1))
                    dve.tensor_scalar(deg[:, CB * q:CB * q + CB].unsqueeze(2), msum[:, :, C:D], UNSCALE, None,
                                      ALU.mult).then_inc(msg_in, 1)

                def gru(q):
                    dve.wait_ge(rz_done, b * NQ + (q + 1))
                    for k in range(2):
                        s = slice(2 * k, 2 * k + 2)
                        ch.do(dve.scalar_tensor_tensor(out=t_w[:, s, :], in0=t_rz[:, s, 0:C], scalar=1.0,
                                                       in1=gate_ps[k][:, :, 3 * C:4 * C], op0=ALU.add, op1=ALU.mult))
                    ch.settle()
                    for k in range(2):
                        s = slice(2 * k, 2 * k + 2)
                        ins = dve.scalar_tensor_tensor(out=t_pre[:, s, :], in0=t_w[:, s, :], scalar=0.5,
                                                       in1=gate_ps[k][:, :, 2 * C:3 * C], op0=ALU.mult, op1=ALU.add)
                    ins.then_inc(pre_done, 1)

                def gru_end(q):
                    hq, xq = h[:, CB * q:CB * q + CB, :], xt[:, CB * q:CB * q + CB, :]
                    dve.wait_ge(n_done, b * NQ + (q + 1))
                    ch.link(dve.tensor_tensor(t_w, hq, t_n, ALU.subtract))
                    ch.link(dve.scalar_tensor_tensor(out=t_w, in0=t_rz[:, :, C:2 * C], scalar=1.0, in1=t_w,
                                                     op0=ALU.add, op1=ALU.mult))
                    ch.link(dve.scalar_tensor_tensor(out=t_w, in0=t_w, scalar=0.5, in1=t_n, op0=ALU.mult, op1=ALU.add))
                    dve.tensor_tensor(xq, xq, t_w, ALU.add).then_inc(gru_done, 1)

                for q in range(NQ):
                    if q >= 1:
                        gru(q - 1)
                    message(q)
                    if q >= 1:
                        gru_end(q - 1)
                gru(NQ - 1)
                gru_end(NQ - 1)
                dve.wait_ge(gru_done, b * NQ + NQ)

            def layer3(b, ch, follow):
                layer_norm(ch, xt[:, :, :], x3_ready)
                dve.wait_ge(x3_ready, b + 1)
                rsqrt(ch, dve, dinv, deg, tn)
                ch.do(dve.tensor_tensor(tmp[:, :, 0:C], h, wide(dinv), ALU.mult))
                dve.tensor_copy(tmp[:, :, C:D], dinv.unsqueeze(2)).then_inc(m3_in, 1)
                ch.link(dve.tensor_tensor(sqd, deg, dinv, ALU.mult))
                ch.link(dve.tensor_scalar(sqd, sqd, -UNSCALE, None, ALU.mult))
                dve.wait_ge(v_hi, b * 2 + 2)
                dve.scalar_tensor_tensor(out=vec[:, :, D:2 * D], in0=tmp[:, :, :], scalar=VEC_SCALE,
                                         in1=vec[:, :, 0:D], op0=ALU.mult, op1=ALU.subtract).then_inc(v_ready, 1)
                dve.wait_ge(v_ready, b * 2 + 2)
                ch.link(dve.tensor_tensor(tmp[:, :, 0:C], h, h, ALU.mult))
                ch.do(dve.tensor_reduce(bn_part[:, 0, :], h.rearrange("p i c -> p c i"), AX, ALU.add))
                ch.link(dve.tensor_reduce(bn_part[:, 1, :], tmp[:, :, 0:C].rearrange("p i c -> p c i"), AX, ALU.add))
                ch.link(dve.tensor_tensor(bn_sum[:, :, :], bn_sum[:, :, :], bn_part[:, :, :], ALU.add))

                def post(q):
                    ch.settle()
                    dve.wait_ge(acc_done, b * (3 * NQ) + 2 * NQ + (q + 1))
                    for k in range(2):
                        ins = dve.tensor_reduce(msum[:, 2 * k:2 * k + 2, :],
                                                acc[q % 2][:, k, 0:4 * D].rearrange("p (i s c) -> p i c s", s=2, c=D),
                                                AX, ALU.add)
                    ins.then_inc(acc_read, 1)
                    dve.wait_ge(acc_read, b * (3 * NQ) + 2 * NQ + (q + 1))
                    ch.link(dve.tensor_tensor(msum, msum, sqd[:, CB * q:CB * q + CB].unsqueeze(2)
                                              .to_broadcast([P, CB, D]), ALU.mult))
                    ins = dve.tensor_tensor(vout[:, CB * q:CB * q + CB, :], msum, h1[:, CB * q:CB * q + CB, :], ALU.add)
                    if q == NQ - 1:
                        ins.then_inc(v3_done, 1)
                    else:
                        ch.do(ins)

                if follow:
                    for c in range(TCH):
                        a_lo(b + 1, c)
                        if c % (NQ * CB) == NQ * (CB - 1) + 1:
                            post(c // (NQ * CB))
                else:
                    for q in range(NQ):
                        post(q)

            def layers(b, follow):
                ch = Chain(dve, v_step, b * V_STEPS)
                layer1(b, ch)
                layer2(b, ch)
                layer3(b, ch, follow)
                assert ch.n == V_STEPS, ch.n

            with dve.Fori(0, B - 1) as b:
                layers(b, True)
            layers(B - 1, False)

            ch = Chain(dve, f_step, 0)
            ch.link(dve.tensor_copy(small[:, 3:4], bn_sum[:, 0, 0:1]))
            assert ch.n == F_SUMS
            dve.wait_ge(f_mm, 1)
            mu, ex2, vr, rs, t1, sc, sh = (bnv[:, i:i + 1] for i in range(7))
            ch.link(dve.tensor_scalar(bnv[:, 0:2], tp[0:C, 0, 0:2], 1.0 / (B * N), None, ALU.mult))
            ch.link(dve.tensor_tensor(vr, mu, mu, ALU.mult))
            ch.link(dve.tensor_tensor(vr, ex2, vr, ALU.subtract))
            ch.link(dve.tensor_scalar(vr, vr, BN_EPS, None, ALU.add))
            rsqrt(ch, dve, rs, vr, t1)
            ch.link(dve.tensor_tensor(sc, gb[:, 0:1], rs, ALU.mult))
            ch.link(dve.tensor_tensor(t1, mu, sc, ALU.mult))
            ch.link(dve.tensor_tensor(sh, gb[:, 1:2], t1, ALU.subtract))
            ch.do(dve.tensor_scalar(fold[:, 0:C], ident[0:C, 0:C], sc, None, ALU.mult))
            ch.link(dve.tensor_copy(fold[:, C:D], sh))
            assert ch.n == F_FOLD, ch.n
            dve.wait_ge(f_mm, 2)
            ch.link(dve.tensor_copy(wfin, tp[0:D, 1, 0:C]))
            assert ch.n == F_ALL, ch.n
            with dve.Fori(0, B // 2) as t:
                for s in range(2):
                    dve.wait_ge(fin_in[s], t * 32 + 32)
                    for q in range(NQ):
                        c = s * NQ + q
                        dve.wait_ge(f_relu, t * (2 * NQ) + (c + 1))
                        dve.scalar_tensor_tensor(out=fin_y[c % 2], in0=acc[c % 2][:, 0, 0:CB * C], scalar=0.01,
                                                 in1=fin_r[c % 2], op0=ALU.mult, op1=ALU.add).then_inc(f_y, 1)
                        dve.wait_ge(f_y, t * (2 * NQ) + (c + 1))
                        xq = fin_x[s][:, CB * q:CB * q + CB, :]
                        dve.tensor_tensor(xq, xq, fin_y[c % 2].rearrange("p (i c) -> p i c", c=C), ALU.add) \
                            .then_inc(f_add, 1)


_INS = ['x', 'adj', 'L0_gnn_U', 'L0_gnn_w_scale', 'L1_gnn_W', 'L1_gnn_a', 'L2_gnn_W1', 'L2_gnn_b1', 'L2_gnn_W2',
        'L2_gnn_b2', 'L2_gnn_W_ih', 'L2_gnn_b_ih', 'L2_gnn_W_hh', 'L2_gnn_b_hh', 'L3_gnn_gamma', 'L3_gnn_beta',
        'L3_gnn_W', 'L3_gnn_b']


def kernel(**inputs):
    import numpy as _np
    import concourse.bacc as _bacc
    from concourse import mybir as _mybir
    from concourse.bass_utils import run_bass_kernel_spmd as _run

    nc = _bacc.Bacc("TRN2", target_bir_lowering=False, num_devices=1)
    arrays, args = {}, []
    for name in _INS:
        a = _np.ascontiguousarray(inputs[name])
        arrays[f"in_{name}_dram"] = a
        args.append(nc.dram_tensor(f"in_{name}_dram", a.shape, _mybir.dt.from_np(a.dtype), kind="ExternalInput").ap())
    b, n, c = inputs["x"].shape
    out = nc.dram_tensor("out_0_dram", (b, n, c), _mybir.dt.float32, kind="ExternalOutput").ap()
    xs = nc.dram_tensor("x_scratch", (b, P, n // P, c), _mybir.dt.float32, kind="Internal").ap()
    vs = nc.dram_tensor("v_scratch", (b, P, n // P, c + 1), _mybir.dt.float32, kind="Internal").ap()
    gnn_kernel(nc, *args, out, xs, vs)
    r = _run(nc, [arrays], core_ids=[0])
    return r.results[0]["out_0_dram"]
```

```python
from contextlib import ExitStack

import concourse.bass as bass
from concourse import mybir

ALU = mybir.AluOpType
ACT = mybir.ActivationFunctionType
AX = mybir.AxisListType.X
F32 = mybir.dt.float32
F16 = mybir.dt.float16
BF16 = mybir.dt.bfloat16
I32 = mybir.dt.int32

P = 128
CB = 4
MAT_SCALE = 1024.0
VEC_SCALE = 64.0
UNSCALE = 1.0 / (MAT_SCALE * VEC_SCALE)
ATT_SCALE = 1024.0
RING = 5
WARM = (40, 30, 20)
LATE = 4
STEEP = float(2 ** 40)
LN_EPS = 1e-5
BN_EPS = 1e-5
DEG_EPS = 1e-12
RSQRT_STEPS = 11
LN_STEPS = 6 + RSQRT_STEPS
U_SCALE = 16.0
W_SCALE = 256.0


class Chain:

    def __init__(self, eng, sem, base):
        self.eng, self.sem, self.base, self.n = eng, sem, base, 0

    def do(self, ins):
        ins.then_inc(self.sem, 1)
        self.n += 1

    def settle(self, back=0):
        self.eng.wait_ge(self.sem, self.base + (self.n - back))

    def link(self, ins):
        self.do(ins)
        self.settle()


def rsqrt(ch, eng, y, x, t):
    yi = y.bitcast(I32)
    ch.link(eng.tensor_scalar(t.bitcast(I32), x.bitcast(I32), 1, None, ALU.logical_shift_right))
    ch.link(eng.tensor_scalar(yi, t.bitcast(I32), -1.0, 1597463007.0, ALU.mult, ALU.add))
    for _ in range(3):
        ch.link(eng.scalar_tensor_tensor(out=t, in0=y, scalar=-0.5, in1=y, op0=ALU.mult, op1=ALU.mult))
        ch.link(eng.tensor_tensor(t, t, x, ALU.mult))
        ch.link(eng.scalar_tensor_tensor(out=y, in0=t, scalar=1.5, in1=y, op0=ALU.add, op1=ALU.mult))


def gnn_kernel(nc, x, adj, U, w_scale, L1W, L1a, W1, b1, W2, b2, W_ih, b_ih, W_hh, b_hh,
               gamma, beta, L3W, L3b, out, xs, vs):
    B, N, C = x.shape
    R = U.shape[1]
    NB = N // P
    NQ = NB // CB
    D = C + 1
    UK = 3 * R
    chunks = [(n, k) for n in range(NB) for k in range(n // CB + 1)]
    NCH = len(chunks)
    first_chunk = [chunks.index((n, 0)) for n in range(NB)]
    off_diag = [min(CB, n - CB * k) for n, k in chunks]
    up_index = [sum(1 for c in off_diag[:i] if c > 0) for i in range(NCH)]
    NUP = sum(1 for c in off_diag if c > 0)
    TCH = NB * NQ

    xv = x.rearrange("b (i p) c -> b p i c", p=P)
    outv = out.rearrange("b (i p) c -> b p i c", p=P)
    adj_rows = adj.rearrange("b (i p) m -> b i p m", p=P)
    adj_cols = adj.rearrange("b (i p) m -> b p i m", p=P)

    ctx = ExitStack()
    with ctx:
        def sb(name, shape, dt):
            return ctx.enter_context(nc.sbuf_tensor(name, shape, dt))

        def sem(name):
            return ctx.enter_context(nc.semaphore(name))

        mat = sb("mat", [P, NB, NB, 2, P], F16)
        rows = sb("rows", [P, 2, N], F32)
        cols = sb("cols", [P, 2, NB, P], F32)
        s1row = cols[:, 0, :, :].rearrange("p i c -> p (i c)")
        m1T = s1row
        h_att = s1row[:, 0:NB * C].rearrange("p (i c) -> p i c", c=C)
        c16 = cols[:, 1, :, :].rearrange("p i c -> p (i c)").bitcast(F16)
        hs = c16[:, 0:NB * P].rearrange("p (i c) -> p i c", c=P)
        hT = c16[:, NB * P:2 * NB * P]
        u_nat = cols[:, 0, :, :].rearrange("p i c -> p (i c)").bitcast(F16)[:, 0:2 * NB * UK] \
            .rearrange("p (o i c) -> p o i c", o=2, i=NB)
        cat = sb("cat", [P, NB, 2 * C + 1], F32)
        h = cat[:, :, C:2 * C]
        h1 = cat[:, :, C:2 * C + 1]
        xt = sb("xt", [P, NB, C], F32)
        vec = sb("vec", [P, NB, 2 * D], F16)
        vec_d = sb("vec_d", [P, NB, 2 * D], F16)
        u_st = vec_d[:, :, :].rearrange("p i c -> p (i c)")[0:UK, 0:N]
        vout = vec_d[:, :, :].bitcast(F32)
        tmp = sb("tmp", [P, NB, D], F32)
        scr = sb("scr", [P, 6 * 512], F32)
        a_sum_b = scr[:, 0:1024].rearrange("p (s n) -> p s n", s=2)
        s_sig_b = scr[:, 1024:2048].rearrange("p (s n) -> p s n", s=2)
        k_f32_b = scr[:, 2048:3072].rearrange("p (s n) -> p s n", s=2)
        half = scr[:, :].bitcast(F16).rearrange("p (s n) -> p s n", n=512)
        pos_b, neg_b = half[:, 0:RING, :], half[:, RING:2 * RING, :]
        t_rz = scr[:, 0:512].rearrange("p (i c) -> p i c", i=CB)
        t_pre = scr[:, 512:768].rearrange("p (i c) -> p i c", i=CB)
        t_n = scr[:, 768:1024].rearrange("p (i c) -> p i c", i=CB)
        t_w = scr[:, 1024:1280].rearrange("p (i c) -> p i c", i=CB)
        msum = scr[:, 1280:1280 + CB * D].rearrange("p (i c) -> p i c", i=CB)
        catT = scr[:, 1600:1600 + CB * P]
        yred = sb("yred", [P, 2, 8 * D], F32)
        u_mv = yred[:, :, :].rearrange("p a c -> p (a c)").bitcast(F16)[0:UK, 0:N]
        nsum = yred[:, 0, :].rearrange("p (s c) -> p s c", c=D)
        nwt = yred[:, 1, :].rearrange("p (s c) -> p s c", c=D)
        yq = sb("yq", [P, CB, C], F32)
        rsum = sb("rsum", [P, NB, NQ], F32)
        st = sb("st", [P, 8, NB], F32)
        mean, var, rstd, tn, dscale, deg, dinv, sqd = (st[:, i, :] for i in range(8))
        coef = sb("coef", [P, 4, NB], F32)
        s2st = sb("s2st", [P, NB], F32)
        small = sb("small", [P, 4], F32)
        wsc = sb("wsc", [P, 1], F32)
        ident = sb("ident", [P, P], F32)
        ident16 = sb("ident16", [P, P], F16)
        zeros16 = sb("zeros16", [P, P], F16)
        ones16 = sb("ones16", [P, P], F16)
        onesf = sb("onesf", [P, P], F32)
        wa_hi = sb("wa_hi", [P, C + 2], F16)
        wa_lo = sb("wa_lo", [P, C + 2], F16)
        wa1_hi = sb("wa1_hi", [P, P], F16)
        wa1_lo = sb("wa1_lo", [P, P], F16)
        w1_hi = sb("w1_hi", [P, C], F16)
        w1_lo = sb("w1_lo", [P, C], F16)
        w2s = sb("w2s", [C, C], F32)
        b1s = sb("b1s", [C, 1], F32)
        b2s = sb("b2s", [P, C], F32)
        wcat = sb("wcat", [P, 4 * C], F32)
        bias2 = sb("bias2", [C, 4 * C], F16)
        bn_sum = sb("bn_sum", [P, 2, C], F32)
        bn_part = yred[:, 1, 0:2 * C].rearrange("p (t c) -> p t c", t=2)
        bnv = sb("bnv", [C, 8], F32)
        gb = sb("gb", [C, 2], F32)
        w3s = yred[0:C, 1, 2 * C:3 * C]
        wfin = yred[0:D, 1, 3 * C:4 * C]
        b3row = yred[0:1, 1, 4 * C:5 * C]
        e_last = yred[0:1, 0, 2 * C:2 * C + D]
        a12 = scr[0:C, 0:2]
        g_rz = scr[:, 128:256]
        g_n = scr[:, 256:384]
        bih = scr[0:C, 384:384 + 3 * C]
        bhh = scr[0:C, 576:576 + 3 * C]
        bsum = scr[0:C, 768:1024]
        bhi = scr[0:C, 1024:1152].bitcast(F16)
        blo = scr[0:C, 1152:1280].bitcast(F16)
        waT = scr[0:C, 1280:1280 + P]
        wa = scr[:, 1408:1408 + C + 2]
        wa_s = scr[:, 1480:1480 + C + 2]
        w1s = scr[:, 1552:1552 + C]
        fold = yred[0:C, 0, 0:D]
        fin_v = [vec[:, :, :].bitcast(F32), vout]
        fin_x = [xt[:, :, :], tmp[:, :, 0:C]]
        fin_vt = [scr[:, 0:512], scr[:, 512:1024]]
        fin_r = [scr[:, 1024:1280], scr[:, 1280:1536]]
        fin_y = [scr[:, 1536:1792], scr[:, 1792:2048]]
        t_elu = scr[:, 2816:2816 + CB * C].rearrange("p (i c) -> p i c", c=C)

        tp = ctx.enter_context(nc.psum_tensor("tp", [P, 2, 512], F32))
        acc = [ctx.enter_context(nc.psum_tensor(f"acc{i}", [P, 3, 512], F32)) for i in range(2)]

        def t_bank(c, wide):
            return (tp[:, 0, :], tp[:, 1, :], acc[0][:, 2, :], acc[1][:, 2, :])[c % (4 if wide else 2)]

        s_ps = acc[0][:, 0:2, :]
        y_ps = acc[0][:, 2, :]
        deg_ps = acc[1][:, 2, 0:NB]
        k_ps = [acc[1][:, i, :].bitcast(F16) for i in range(2)]
        wh_ps = acc[0][:, 0:2, :].rearrange("p a (i c) -> p (a i) c", c=C)
        mx_ps = acc[0][:, 2, 128:257]
        s1_ps = [tp[:, 0, :], tp[:, 1, :], acc[1][:, 2, :], tp[:, 0, :]]
        hT_ps = [[acc[0][:, i, :].bitcast(F16) for i in range(2)], [acc[i][:, 2, :].bitcast(F16) for i in range(2)]]
        s12_ps = acc[0][:, 2, 0:2 * NB].rearrange("p (i t) -> p i t", t=2)
        m_ps = acc[1][:, 1:3, :].rearrange("p a (i c) -> p (a i) c", c=C)
        gate_ps = [acc[i][:, 2, :].rearrange("p (i c) -> p i c", c=4 * C) for i in range(2)]

        w_in, set_pe, set_dve, set_pool = (sem(n) for n in ("w_in", "set_pe", "set_dve", "set_pool"))
        row_in = [sem(f"row_in{i}") for i in range(2)]
        col_in = [sem(f"col_in{i}") for i in range(2)]
        arow_in = [sem(f"arow_in{i}") for i in range(2)]
        x0_in, xr_in, x1_out, x1_in = (sem(n) for n in ("x0_in", "xr_in", "x1_out", "x1_in"))
        x3_out, v3_out = sem("x3_out"), sem("v3_out")
        w3_in, e_set = sem("w3_in"), sem("e_set")
        fin_in = [sem(f"fin_in{i}") for i in range(2)]
        fin_out = [sem(f"fin_out{i}") for i in range(2)]
        at_done, slog_done, sig_done, asum_done, kf_done, khi_done, klo_done, kup_t, kup_done = (
            sem(n) for n in ("at_done", "slog_done", "sig_done", "asum_done", "kf_done", "khi_done",
                             "klo_done", "kup_t", "kup_done"))
        deg_done, deg_read, dh_done, v0_hi, v0_done, y_done, y_read, x1_done = (
            sem(n) for n in ("deg_done", "deg_read", "dh_done", "v0_hi", "v0_done", "y_done", "y_read", "x1_done"))
        ln0_step, h0_ready, deg_step, y_step, v_step, f_step = (
            sem(n) for n in ("ln0_step", "h0_ready", "deg_step", "y_step", "v_step", "f_step"))
        a2t_done, ahi_done, alo_done = (sem(n) for n in ("a2t_done", "ahi_done", "alo_done"))
        h_ready, ht_t, ht_cp, wh_mm, s1_mm, s1_cp, mx_in, mx_t, mx_r, mx_b = (sem(n) for n in (
            "h_ready", "ht_t", "ht_cp", "wh_mm", "s1_mm", "s1_cp", "mx_in", "mx_t", "mx_r", "mx_b"))
        nb_done, wh_read, hatt_ready, hs_hi, hs_lo, p_step = (sem(n) for n in (
            "nb_done", "wh_read", "hatt_ready", "hs_hi", "hs_lo", "p_step"))
        coef_in, coef_done, bw_ready, bw_hi, b_ready, g1_done, g2_pool, g2_dve, pos_done, g_used = (sem(n) for n in (
            "coef_in", "coef_done", "bw_ready", "bw_hi", "b_ready", "g1_done", "g2_pool", "g2_dve", "pos_done", "g_used"))
        acc_done, acc_read, elu_in, elu_exp, m1_mm, m1_cp, m_mm, m_sum, v_hi, v_ready = (sem(n) for n in (
            "acc_done", "acc_read", "elu_in", "elu_exp", "m1_mm", "m1_cp", "m_mm", "m_sum", "v_hi", "v_ready"))
        msg_in, msg_done, cat_t, cat_cp, gate_mm, rz_done, pre_done, n_done, gru_done = (sem(n) for n in (
            "msg_in", "msg_done", "cat_t", "cat_cp", "gate_mm", "rz_done", "pre_done", "n_done", "gru_done"))
        x3_ready, m3_in, v3_done = sem("x3_ready"), sem("m3_in"), sem("v3_done")
        f_mm, f_vt, f_vtcp, f_out, f_relu, f_y, f_add = (sem(n) for n in (
            "f_mm", "f_vt", "f_vtcp", "f_out", "f_relu", "f_y", "f_add"))

        def known(b, k):
            return isinstance(b, int) and b * NCH + k <= 0

        def pool_g2(g):
            return g - g // 3

        POOL_G2 = pool_g2(TCH)
        PREP_AT = (22, 38)
        HT_AT = 13

        block = ctx.enter_context(nc.Block())

        W_DMAS = 19
        SET_POOL, SET_IDENT, SET_WAT, SET_WA, SET_DVE = 10, 1, 16, 27, 29
        DEG_STEPS, V_STEPS = 3 + RSQRT_STEPS, 143
        F_SUMS, F_FOLD, F_ALL = 1, 21, 22

        @block.sync
        def _(sp):
            sp.dma_start(tmp[:, :, 0:R], U.rearrange("(i p) r -> p i r", p=P)).then_inc(w_in, 16)
            sp.dma_start(wsc[:, :], w_scale.partition_broadcast(P)).then_inc(w_in, 16)
            for o in (0, C):
                sp.dma_start(wa[o:o + C, 0:C], L1W).then_inc(w_in, 16)
                sp.dma_start(w1s[o:o + C, :], W1).then_inc(w_in, 16)
            for t in range(2):
                sp.dma_start(a12[:, t:t + 1], L1a[C * t:C * t + C, :]).then_inc(w_in, 16)
            sp.dma_start(w2s[:, :], W2).then_inc(w_in, 16)
            sp.dma_start(b1s[:, :], b1.rearrange("(c o) -> c o", o=1)).then_inc(w_in, 16)
            sp.dma_start(b2s[:, :], b2.partition_broadcast(P)).then_inc(w_in, 16)
            sp.dma_start(g_rz[:, 0:C], W_ih[0:2 * C, :]).then_inc(w_in, 16)
            sp.dma_start(g_rz[:, C:2 * C], W_hh[0:2 * C, :]).then_inc(w_in, 16)
            sp.wait_ge(set_pool, 1)
            sp.dma_start(g_n[0:C, 0:C], W_ih[2 * C:3 * C, :]).then_inc(w_in, 16)
            sp.dma_start(g_n[C:2 * C, C:2 * C], W_hh[2 * C:3 * C, :]).then_inc(w_in, 16)
            sp.dma_start(bih, b_ih.partition_broadcast(C)).then_inc(w_in, 16)
            sp.dma_start(bhh, b_hh.partition_broadcast(C)).then_inc(w_in, 16)
            sp.dma_start(gb[:, 0:1], gamma.rearrange("(c o) -> c o", o=1)).then_inc(w_in, 16)
            sp.dma_start(gb[:, 1:2], beta.rearrange("(c o) -> c o", o=1)).then_inc(w_in, 16)

            def load_step(b, n, first):
                s = n % 2
                if not (first and n < 2):
                    back = first_chunk[n - 1] if n >= 2 else first_chunk[NB - 1] - NCH if n == 0 else 0
                    sp.wait_ge(asum_done, b * NCH + back)
                sp.dma_start(rows[:, s, 0:(n + 1) * P], adj_rows[b, n, :, 0:(n + 1) * P]).then_inc(row_in[s], 16)
                if n > 0:
                    if first and n == 1:
                        sp.wait_ge(set_dve, SET_DVE)
                    sp.dma_start(cols[:, s, 0:n, :], adj_cols[b, :, 0:n, n * P:(n + 1) * P]).then_inc(col_in[s], 16)

            def load_residual(b):
                sp.dma_start(xt[:, :, :], xv[b]).then_inc(xr_in, 16)

            def store_x1(b):
                sp.wait_ge(x1_done, b * NQ + NQ)
                sp.dma_start(xs[b], xt[:, :, :]).then_inc(x1_out, 16)
                sp.wait_ge(x1_out, b * 16 + 16)

            sp.dma_start(h, xv[0]).then_inc(x0_in, 16)
            for n in range(NB):
                load_step(0, n, True)
            load_residual(0)
            with sp.Fori(1, B) as b:
                sp.wait_ge(v0_done, b)
                sp.dma_start(h, xv[b]).then_inc(x0_in, 16)
                for n in range(NB):
                    load_step(b, n, False)
                store_x1(b - 1)
                load_residual(b)

            def load_row(b, i, first):
                s = i % 2
                if first and i < 2:
                    sp.wait_ge(asum_done, B * NCH)
                else:
                    sp.wait_ge(a2t_done, b * TCH + NQ * (i - 1))
                sp.dma_start(rows[:, s, :], adj_rows[b, i]).then_inc(arow_in[s], 16)

            def store_x3(b):
                sp.wait_ge(gru_done, b * NQ + NQ)
                sp.dma_start(xs[b], xt[:, :, :]).then_inc(x3_out, 16)

            def store_v(b):
                sp.wait_ge(v3_done, b + 1)
                sp.dma_start(vs[b], vout).then_inc(v3_out, 16)

            for i in range(NB):
                load_row(0, i, True)
            store_x1(B - 1)
            sp.dma_start(xt[:, :, :], xs[0]).then_inc(x1_in, 16)
            with sp.Fori(0, B - 1) as b:
                store_x3(b)
                load_row(b + 1, 0, False)
                load_row(b + 1, 1, False)
                sp.wait_ge(x3_out, b * 16 + 16)
                sp.wait_ge(x3_ready, b * 2 + 2)
                sp.dma_start(xt[:, :, :], xs[b + 1]).then_inc(x1_in, 16)
                for i in range(2, NB):
                    load_row(b + 1, i, False)
                store_v(b)
            store_x3(B - 1)
            sp.dma_start(w3s, L3W).then_inc(w3_in, 16)
            sp.dma_start(b3row, L3b.rearrange("(o c) -> o c", o=1)).then_inc(w3_in, 16)
            store_v(B - 1)
            sp.wait_ge(x3_out, B * 16)
            sp.wait_ge(v3_out, B * 16 + 16)
            sp.wait_ge(f_step, F_ALL)

            def load_final(t, s):
                sp.dma_start(fin_v[s], vs[t * 2 + s]).then_inc(fin_in[s], 16)
                sp.dma_start(fin_x[s], xs[t * 2 + s]).then_inc(fin_in[s], 16)

            def store_final(t, s):
                sp.wait_ge(f_add, t * (2 * NQ) + (s + 1) * NQ)
                sp.dma_start(outv[t * 2 + s], fin_x[s]).then_inc(fin_out[s], 16)

            for s in range(2):
                load_final(0, s)
            with sp.Fori(0, B // 2 - 1) as t:
                for s in range(2):
                    store_final(t, s)
                for s in range(2):
                    sp.wait_ge(fin_out[s], t * 16 + 16)
                    load_final(t + 1, s)
            for s in range(2):
                store_final(B // 2 - 1, s)
            for s in range(2):
                sp.wait_ge(fin_out[s], 16 * (B // 2))

        USES = NB // 2

        def row_landed(eng, b, n):
            eng.wait_ge(row_in[n % 2], b * (16 * USES) + 16 * (n // 2 + 1))

        def col_landed(eng, b, n):
            uses, use = (USES - 1, n // 2) if n % 2 == 0 else (USES, n // 2 + 1)
            eng.wait_ge(col_in[n % 2], b * (16 * uses) + 16 * use)

        @block.tensor
        def _(pe):
            pe.wait_ge(set_pool, SET_POOL)
            pe.wait_ge(w_in, 16 * W_DMAS)
            pe.wait_ge(set_dve, SET_IDENT)
            pe.transpose(tp[0:C, 0, 0:P], wa[:, 0:C], ident[:, :])
            pe.transpose(tp[:, 0, P:2 * P], g_rz, ident[:, :])
            pe.transpose(tp[:, 0, 2 * P:3 * P], g_n, ident[:, :]).then_inc(set_pe, 1)
            pe.wait_ge(set_dve, SET_WAT)
            pe.matmul(tp[:, 1, 0:2], waT, a12, start=True, stop=True).then_inc(set_pe, 1)
            pe.wait_ge(set_dve, SET_WA)
            for o in range(2):
                for i in range(NB):
                    ins = pe.transpose(acc[o][0:UK, i // 8, :].bitcast(F16)[:, (i % 8) * P:(i % 8 + 1) * P],
                                       u_nat[:, o, i, :], ident16[:, :])
            ins.then_inc(set_pe, 1)
            pe.wait_ge(set_dve, SET_DVE)

            def k_step(b, n, late):
                for k in range(n // CB + 1):
                    ck = first_chunk[n] + k
                    m0, m1 = CB * k, min(CB * k + CB, n + 1)
                    if k == 0:
                        row_landed(pe, b, n)
                        if n > 0:
                            col_landed(pe, b, n)
                    if not known(b, ck - 1):
                        pe.wait_ge(asum_done, b * NCH + (ck - 1))
                        pe.wait_ge(sig_done, b * NCH + (ck - 1))
                    for m in range(m0, m1):
                        src = cols[:, n % 2, m, :] if m < n else rows[:, n % 2, n * P:(n + 1) * P]
                        ins = pe.transpose(tp[:, ck % 2, (m - m0) * P:(m - m0 + 1) * P], src, ident[:, :])
                    ins.then_inc(at_done, 1)
                    pe.matmul(s_ps[:, ck % 2, 0:(m1 - m0) * P], u_st[:, n * P:(n + 1) * P],
                              u_mv[:, m0 * P:m1 * P], start=True, stop=True).then_inc(slog_done, 1)
                    late.append(ck)
                    if len(late) > LATE:
                        upper(b, late.pop(0))

            def upper(b, ck):
                n, k = chunks[ck]
                off, u = off_diag[ck], up_index[ck]
                if off <= 0:
                    return
                pe.wait_ge(klo_done, b * NCH + (ck + 1))
                if u == 0:
                    if not known(b, 0):
                        pe.wait_ge(deg_read, b)
                    pe.matmul(deg_ps, zeros16[:, :], zeros16[:, 0:NB], start=True, stop=False,
                              skip_group_check=True)
                if not (isinstance(b, int) and b == 0 and u < 2):
                    pe.wait_ge(kup_done, b * NUP + (u - 1))
                for m in range(CB * k, CB * k + off):
                    for part in range(2):
                        pe.matmul(deg_ps[:, m:m + 1], mat[:, n, m, part, :], ones16[:, 0:1],
                                  start=False, stop=False, skip_group_check=True)
                        c = (m - CB * k) * 2 + part
                        ins = pe.transpose(k_ps[u % 2][:, c * P:(c + 1) * P], mat[:, n, m, part, :], ident16[:, :])
                ins.then_inc(kup_t, 1)

            def finish_k(b, late):
                while late:
                    upper(b, late.pop(0))
                pe.matmul(deg_ps, zeros16[:, :], zeros16[:, 0:NB], start=False, stop=True,
                          skip_group_check=True).then_inc(deg_done, 1)

            def y_block(b, i, part=None):
                if part is not None and part > 0:
                    pass
                elif i == 0:
                    pe.wait_ge(v0_done, b + 1)
                    pe.wait_ge(kup_done, b * NUP + NUP)
                elif i % CB == 0:
                    pe.wait_ge(y_read, b * NQ + i // CB)
                o = (i % CB) * P
                for j in range(NB) if part is None else range(CB * part, CB * part + CB):
                    pe.matmul(y_ps[:, o:o + P], mat[:, j, i, 0, :], vec[:, j, 0:2 * C],
                              start=(j == 0), stop=False, skip_group_check=True)
                    ins = pe.matmul(y_ps[:, o:o + C], mat[:, j, i, 1, :], vec[:, j, 0:C],
                                    start=False, stop=(j == NB - 1), skip_group_check=True)
                if i % CB == CB - 1 and part in (None, NQ - 1):
                    ins.then_inc(y_done, 1)

            late = []
            for n in range(NB):
                k_step(0, n, late)
            finish_k(0, late)
            with pe.Fori(1, B) as b:
                for n in range(NB):
                    y_block(b - 1, n)
                    k_step(b, n, late)
                finish_k(b, late)

            def a_step(b, i, wide, beside=None):
                pe.wait_ge(arow_in[i % 2], b * (16 * USES) + 16 * (i // 2 + 1))
                for k in range(NQ):
                    c = i * NQ + k
                    ring = 4 if wide else 2
                    if c >= ring:
                        pe.wait_ge(alo_done, b * TCH + (c - ring + 1))
                    for j in range(CB):
                        ins = pe.transpose(t_bank(c, wide)[:, j * P:(j + 1) * P],
                                           rows[:, i % 2, (CB * k + j) * P:(CB * k + j + 1) * P], ident[:, :])
                    ins.then_inc(a2t_done, 1)
                    if beside is not None:
                        beside(k)

            y_block(B - 1, 0)
            for n in range(NB):
                a_step(0, n, False, (lambda k: y_block(B - 1, n + 1, k)) if n + 1 < NB else None)

            def vec_part(a, o, i, js):
                for j in js:
                    pe.matmul(a[:, o:o + 2 * D], mat[:, j, i, 0, :], vec[:, j, :],
                              start=(j == 0), stop=False, skip_group_check=True)
                    ins = pe.matmul(a[:, o:o + D], mat[:, j, i, 1, :], vec[:, j, 0:D],
                                    start=False, stop=(j == NB - 1), skip_group_check=True)
                return ins

            def h_transposed(b, layer):
                use = b * 2 + (layer - 1)
                for half in range(2):
                    pe.wait_ge(hs_lo, use * 2 + (half + 1))
                    for i in range(8):
                        ins = pe.transpose(hT_ps[layer - 1][half][:, i * P:(i + 1) * P], hs[:, 8 * half + i, :], ident16[:, :])
                    ins.then_inc(ht_t, 1)

            def stay_warm(bank, n):
                for _ in range(n):
                    pe.matmul(bank, zeros16[:, :], hT[:, 0:512], start=True, stop=True)

            def split_product(dst, hT_part, w_hi, w_lo, h_stationary):
                for part, w, rows_ in ((0, w_hi, P), (1, w_lo, C)):
                    a, v = (hT_part, w) if h_stationary else (w, hT_part)
                    ins = pe.matmul(dst, a[0:rows_], v[0:rows_], start=(part == 0), stop=(part == 1))
                return ins

            def layer1(b):
                pe.wait_ge(alo_done, b * TCH + TCH)
                pe.wait_ge(ht_cp, b * 4 + 2)
                for i in range(NB):
                    nodes = hT[:, i * P:(i + 1) * P]
                    split_product(wh_ps[:, i, :], nodes, wa_hi[:, 0:C], wa_lo[:, 0:C], True)
                    ins = split_product(s12_ps[:, i, :], nodes, wa_hi[:, C:C + 2], wa_lo[:, C:C + 2], True)
                ins.then_inc(wh_mm, 1)
                for c in range(NQ):
                    if c == 3:
                        pe.wait_ge(s1_cp, b * NQ + 1)
                    split_product(s1_ps[c], hT[:, c * 512:(c + 1) * 512], wa1_hi, wa1_lo, False).then_inc(s1_mm, 1)
                pe.wait_ge(mx_in, b + 1)
                pe.transpose(mx_ps[0:1, 0:P], small[:, 0:1], ident[:, :]).then_inc(mx_t, 1)
                pe.wait_ge(mx_r, b + 1)
                pe.matmul(mx_ps[:, P:P + 1], onesf[0:1, :], small[0:1, 1:2], start=True, stop=True) \
                    .then_inc(mx_b, 1)
                pe.wait_ge(s1_cp, b * NQ + NQ)
                stay_warm(tp[:, 0, :], WARM[2])
                pe.wait_ge(b_ready, b * 2 + 1)
                pe.wait_ge(wh_read, b + 1)
                for q in range(NQ):
                    a = acc[q % 2]
                    if q >= 2:
                        pe.wait_ge(acc_read, b * (3 * NQ) + (q - 1))
                    for bank in range(3):
                        pe.matmul(a[:, bank, 0:3 * 2 * D], zeros16[:, :],
                                  vec[:, 0:3, :].rearrange("p i c -> p (i c)"),
                                  start=True, stop=False, skip_group_check=True)
                    for j in range(NB):
                        g = q * NB + j
                        if g == NB // 2:
                            pe.wait_ge(b_ready, b * 2 + 2)
                        if g % 3 < 2:
                            pe.wait_ge(g2_pool, b * POOL_G2 + pool_g2(g + 1))
                        else:
                            pe.wait_ge(g2_dve, b * (TCH - POOL_G2) + (g + 1 - pool_g2(g + 1)))
                        for s in range(2 * CB):
                            m = (pos_b, neg_b)[s // CB][:, g % RING, (s % CB) * P:(s % CB + 1) * P]
                            ins = pe.matmul(a[:, s // 3, (s % 3) * 2 * D:(s % 3 + 1) * 2 * D], m,
                                            (vec, vec_d)[s // CB][:, j, :], start=False,
                                            stop=(j == NB - 1), skip_group_check=True)
                        ins.then_inc(g_used, 1)
                    pe.matmul(a[:, 2, 2 * 2 * D:3 * 2 * D], zeros16[:, :], vec[:, 0, :], start=False, stop=True,
                              skip_group_check=True).then_inc(acc_done, 1)

            def layer2(b):
                pe.wait_ge(acc_read, b * (3 * NQ) + (NQ - 1))
                stay_warm(acc[0][:, 0, :], WARM[0])
                h_transposed(b, 2)
                for c in range(NQ):
                    pe.wait_ge(ht_cp, b * 4 + 2 + (c // 2 + 1))
                    split_product(acc[0][0:C, c, :] if c < 2 else acc[1][0:C, 0, :] if c == 2 else tp[0:C, 0, :],
                                  hT[:, c * 512:(c + 1) * 512], w1_hi, w1_lo, False).then_inc(m1_mm, 1)
                for c in range(NQ):
                    pe.wait_ge(m1_cp, b * NQ + (c + 1))
                    for i in range(CB * c, CB * c + CB):
                        ins = pe.matmul(m_ps[:, i, :], m1T[0:C, i * P:(i + 1) * P], w2s[:, :], start=True, stop=True)
                    if c % 2 == 1:
                        ins.then_inc(m_mm, 1)
                pe.wait_ge(v_ready, b * 4 + 2)
                for q in range(NQ):
                    if q >= 2:
                        pe.wait_ge(acc_read, b * (3 * NQ) + NQ + (q - 1))
                    for i in range(CB):
                        ins = vec_part(acc[q % 2][:, i // 2, :], (i % 2) * 2 * D, CB * q + i, range(NB))
                        if i == CB - 1:
                            ins.then_inc(acc_done, 1)
                        if q >= 1 and i == 1:
                            cat_transposed(b, q - 1)
                        if q >= 1 and i == 2:
                            gates(b, q - 1)
                cat_transposed(b, NQ - 1)
                gates(b, NQ - 1)

            def cat_transposed(b, q):
                pe.wait_ge(msg_done, b * NQ + (q + 1))
                for i in range(CB):
                    ins = pe.transpose(tp[:, q % 2, i * P:(i + 1) * P], cat[:, CB * q + i, 0:2 * C], ident[:, :])
                ins.then_inc(cat_t, 1)

            def gates(b, q):
                pe.wait_ge(cat_cp, b * NQ + (q + 1))
                if q >= 1:
                    pe.wait_ge(pre_done, b * NQ + q)
                for i in range(CB):
                    g = gate_ps[i // 2][:, i % 2, :]
                    pe.matmul(g, catT[:, i * P:(i + 1) * P], wcat[:, :], start=True, stop=False)
                    ins = pe.matmul(g, ones16[0:C, :], bias2[:, :], start=False, stop=True)
                ins.then_inc(gate_mm, 1)

            def layer3(b, follow):
                pe.wait_ge(acc_read, b * (3 * NQ) + NQ + (NQ - 1))
                stay_warm(acc[0][:, 0, :], WARM[1])
                pe.wait_ge(v_ready, b * 4 + 4)

                def block_part(i, k):
                    q = i // CB
                    if q >= 2 and i % CB == 0 and k == 0:
                        pe.wait_ge(acc_read, b * (3 * NQ) + 2 * NQ + (q - 1))
                    ins = vec_part(acc[q % 2][:, (i % CB) // 2, :], (i % 2) * 2 * D, i, range(CB * k, CB * k + CB))
                    if i % CB == CB - 1 and k == NQ - 1:
                        ins.then_inc(acc_done, 1)

                for k in range(NQ):
                    block_part(0, k)
                for i in range(NB):
                    if follow and i == HT_AT:
                        pe.wait_ge(acc_read, b * (3 * NQ) + 2 * NQ + 3)
                        h_transposed(b + 1, 1)
                    if follow:
                        a_step(b + 1, i, True, (lambda k: block_part(i + 1, k)) if i + 1 < NB else None)
                    elif i + 1 < NB:
                        for k in range(NQ):
                            block_part(i + 1, k)

            pe.wait_ge(sig_done, B * NCH)
            h_transposed(0, 1)
            with pe.Fori(0, B - 1) as b:
                layer1(b)
                layer2(b)
                layer3(b, True)
            layer1(B - 1)
            layer2(B - 1)
            layer3(B - 1, False)

            pe.wait_ge(f_step, F_SUMS)
            pe.matmul(tp[0:C, 0, 0:1], bn_sum[:, 0, :], onesf[:, 0:1], start=True, stop=True)
            pe.matmul(tp[0:C, 0, 1:2], bn_sum[:, 1, :], onesf[:, 0:1], start=True, stop=True).then_inc(f_mm, 1)
            pe.wait_ge(f_step, F_FOLD)
            pe.wait_ge(w3_in, 32)
            pe.wait_ge(e_set, 2)
            pe.matmul(tp[0:D, 1, 0:C], fold, w3s, start=True, stop=False)
            pe.matmul(tp[0:D, 1, 0:C], e_last, b3row, start=False, stop=True).then_inc(f_mm, 1)
            pe.wait_ge(f_step, F_ALL)
            with pe.Fori(0, B // 2) as t:
                for s in range(2):
                    pe.wait_ge(fin_in[s], t * 32 + 32)
                    for q in range(NQ):
                        c = s * NQ + q
                        if c >= 2:
                            pe.wait_ge(f_vtcp, t * (2 * NQ) + (c - 1))
                        for i in range(CB):
                            ins = pe.transpose(tp[0:D, c % 2, i * P:(i + 1) * P], fin_v[s][:, CB * q + i, :], ident[:, :])
                        ins.then_inc(f_vt, 1)
                        pe.wait_ge(f_vtcp, t * (2 * NQ) + (c + 1))
                        if c >= 2:
                            pe.wait_ge(f_y, t * (2 * NQ) + (c - 1))
                        for i in range(CB):
                            ins = pe.matmul(acc[c % 2][:, 0, i * C:(i + 1) * C], fin_vt[c % 2][0:D, i * P:(i + 1) * P],
                                            wfin, start=True, stop=True)
                        ins.then_inc(f_out, 1)
                pe.wait_ge(f_y, t * (2 * NQ) + 2 * NQ)

        @block.scalar
        def _(act):
            def k_sig(b, ck):
                w = (min(CB, chunks[ck][0] + 1 - CB * chunks[ck][1])) * P
                act.wait_ge(slog_done, b * NCH + (ck + 1))
                if not known(b, ck - 1):
                    act.wait_ge(kf_done, b * NCH + (ck - 1))
                act.activation(s_sig_b[:, ck % 2, 0:w], s_ps[:, ck % 2, 0:w], ACT.Sigmoid,
                               scale=1.0 / (U_SCALE * U_SCALE)).then_inc(sig_done, 1)

            def k_hi(b, ck):
                n, k = chunks[ck]
                m0, m1 = CB * k, min(CB * k + CB, n + 1)
                act.wait_ge(kf_done, b * NCH + (ck + 1))
                act.activation(mat[:, n, m0:m1, 0, :],
                               k_f32_b[:, ck % 2, 0:(m1 - m0) * P].rearrange("p (i c) -> p i c", c=P),
                               ACT.Copy).then_inc(khi_done, 1)

            def k_up(b, ck):
                n, k = chunks[ck]
                off, u = off_diag[ck], up_index[ck]
                if off <= 0:
                    return
                act.wait_ge(kup_t, b * NUP + (u + 1))
                act.activation(mat[:, CB * k:CB * k + off, n, :, :],
                               k_ps[u % 2][:, 0:off * 2 * P].rearrange("p (m s c) -> p m s c", s=2, c=P),
                               ACT.Copy).then_inc(kup_done, 1)

            def k_batch(b):
                for ck in range(NCH + LATE + 1):
                    if ck < NCH:
                        k_sig(b, ck)
                    if 1 <= ck <= NCH:
                        k_hi(b, ck - 1)
                    if ck >= LATE + 1:
                        k_up(b, ck - LATE - 1)
                act.wait_ge(dh_done, b + 1)
                act.activation(vec[:, :, 0:C], tmp[:, :, 0:C], ACT.Copy, scale=VEC_SCALE).then_inc(v0_hi, 1)

            k_batch(0)
            with act.Fori(1, B) as b:
                k_batch(b)

            def a_hi(b, c, wide):
                i, k = c // NQ, c % NQ
                act.wait_ge(a2t_done, b * TCH + (c + 1))
                act.activation(mat[:, CB * k:CB * k + CB, i, 0, :],
                               t_bank(c, wide).rearrange("p (j c) -> p j c", c=P), ACT.Copy,
                               scale=MAT_SCALE).then_inc(ahi_done, 1)

            for c in range(TCH):
                a_hi(0, c, False)

            def h_parts(b, layer, half):
                src, ready = (h_att, hatt_ready) if layer == 1 else (h, h_ready)
                act.wait_ge(ready, b * 2 + (half + 1))
                s = slice(8 * half, 8 * half + 8)
                act.activation(hs[:, s, 0:C], src[:, s, :], ACT.Copy).then_inc(hs_hi, 1)

            def h_copy(b, layer):
                for half in range(2):
                    act.wait_ge(ht_t, (b * 2 + (layer - 1)) * 2 + (half + 1))
                    act.activation(hT[:, half * 8 * P:(half + 1) * 8 * P], hT_ps[layer - 1][half], ACT.Copy).then_inc(ht_cp, 1)

            def layer1(b):
                for c in range(NQ):
                    act.wait_ge(s1_mm, b * NQ + (c + 1))
                    act.activation(s1row[:, c * 512:(c + 1) * 512], s1_ps[c], ACT.Copy,
                                   scale=1.0 / W_SCALE).then_inc(s1_cp, 1)
                act.wait_ge(coef_in, b + 1)
                act.activation(coef[:, :, :], coef[:, :, :], ACT.Exp, scale=1.0 / W_SCALE).then_inc(coef_done, 1)
                for half in range(2):
                    for t in range(2):
                        act.wait_ge(bw_ready, b * 4 + (2 * half + t + 1))
                        if half == 0 and t == 1:
                            act.wait_ge(v3_out, b * 16 + 16)
                        act.activation((vec, vec_d)[t][:, 8 * half:8 * half + 8, 0:D], tmp[:, 8 * t:8 * t + 8, :],
                                       ACT.Copy).then_inc(bw_hi, 1)
                for g in range(TCH):
                    q, j = g // NB, g % NB
                    if g >= RING:
                        act.wait_ge(g_used, b * TCH + (g - RING + 1))
                    act.activation(pos_b[:, g % RING, :], s1row[:, q * 512:(q + 1) * 512], ACT.Sigmoid,
                                   bias=s2st[:, j:j + 1], scale=STEEP).then_inc(pos_done, 1)
                    if q >= 1 and j == 5:
                        elu(b, q - 1)
                elu(b, NQ - 1)

            def elu(b, q):
                act.wait_ge(elu_in, b * NQ + (q + 1))
                act.activation(t_elu, t_elu, ACT.Exp).then_inc(elu_exp, 1)

            def layer2(b):
                for half in range(2):
                    h_parts(b, 2, half)
                h_copy(b, 2)
                for c in range(NQ):
                    act.wait_ge(m1_mm, b * NQ + (c + 1))
                    src = acc[0][0:C, c, :] if c < 2 else acc[1][0:C, 0, :] if c == 2 else tp[0:C, 0, :]
                    act.activation(m1T[0:C, c * 512:(c + 1) * 512], src, ACT.Relu, bias=b1s[:, 0:1],
                                   scale=1.0 / W_SCALE).then_inc(m1_cp, 1)
                for half in range(2):
                    s = slice(8 * half, 8 * half + 8)
                    act.wait_ge(m_sum, b * 2 + (half + 1))
                    act.activation(vec[:, s, 0:C], tmp[:, s, 0:C], ACT.Relu, scale=VEC_SCALE).then_inc(v_hi, 1)

                def gate_copies(q):
                    act.wait_ge(cat_t, b * NQ + (q + 1))
                    if q >= 1:
                        act.wait_ge(gate_mm, b * NQ + q)
                    act.activation(catT, tp[:, q % 2, :], ACT.Copy).then_inc(cat_cp, 1)
                    act.wait_ge(gate_mm, b * NQ + (q + 1))
                    if q >= 1:
                        act.wait_ge(gru_done, b * NQ + q)
                    for i in range(2):
                        ins = act.activation(t_rz[:, 2 * i:2 * i + 2, :], gate_ps[i][:, :, 0:2 * C], ACT.Tanh, scale=0.5)
                    ins.then_inc(rz_done, 1)

                def n_gate(q):
                    act.wait_ge(pre_done, b * NQ + (q + 1))
                    act.activation(t_n, t_pre, ACT.Tanh).then_inc(n_done, 1)

                for q in range(NQ):
                    if q >= 1:
                        gate_copies(q - 1)
                    act.wait_ge(msg_in, b * NQ + (q + 1))
                    act.activation(cat[:, CB * q:CB * q + CB, 0:C], msum[:, :, 0:C], ACT.Relu,
                                   scale=UNSCALE).then_inc(msg_done, 1)
                    if q >= 1:
                        n_gate(q - 1)
                gate_copies(NQ - 1)
                n_gate(NQ - 1)

            def layer3(b, follow):
                for half in range(2):
                    s = slice(8 * half, 8 * half + 8)
                    act.wait_ge(m3_in, b * 2 + (half + 1))
                    act.activation(vec[:, s, 0:D], tmp[:, s, :], ACT.Copy, scale=VEC_SCALE).then_inc(v_hi, 1)
                if follow:
                    for c in range(TCH):
                        a_hi(b + 1, c, True)
                        if c in PREP_AT:
                            h_parts(b + 1, 1, PREP_AT.index(c))
                        if c == HT_AT * NQ:
                            h_copy(b + 1, 1)

            for half in range(2):
                h_parts(0, 1, half)
            h_copy(0, 1)
            with act.Fori(0, B - 1) as b:
                layer1(b)
                layer2(b)
                layer3(b, True)
            layer1(B - 1)
            layer2(B - 1)
            layer3(B - 1, False)

            with act.Fori(0, B // 2) as t:
                for c in range(2 * NQ):
                    act.wait_ge(f_vt, t * (2 * NQ) + (c + 1))
                    act.activation(fin_vt[c % 2][0:D, :], tp[0:D, c % 2, :], ACT.Copy).then_inc(f_vtcp, 1)
                    act.wait_ge(f_out, t * (2 * NQ) + (c + 1))
                    if c >= 2:
                        act.wait_ge(f_y, t * (2 * NQ) + (c - 1))
                    act.activation(fin_r[c % 2], acc[c % 2][:, 0, 0:CB * C], ACT.Relu, scale=0.99).then_inc(f_relu, 1)

        @block.gpsimd
        def _(pool):
            pool.memset(g_n, 0.0).then_inc(set_pool, 1)
            pool.memset(ident[:, :], 0.0).then_inc(set_pool, 1)
            pool.wait_ge(set_pool, 2)
            pool.affine_select(out=ident[:, :], in_=ident[:, :], compare_op=ALU.not_equal, fill=1.0, base=0,
                               pattern=[[-1, P]], channel_multiplier=1).then_inc(set_pool, 1)
            pool.memset(onesf[:, :], 1.0).then_inc(set_pool, 1)
            pool.memset(zeros16[:, :], 0.0).then_inc(set_pool, 1)
            pool.memset(ones16[:, :], 1.0).then_inc(set_pool, 1)
            pool.memset(bn_sum[:, :, :], 0.0).then_inc(set_pool, 1)
            pool.memset(bias2[:, :], 0.0).then_inc(set_pool, 1)
            pool.memset(cat[:, :, 2 * C:2 * C + 1], 1.0).then_inc(set_pool, 1)
            pool.memset(rsum[:, :, :], 0.0).then_inc(set_pool, 1)
            pool.memset(small[:, 3:4], 0.0).then_inc(v3_out, 16)

            with pool.Fori(0, B) as b:
                for ck, (n, k) in enumerate(chunks):
                    m0, m1 = CB * k, min(CB * k + CB, n + 1)
                    pool.wait_ge(khi_done, b * NCH + (ck + 1))
                    pool.tensor_tensor(mat[:, n, m0:m1, 1, :],
                                       k_f32_b[:, ck % 2, 0:(m1 - m0) * P].rearrange("p (i c) -> p i c", c=P),
                                       mat[:, n, m0:m1, 0, :], ALU.subtract).then_inc(klo_done, 1)
            with pool.Fori(0, B) as b:
                for g in range(TCH):
                    if g % 3 < 2:
                        pool.wait_ge(g1_done, b * TCH + (g + 1))
                        pool.tensor_tensor(neg_b[:, g % RING, :], neg_b[:, g % RING, :], pos_b[:, g % RING, :],
                                           ALU.subtract).then_inc(g2_pool, 1)
            pool.wait_ge(x3_ready, 2 * B)
            pool.memset(e_last[:, 0:C], 0.0).then_inc(e_set, 1)
            pool.memset(e_last[:, C:D], 1.0).then_inc(e_set, 1)

        @block.vector
        def _(dve):
            def centred(ch, src, dst, blocks):
                s = slice(*blocks)
                wide = [P, blocks[1] - blocks[0], C]
                src, sq, xc = src[:, s, :], dst[:, s, :], tmp[:, s, 0:C]
                mean, var = (st[:, i, s] for i in range(2))
                ch.link(dve.tensor_reduce(mean, src, AX, ALU.add))
                ch.link(dve.tensor_scalar(mean, mean, -1.0 / C, None, ALU.mult))
                ch.link(dve.tensor_tensor(xc, src, mean.unsqueeze(2).to_broadcast(wide), ALU.add))
                ch.link(dve.tensor_tensor(sq, xc, xc, ALU.mult))
                ch.link(dve.tensor_reduce(var, sq, AX, ALU.add))
                ch.link(dve.tensor_scalar(var, var, 1.0 / C, LN_EPS, ALU.mult, ALU.add))

            def scaled(dst, ready, blocks):
                s = slice(*blocks)
                wide = [P, blocks[1] - blocks[0], C]
                dve.scalar_tensor_tensor(out=dst[:, s, :], in0=tmp[:, s, 0:C], scalar=0.0,
                                         in1=rstd[:, s].unsqueeze(2).to_broadcast(wide),
                                         op0=ALU.max, op1=ALU.mult).then_inc(ready, 1)

            def layer_norm(ch, src, dst, ready, blocks=(0, NB)):
                s = slice(*blocks)
                centred(ch, src, dst, blocks)
                rsqrt(ch, dve, rstd[:, s], var[:, s], tn[:, s])
                scaled(dst, ready, blocks)

            dve.wait_ge(set_pool, SET_POOL)
            dve.wait_ge(w_in, 16 * W_DMAS)
            ch = Chain(dve, set_dve, 0)
            u16 = tmp[:, :, R:2 * R]
            ch.link(dve.tensor_copy(ident16[:, :], ident[:, :]))
            assert ch.n == SET_IDENT
            ch.link(dve.tensor_scalar(u16, tmp[:, :, 0:R], U_SCALE, None, ALU.mult))
            ch.link(dve.tensor_copy(u_nat[:, 0, :, 0:R], u16))
            ch.link(dve.tensor_tensor(u_nat[:, 0, :, 2 * R:3 * R], u16, u_nat[:, 0, :, 0:R], ALU.subtract))
            ch.do(dve.tensor_copy(u_nat[:, 0, :, R:2 * R], u_nat[:, 0, :, 0:R]))
            ch.do(dve.tensor_copy(u_nat[:, 1, :, 0:R], u_nat[:, 0, :, 0:R]))
            ch.do(dve.tensor_copy(u_nat[:, 1, :, R:2 * R], u_nat[:, 0, :, 2 * R:3 * R]))
            ch.do(dve.tensor_copy(u_nat[:, 1, :, 2 * R:3 * R], u_nat[:, 0, :, 0:R]))
            ch.do(dve.tensor_tensor(bsum[:, 0:2 * C], bih[:, 0:2 * C], bhh[:, 0:2 * C], ALU.add))
            ch.do(dve.tensor_copy(bsum[:, 2 * C:3 * C], bih[:, 2 * C:3 * C]))
            ch.link(dve.tensor_copy(bsum[:, 3 * C:4 * C], bhh[:, 2 * C:3 * C]))
            ch.link(dve.tensor_copy(bhi, bsum))
            ch.link(dve.tensor_tensor(blo, bsum, bhi, ALU.subtract))
            ch.do(dve.tensor_copy(bias2[0:1, :], bhi[0:1, :]))
            ch.do(dve.tensor_copy(bias2[32:33, :], blo[32:33, :]))
            dve.wait_ge(set_pe, 1)
            ch.do(dve.tensor_copy(waT, tp[0:C, 0, 0:P]))
            assert ch.n == SET_WAT, ch.n
            ch.do(dve.tensor_copy(wcat[:, 0:P], tp[:, 0, P:2 * P]))
            ch.do(dve.tensor_copy(wcat[:, P:2 * P], tp[:, 0, 2 * P:3 * P]))
            dve.wait_ge(set_pe, 2)
            ch.link(dve.tensor_copy(wa[:, C:C + 2], tp[:, 1, 0:2]))
            ch.link(dve.tensor_scalar(wa_s, wa, W_SCALE, None, ALU.mult))
            ch.link(dve.tensor_copy(wa_hi[:, :], wa_s))
            ch.do(dve.tensor_tensor(wa_lo[:, :], wa_s, wa_hi[:, :], ALU.subtract))
            ch.link(dve.tensor_scalar(w1s, w1s, W_SCALE, None, ALU.mult))
            ch.link(dve.tensor_copy(w1_hi[:, :], w1s))
            ch.do(dve.tensor_tensor(w1_lo[:, :], w1s, w1_hi[:, :], ALU.subtract))
            ch.do(dve.tensor_copy(wa1_hi[:, :], wa_hi[:, C:C + 1].to_broadcast([P, P])))
            ch.link(dve.tensor_copy(wa1_lo[:, :], wa_lo[:, C:C + 1].to_broadcast([P, P])))
            assert ch.n == SET_WA, ch.n
            dve.wait_ge(set_pe, 3)
            for o, dst in enumerate((u_st, u_mv)):
                ch.do(dve.tensor_copy(dst.rearrange("p (a c) -> p a c", a=2),
                                      acc[o][0:UK, 0:2, :].bitcast(F16)))
            assert ch.n == SET_DVE, ch.n
            ch.settle()

            def k_sum(b, ck):
                n, k = chunks[ck]
                w = min(CB, n + 1 - CB * k) * P
                if k == 0:
                    row_landed(dve, b, n)
                dve.wait_ge(at_done, b * NCH + (ck + 1))
                if not known(b, ck - 1):
                    dve.wait_ge(kf_done, b * NCH + (ck - 1))
                dve.tensor_tensor(a_sum_b[:, ck % 2, 0:w], rows[:, n % 2, CB * k * P:CB * k * P + w],
                                  tp[:, ck % 2, 0:w], ALU.add).then_inc(asum_done, 1)

            def k_mul(b, ck):
                n, k = chunks[ck]
                w = min(CB, n + 1 - CB * k) * P
                dve.wait_ge(sig_done, b * NCH + (ck + 1))
                dve.wait_ge(asum_done, b * NCH + (ck + 1))
                if not known(b, ck - 1):
                    dve.wait_ge(klo_done, b * NCH + (ck - 1))
                dve.scalar_tensor_tensor(out=k_f32_b[:, ck % 2, 0:w], in0=a_sum_b[:, ck % 2, 0:w],
                                         scalar=0.5 * MAT_SCALE, in1=s_sig_b[:, ck % 2, 0:w], op0=ALU.mult,
                                         op1=ALU.mult, accum_out=rsum[:, n, k:k + 1]).then_inc(kf_done, 1)

            def y_post(b, q):
                dve.wait_ge(y_done, b * NQ + (q + 1))
                if q == 0:
                    dve.wait_ge(xr_in, b * 16 + 16)
                dve.tensor_reduce(yq[:, :, :], y_ps.rearrange("p (i s c) -> p i c s", s=2, c=C), AX,
                                  ALU.add).then_inc(y_read, 1)
                dve.wait_ge(y_read, b * NQ + (q + 1))
                dve.tensor_tensor(yq[:, :, :], yq[:, :, :],
                                  dscale[:, CB * q:CB * q + CB].unsqueeze(2).to_broadcast([P, CB, C]),
                                  ALU.mult).then_inc(y_step, 1)
                dve.wait_ge(y_step, b * NQ + (q + 1))
                dve.tensor_tensor(xt[:, CB * q:CB * q + CB, :], xt[:, CB * q:CB * q + CB, :], yq[:, :, :],
                                  ALU.add).then_inc(x1_done, 1)
                dve.wait_ge(x1_done, b * NQ + (q + 1))

            def k_batch(b, last):
                for ck in range(NCH + 1):
                    n = chunks[ck][0] if ck < NCH else NB
                    if last is not None and n % CB == 0 and n > 0 and (n == NB or chunks[ck][1] == 0):
                        y_post(last, n // CB - 1)
                    if ck < NCH:
                        k_sum(b, ck)
                    if ck >= 1:
                        k_mul(b, ck - 1)
                    if ck < NCH and chunks[ck][1] == 0:
                        if n == 11:
                            dve.wait_ge(x0_in, b * 16 + 16)
                            ch = Chain(dve, ln0_step, b * LN_STEPS)
                            layer_norm(ch, h, h, h0_ready)
                            assert ch.n == LN_STEPS
                ch = Chain(dve, deg_step, b * DEG_STEPS)
                dve.wait_ge(kf_done, b * NCH + NCH)
                ch.link(dve.tensor_reduce(deg, rsum[:, :, :], AX, ALU.add))
                dve.wait_ge(deg_done, b + 1)
                dve.tensor_tensor(deg, deg, deg_ps, ALU.add).then_inc(deg_read, 1)
                dve.wait_ge(deg_read, b + 1)
                dve.wait_ge(h0_ready, b + 1)
                ch.link(dve.tensor_scalar(deg, deg, 1.0 / MAT_SCALE, DEG_EPS, ALU.mult, ALU.max))
                rsqrt(ch, dve, dinv, deg, tn)
                ch.do(dve.tensor_scalar(dscale, dinv, wsc[:, 0:1], UNSCALE, ALU.mult, ALU.mult))
                dve.tensor_tensor(tmp[:, :, 0:C], h, dinv.unsqueeze(2).to_broadcast([P, NB, C]),
                                  ALU.mult).then_inc(dh_done, 1)
                dve.wait_ge(v0_hi, b + 1)
                dve.scalar_tensor_tensor(out=vec[:, :, C:2 * C], in0=tmp[:, :, 0:C], scalar=VEC_SCALE,
                                         in1=vec[:, :, 0:C], op0=ALU.mult, op1=ALU.subtract).then_inc(v0_done, 1)
                assert ch.n == DEG_STEPS, ch.n

            k_batch(0, None)
            with dve.Fori(1, B) as b:
                k_batch(b, b - 1)

            def a_lo(b, c, wide):
                i, k = c // NQ, c % NQ
                dve.wait_ge(ahi_done, b * TCH + (c + 1))
                dve.scalar_tensor_tensor(out=mat[:, CB * k:CB * k + CB, i, 1, :],
                                         in0=t_bank(c, wide).rearrange("p (j c) -> p j c", c=P), scalar=MAT_SCALE,
                                         in1=mat[:, CB * k:CB * k + CB, i, 0, :], op0=ALU.mult,
                                         op1=ALU.subtract).then_inc(alo_done, 1)

            for c in range(TCH):
                if c % (NQ * CB) == NQ * (CB - 1):
                    y_post(B - 1, c // (NQ * CB))
                a_lo(0, c, False)

            def wide(v, q=None):
                if q is None:
                    return v.unsqueeze(2).to_broadcast([P, NB, C])
                return v[:, CB * q:CB * q + CB].unsqueeze(2).to_broadcast([P, CB, C])

            def low_part(b, layer, half):
                src = h_att if layer == 1 else h
                s = slice(8 * half, 8 * half + 8)
                dve.wait_ge(hs_hi, (b * 2 + (layer - 1)) * 2 + (half + 1))
                dve.tensor_tensor(hs[:, s, C:2 * C], src[:, s, :], hs[:, s, 0:C], ALU.subtract).then_inc(hs_lo, 1)

            def prepare(b, half):
                if half == 0:
                    dve.wait_ge(x1_in, b * 16 + 16)
                ch = Chain(dve, p_step, b * (2 * LN_STEPS) + half * LN_STEPS)
                layer_norm(ch, xt, h_att, hatt_ready, (8 * half, 8 * half + 8))
                assert ch.n == LN_STEPS

            def layer1(b, ch):
                s1, s2 = s12_ps[:, :, 0], s12_ps[:, :, 1]
                dve.wait_ge(wh_mm, b + 1)
                dve.tensor_reduce(small[:, 0:1], s2, AX, ALU.max).then_inc(mx_in, 1)
                dve.wait_ge(mx_t, b + 1)
                dve.tensor_reduce(small[0:1, 1:2], mx_ps[0:1, 0:P], AX, ALU.max).then_inc(mx_r, 1)
                dve.wait_ge(mx_b, b + 1)
                ch.link(dve.tensor_copy(small[:, 2:3], mx_ps[:, P:P + 1]))
                top = small[:, 2:3]
                ch.link(dve.tensor_scalar(var, s1, top, None, ALU.add))
                ch.link(dve.scalar_tensor_tensor(out=tn, in0=var, scalar=0.2, in1=var, op0=ALU.mult, op1=ALU.max))
                ch.do(dve.tensor_tensor(coef[:, 0, :], var, tn, ALU.subtract))
                ch.do(dve.scalar_tensor_tensor(out=coef[:, 1, :], in0=var, scalar=0.2, in1=tn, op0=ALU.mult,
                                               op1=ALU.subtract))
                ch.do(dve.tensor_scalar(coef[:, 2, :], s2, top, None, ALU.subtract))
                ch.do(dve.tensor_scalar(s2st[:, :], s2, STEEP / W_SCALE, None, ALU.mult))
                ch.settle(1)
                dve.tensor_scalar(coef[:, 3, :], coef[:, 2, :], 0.2, None, ALU.mult).then_inc(coef_in, 1)
                dve.wait_ge(coef_done, b + 1)
                ch.link(dve.tensor_scalar(coef[:, 2:4, :], coef[:, 2:4, :], ATT_SCALE / W_SCALE, None, ALU.mult))
                for half in range(2):
                    s = slice(8 * half, 8 * half + 8)
                    for t in range(2):
                        w, part = coef[:, 2 + t, s], tmp[:, 8 * t:8 * t + 8, :]
                        if half == 1:
                            dve.wait_ge(b_ready, b * 2 + 1)
                        ins = dve.tensor_tensor(part[:, :, 0:C], wh_ps[:, s, :],
                                                w.unsqueeze(2).to_broadcast([P, 8, C]), ALU.mult)
                        if half == 1 and t == 1:
                            ins.then_inc(wh_read, 1)
                        dve.tensor_scalar(part[:, :, C:D], w.unsqueeze(2), W_SCALE, None, ALU.mult).then_inc(bw_ready, 1)
                    for t in range(2):
                        v = (vec, vec_d)[t]
                        dve.wait_ge(bw_hi, b * 4 + (2 * half + t + 1))
                        ins = dve.tensor_tensor(v[:, s, D:2 * D], tmp[:, 8 * t:8 * t + 8, :], v[:, s, 0:D], ALU.subtract)
                    ins.then_inc(b_ready, 1)
                dve.wait_ge(s1_cp, b * NQ + NQ)

                def neighbours(g):
                    q, j = g // NB, g % NB
                    if g >= RING:
                        dve.wait_ge(g_used, b * TCH + (g - RING + 1))
                    dve.tensor_scalar(neg_b[:, g % RING, :].rearrange("p (i c) -> p i c", c=P),
                                      mat[:, j, CB * q:CB * q + CB, 0, :], 0.0, None, ALU.is_gt).then_inc(nb_done, 1)

                def positive(g):
                    dve.wait_ge(nb_done, b * TCH + (g + 1))
                    dve.wait_ge(pos_done, b * TCH + (g + 1))
                    dve.tensor_tensor(pos_b[:, g % RING, :], neg_b[:, g % RING, :], pos_b[:, g % RING, :],
                                      ALU.mult).then_inc(g1_done, 1)

                def negative(g):
                    if g % 3 == 2:
                        dve.wait_ge(g1_done, b * TCH + (g + 1))
                        dve.tensor_tensor(neg_b[:, g % RING, :], neg_b[:, g % RING, :], pos_b[:, g % RING, :],
                                          ALU.subtract).then_inc(g2_dve, 1)

                def post(q):
                    a = acc[q % 2]
                    dve.wait_ge(acc_done, b * (3 * NQ) + (q + 1))
                    for bank in range(3):
                        k = min(3, 2 * CB - 3 * bank)
                        ins = dve.tensor_reduce(nsum[:, 3 * bank:3 * bank + k, :],
                                                a[:, bank, 0:k * 2 * D].rearrange("p (i s c) -> p i c s", s=2, c=D),
                                                AX, ALU.add)
                    ins.then_inc(acc_read, 1)
                    dve.wait_ge(acc_read, b * (3 * NQ) + (q + 1))
                    for t in range(2):
                        ch.do(dve.tensor_tensor(nwt[:, CB * t:CB * t + CB, :], nsum[:, CB * t:CB * t + CB, :],
                                                coef[:, t, CB * q:CB * q + CB].unsqueeze(2).to_broadcast([P, CB, D]),
                                                ALU.mult))
                    ch.settle()
                    ch.link(dve.tensor_tensor(nsum[:, 0:CB, :], nwt[:, 0:CB, :], nwt[:, CB:2 * CB, :], ALU.add))
                    den = tn[:, 0:CB]
                    ch.link(dve.reciprocal(den.unsqueeze(2), nsum[:, 0:CB, C:D]))
                    ch.link(dve.tensor_tensor(yq[:, :, :], nsum[:, 0:CB, 0:C],
                                              den.unsqueeze(2).to_broadcast([P, CB, C]), ALU.mult))
                    dve.tensor_scalar(t_elu, yq[:, :, :], 0.0, None, ALU.min).then_inc(elu_in, 1)
                    return q

                def post_end(q):
                    dve.wait_ge(elu_exp, b * NQ + (q + 1))
                    ch.link(dve.scalar_tensor_tensor(out=yq[:, :, :], in0=yq[:, :, :], scalar=0.0, in1=t_elu,
                                                     op0=ALU.max, op1=ALU.add))
                    x_q = xt[:, CB * q:CB * q + CB, :]
                    ch.link(dve.scalar_tensor_tensor(out=x_q, in0=yq[:, :, :], scalar=-1.0, in1=x_q,
                                                     op0=ALU.add, op1=ALU.add))

                for g in range(TCH + 2):
                    if g < TCH:
                        neighbours(g)
                    if 1 <= g <= TCH:
                        positive(g - 1)
                    if g >= 2:
                        negative(g - 2)
                    if NB <= g < TCH and g % NB == 4:
                        post(g // NB - 1)
                    if NB <= g < TCH and g % NB == 8:
                        post_end(g // NB - 1)
                post(NQ - 1)
                post_end(NQ - 1)

            def layer2(b, ch):
                for half in range(2):
                    centred(ch, xt, h, (8 * half, 8 * half + 8))
                rsqrt(ch, dve, rstd, var, tn)
                for half in range(2):
                    scaled(h, h_ready, (8 * half, 8 * half + 8))
                for half in range(2):
                    low_part(b, 2, half)
                ch.do(dve.memset(vec[:, :, C:D], VEC_SCALE))
                ch.do(dve.memset(vec[:, :, 2 * D - 1:2 * D], 0.0))
                for half in range(2):
                    s = slice(8 * half, 8 * half + 8)
                    dve.wait_ge(m_mm, b * 2 + (half + 1))
                    dve.tensor_tensor(tmp[:, s, 0:C], m_ps[:, s, :], b2s[:, :].unsqueeze(1).to_broadcast([P, 8, C]),
                                      ALU.add).then_inc(m_sum, 1)
                for half in range(2):
                    s = slice(8 * half, 8 * half + 8)
                    dve.wait_ge(v_hi, b * 4 + (half + 1))
                    ch.link(dve.tensor_scalar(tmp[:, s, 0:C], tmp[:, s, 0:C], 0.0, VEC_SCALE, ALU.max, ALU.mult))
                    dve.tensor_tensor(vec[:, s, D:D + C], tmp[:, s, 0:C], vec[:, s, 0:C],
                                      ALU.subtract).then_inc(v_ready, 1)

                def message(q):
                    dve.wait_ge(acc_done, b * (3 * NQ) + NQ + (q + 1))
                    if q >= 1:
                        dve.wait_ge(msg_done, b * NQ + q)
                    for k in range(2):
                        ins = dve.tensor_reduce(msum[:, 2 * k:2 * k + 2, :],
                                                acc[q % 2][:, k, 0:4 * D].rearrange("p (i s c) -> p i c s", s=2, c=D),
                                                AX, ALU.add)
                    ins.then_inc(acc_read, 1)
                    dve.wait_ge(acc_read, b * (3 * NQ) + NQ + (q + 1))
                    dve.tensor_scalar(deg[:, CB * q:CB * q + CB].unsqueeze(2), msum[:, :, C:D], UNSCALE, None,
                                      ALU.mult).then_inc(msg_in, 1)

                def gru(q):
                    dve.wait_ge(rz_done, b * NQ + (q + 1))
                    for k in range(2):
                        s = slice(2 * k, 2 * k + 2)
                        ch.do(dve.scalar_tensor_tensor(out=t_w[:, s, :], in0=t_rz[:, s, 0:C], scalar=1.0,
                                                       in1=gate_ps[k][:, :, 3 * C:4 * C], op0=ALU.add, op1=ALU.mult))
                    ch.settle()
                    for k in range(2):
                        s = slice(2 * k, 2 * k + 2)
                        ins = dve.scalar_tensor_tensor(out=t_pre[:, s, :], in0=t_w[:, s, :], scalar=0.5,
                                                       in1=gate_ps[k][:, :, 2 * C:3 * C], op0=ALU.mult, op1=ALU.add)
                    ins.then_inc(pre_done, 1)

                def gru_end(q):
                    hq, xq = h[:, CB * q:CB * q + CB, :], xt[:, CB * q:CB * q + CB, :]
                    dve.wait_ge(n_done, b * NQ + (q + 1))
                    ch.link(dve.tensor_tensor(t_w, hq, t_n, ALU.subtract))
                    ch.link(dve.scalar_tensor_tensor(out=t_w, in0=t_rz[:, :, C:2 * C], scalar=1.0, in1=t_w,
                                                     op0=ALU.add, op1=ALU.mult))
                    ch.link(dve.scalar_tensor_tensor(out=t_w, in0=t_w, scalar=0.5, in1=t_n, op0=ALU.mult, op1=ALU.add))
                    dve.tensor_tensor(xq, xq, t_w, ALU.add).then_inc(gru_done, 1)

                for q in range(NQ):
                    if q >= 1:
                        gru(q - 1)
                    message(q)
                    if q >= 1:
                        gru_end(q - 1)
                    if q == 2:
                        dve.wait_ge(gru_done, b * NQ + 2)
                        layer_norm(ch, xt, h, x3_ready, (0, 8))
                rsqrt(ch, dve, dinv, deg, tn)
                gru(NQ - 1)
                gru_end(NQ - 1)
                dve.wait_ge(gru_done, b * NQ + NQ)

            def layer3(b, ch, follow):
                dve.wait_ge(x3_ready, b * 2 + 1)

                def values(half):
                    s = slice(8 * half, 8 * half + 8)
                    ch.do(dve.tensor_tensor(tmp[:, s, 0:C], h[:, s, :], dinv[:, s].unsqueeze(2).to_broadcast([P, 8, C]),
                                            ALU.mult))
                    dve.tensor_copy(tmp[:, s, C:D], dinv[:, s].unsqueeze(2)).then_inc(m3_in, 1)

                def values_low(half):
                    s = slice(8 * half, 8 * half + 8)
                    dve.wait_ge(v_hi, b * 4 + 2 + (half + 1))
                    dve.scalar_tensor_tensor(out=vec[:, s, D:2 * D], in0=tmp[:, s, :], scalar=VEC_SCALE,
                                             in1=vec[:, s, 0:D], op0=ALU.mult, op1=ALU.subtract).then_inc(v_ready, 1)

                values(0)
                layer_norm(ch, xt, h, x3_ready, (8, NB))
                dve.wait_ge(x3_ready, b * 2 + 2)
                values(1)
                values_low(0)
                ch.link(dve.tensor_tensor(sqd, deg, dinv, ALU.mult))
                ch.link(dve.tensor_scalar(sqd, sqd, -UNSCALE, None, ALU.mult))
                values_low(1)
                dve.wait_ge(v_ready, b * 4 + 4)
                ch.link(dve.tensor_tensor(tmp[:, :, 0:C], h, h, ALU.mult))
                ch.do(dve.tensor_reduce(bn_part[:, 0, :], h.rearrange("p i c -> p c i"), AX, ALU.add))
                ch.link(dve.tensor_reduce(bn_part[:, 1, :], tmp[:, :, 0:C].rearrange("p i c -> p c i"), AX, ALU.add))
                ch.link(dve.tensor_tensor(bn_sum[:, :, :], bn_sum[:, :, :], bn_part[:, :, :], ALU.add))

                def post(q):
                    ch.settle()
                    dve.wait_ge(acc_done, b * (3 * NQ) + 2 * NQ + (q + 1))
                    for k in range(2):
                        ins = dve.tensor_reduce(msum[:, 2 * k:2 * k + 2, :],
                                                acc[q % 2][:, k, 0:4 * D].rearrange("p (i s c) -> p i c s", s=2, c=D),
                                                AX, ALU.add)
                    ins.then_inc(acc_read, 1)
                    dve.wait_ge(acc_read, b * (3 * NQ) + 2 * NQ + (q + 1))
                    ch.link(dve.tensor_tensor(msum, msum, sqd[:, CB * q:CB * q + CB].unsqueeze(2)
                                              .to_broadcast([P, CB, D]), ALU.mult))
                    ins = dve.tensor_tensor(vout[:, CB * q:CB * q + CB, :], msum, h1[:, CB * q:CB * q + CB, :], ALU.add)
                    if q == NQ - 1:
                        ins.then_inc(v3_done, 1)
                    else:
                        ch.do(ins)

                if follow:
                    for c in range(TCH):
                        a_lo(b + 1, c, True)
                        if c in PREP_AT:
                            prepare(b + 1, PREP_AT.index(c))
                            low_part(b + 1, 1, PREP_AT.index(c))
                        if c % (NQ * CB) == NQ * (CB - 1) + 1:
                            post(c // (NQ * CB))
                else:
                    for q in range(NQ):
                        post(q)

            def layers(b, follow):
                ch = Chain(dve, v_step, b * V_STEPS)
                layer1(b, ch)
                layer2(b, ch)
                layer3(b, ch, follow)
                assert ch.n == V_STEPS, ch.n

            for half in range(2):
                prepare(0, half)
                low_part(0, 1, half)
            with dve.Fori(0, B - 1) as b:
                layers(b, True)
            layers(B - 1, False)

            ch = Chain(dve, f_step, 0)
            ch.link(dve.tensor_copy(small[:, 3:4], bn_sum[:, 0, 0:1]))
            assert ch.n == F_SUMS
            dve.wait_ge(f_mm, 1)
            mu, ex2, vr, rs, t1, sc, sh = (bnv[:, i:i + 1] for i in range(7))
            ch.link(dve.tensor_scalar(bnv[:, 0:2], tp[0:C, 0, 0:2], 1.0 / (B * N), None, ALU.mult))
            ch.link(dve.tensor_tensor(vr, mu, mu, ALU.mult))
            ch.link(dve.tensor_tensor(vr, ex2, vr, ALU.subtract))
            ch.link(dve.tensor_scalar(vr, vr, BN_EPS, None, ALU.add))
            rsqrt(ch, dve, rs, vr, t1)
            ch.link(dve.tensor_tensor(sc, gb[:, 0:1], rs, ALU.mult))
            ch.link(dve.tensor_tensor(t1, mu, sc, ALU.mult))
            ch.link(dve.tensor_tensor(sh, gb[:, 1:2], t1, ALU.subtract))
            ch.do(dve.tensor_scalar(fold[:, 0:C], ident[0:C, 0:C], sc, None, ALU.mult))
            ch.link(dve.tensor_copy(fold[:, C:D], sh))
            assert ch.n == F_FOLD, ch.n
            dve.wait_ge(f_mm, 2)
            ch.link(dve.tensor_copy(wfin, tp[0:D, 1, 0:C]))
            assert ch.n == F_ALL, ch.n
            with dve.Fori(0, B // 2) as t:
                for s in range(2):
                    dve.wait_ge(fin_in[s], t * 32 + 32)
                    for q in range(NQ):
                        c = s * NQ + q
                        dve.wait_ge(f_relu, t * (2 * NQ) + (c + 1))
                        dve.scalar_tensor_tensor(out=fin_y[c % 2], in0=acc[c % 2][:, 0, 0:CB * C], scalar=0.01,
                                                 in1=fin_r[c % 2], op0=ALU.mult, op1=ALU.add).then_inc(f_y, 1)
                        dve.wait_ge(f_y, t * (2 * NQ) + (c + 1))
                        xq = fin_x[s][:, CB * q:CB * q + CB, :]
                        dve.tensor_tensor(xq, xq, fin_y[c % 2].rearrange("p (i c) -> p i c", c=C), ALU.add) \
                            .then_inc(f_add, 1)


_INS = ['x', 'adj', 'L0_gnn_U', 'L0_gnn_w_scale', 'L1_gnn_W', 'L1_gnn_a', 'L2_gnn_W1', 'L2_gnn_b1', 'L2_gnn_W2',
        'L2_gnn_b2', 'L2_gnn_W_ih', 'L2_gnn_b_ih', 'L2_gnn_W_hh', 'L2_gnn_b_hh', 'L3_gnn_gamma', 'L3_gnn_beta',
        'L3_gnn_W', 'L3_gnn_b']


def kernel(**inputs):
    import numpy as _np
    import concourse.bacc as _bacc
    from concourse import mybir as _mybir
    from concourse.bass_utils import run_bass_kernel_spmd as _run

    nc = _bacc.Bacc("TRN2", target_bir_lowering=False, num_devices=1)
    arrays, args = {}, []
    for name in _INS:
        a = _np.ascontiguousarray(inputs[name])
        arrays[f"in_{name}_dram"] = a
        args.append(nc.dram_tensor(f"in_{name}_dram", a.shape, _mybir.dt.from_np(a.dtype), kind="ExternalInput").ap())
    b, n, c = inputs["x"].shape
    out = nc.dram_tensor("out_0_dram", (b, n, c), _mybir.dt.float32, kind="ExternalOutput").ap()
    xs = nc.dram_tensor("x_scratch", (b, P, n // P, c), _mybir.dt.float32, kind="Internal").ap()
    vs = nc.dram_tensor("v_scratch", (b, P, n // P, c + 1), _mybir.dt.float32, kind="Internal").ap()
    gnn_kernel(nc, *args, out, xs, vs)
    r = _run(nc, [arrays], core_ids=[0])
    return r.results[0]["out_0_dram"]
```

```python
from contextlib import ExitStack

import concourse.bass as bass
from concourse import mybir

ALU = mybir.AluOpType
ACT = mybir.ActivationFunctionType
AX = mybir.AxisListType.X
F32 = mybir.dt.float32
F16 = mybir.dt.float16
BF16 = mybir.dt.bfloat16
I32 = mybir.dt.int32

P = 128
CB = 4
MAT_SCALE = 1024.0
VEC_SCALE = 64.0
UNSCALE = 1.0 / (MAT_SCALE * VEC_SCALE)
ATT_SCALE = 1024.0
RING = 5
WARM = (64, 44, 16, 12)
FIN = 4
LEAD = 1
LATE = 3
STEEP = float(2 ** 40)
LN_EPS = 1e-5
BN_EPS = 1e-5
DEG_EPS = 1e-12
RSQRT_STEPS = 11
LN_STEPS = 6 + RSQRT_STEPS
U_SCALE = 16.0
W_SCALE = 256.0


class Chain:

    def __init__(self, eng, sem, base):
        self.eng, self.sem, self.base, self.n = eng, sem, base, 0

    def do(self, ins):
        ins.then_inc(self.sem, 1)
        self.n += 1

    def settle(self, back=0):
        self.eng.wait_ge(self.sem, self.base + (self.n - back))

    def link(self, ins):
        self.do(ins)
        self.settle()


def rsqrt(ch, eng, y, x, t):
    yi = y.bitcast(I32)
    ch.link(eng.tensor_scalar(t.bitcast(I32), x.bitcast(I32), 1, None, ALU.logical_shift_right))
    ch.link(eng.tensor_scalar(yi, t.bitcast(I32), -1.0, 1597463007.0, ALU.mult, ALU.add))
    for _ in range(3):
        ch.link(eng.scalar_tensor_tensor(out=t, in0=y, scalar=-0.5, in1=y, op0=ALU.mult, op1=ALU.mult))
        ch.link(eng.tensor_tensor(t, t, x, ALU.mult))
        ch.link(eng.scalar_tensor_tensor(out=y, in0=t, scalar=1.5, in1=y, op0=ALU.add, op1=ALU.mult))


def gnn_kernel(nc, x, adj, U, w_scale, L1W, L1a, W1, b1, W2, b2, W_ih, b_ih, W_hh, b_hh,
               gamma, beta, L3W, L3b, out, xs, vs):
    B, N, C = x.shape
    R = U.shape[1]
    NB = N // P
    NQ = NB // CB
    D = C + 1
    UK = 3 * R
    chunks = [(n, k) for n in range(NB) for k in range(n // CB + 1)]
    NCH = len(chunks)
    first_chunk = [chunks.index((n, 0)) for n in range(NB)]
    off_diag = [min(CB, n - CB * k) for n, k in chunks]
    up_index = [sum(1 for c in off_diag[:i] if c > 0) for i in range(NCH)]
    NUP = sum(1 for c in off_diag if c > 0)
    UPS = ((NUP + 1) // 2, NUP // 2)
    TCH = NB * NQ

    xv = x.rearrange("b (i p) c -> b p i c", p=P)
    outv = out.rearrange("b (i p) c -> b p i c", p=P)
    adj_rows = adj.rearrange("b (i p) m -> b i p m", p=P)
    adj_cols = adj.rearrange("b (i p) m -> b p i m", p=P)

    ctx = ExitStack()
    with ctx:
        def sb(name, shape, dt):
            return ctx.enter_context(nc.sbuf_tensor(name, shape, dt))

        def sem(name):
            return ctx.enter_context(nc.semaphore(name))

        mat = sb("mat", [P, NB, NB, 2, P], F16)
        rows = sb("rows", [P, 2, N], F32)
        cols = sb("cols", [P, 2, NB, P], F32)
        s1row = cols[:, 0, :, :].rearrange("p i c -> p (i c)")
        m1T = s1row
        h_att = s1row[:, 0:NB * C].rearrange("p (i c) -> p i c", c=C)
        h_sq = s1row[:, NB * C:2 * NB * C].rearrange("p (i c) -> p i c", c=C)
        c16 = cols[:, 1, :, :].rearrange("p i c -> p (i c)").bitcast(F16)
        hs = c16[:, 0:NB * P].rearrange("p (i c) -> p i c", c=P)
        hT = c16[:, NB * P:2 * NB * P]
        u_nat = cols[:, 0, :, :].rearrange("p i c -> p (i c)").bitcast(F16)[:, 0:2 * NB * UK] \
            .rearrange("p (o i c) -> p o i c", o=2, i=NB)
        cat = sb("cat", [P, NB, 2 * C + 1], F32)
        h = cat[:, :, C:2 * C]
        h1 = cat[:, :, C:2 * C + 1]
        xt = sb("xt", [P, NB, C], F32)
        vec = sb("vec", [P, NB, 2 * D], F16)
        vec_d = sb("vec_d", [P, NB, 2 * D], F16)
        u_st = vec_d[:, :, :].rearrange("p i c -> p (i c)")[0:UK, 0:N]
        vout = vec_d[:, :, :].bitcast(F32)
        tmp = sb("tmp", [P, NB, D], F32)
        scr = sb("scr", [P, 6 * 512], F32)
        a_sum_b = scr[:, 0:1024].rearrange("p (s n) -> p s n", s=2)
        s_sig_b = scr[:, 1024:2048].rearrange("p (s n) -> p s n", s=2)
        k_f32_b = scr[:, 2048:3072].rearrange("p (s n) -> p s n", s=2)
        half = scr[:, :].bitcast(F16).rearrange("p (s n) -> p s n", n=512)
        pos_b, neg_b = half[:, 0:RING, :], half[:, RING:2 * RING, :]
        large_b = scr[:, :].bitcast(BF16).rearrange("p (s n) -> p s n", n=512)[:, 0:RING, :]
        t_rz = scr[:, 0:512].rearrange("p (i c) -> p i c", i=CB)
        t_pre = scr[:, 512:768].rearrange("p (i c) -> p i c", i=CB)
        t_n = scr[:, 768:1024].rearrange("p (i c) -> p i c", i=CB)
        t_w = scr[:, 1024:1280].rearrange("p (i c) -> p i c", i=CB)
        msum = scr[:, 1280:1280 + CB * D].rearrange("p (i c) -> p i c", i=CB)
        catT = scr[:, 1600:1600 + CB * P]
        yred = sb("yred", [P, 2, 8 * D], F32)
        u_mv = yred[:, :, :].rearrange("p a c -> p (a c)").bitcast(F16)[0:UK, 0:N]
        nsum = yred[:, 0, :].rearrange("p (s c) -> p s c", c=D)
        nwt = yred[:, 1, :].rearrange("p (s c) -> p s c", c=D)
        yq = sb("yq", [P, CB, C], F32)
        rsum = sb("rsum", [P, NB, NQ], F32)
        st = sb("st", [P, 8, NB], F32)
        mean, var, deg, rstd, dinv, tn, dscale, sqd = (st[:, i, :] for i in range(8))
        var_deg, roots, root_tmp = (st[:, i:i + 2, :].rearrange("p t i -> p (t i)") for i in (1, 3, 5))
        coef = sb("coef", [P, 4, NB], F32)
        s2st = sb("s2st", [P, NB], F32)
        small = sb("small", [P, 4], F32)
        wsc = sb("wsc", [P, 1], F32)
        ident = sb("ident", [P, P], F32)
        ident16 = sb("ident16", [P, P], F16)
        zeros16 = sb("zeros16", [P, P], F16)
        ones16 = sb("ones16", [P, P], F16)
        onesf = sb("onesf", [P, P], F32)
        wa_hi = sb("wa_hi", [P, C + 2], F16)
        wa_lo = sb("wa_lo", [P, C + 2], F16)
        wa1_hi = sb("wa1_hi", [P, P], F16)
        wa1_lo = sb("wa1_lo", [P, P], F16)
        w1_hi = sb("w1_hi", [P, C], F16)
        w1_lo = sb("w1_lo", [P, C], F16)
        w2s = sb("w2s", [C, C], F32)
        b1s = sb("b1s", [C, 1], F32)
        b2s = sb("b2s", [P, C], F32)
        wcat = sb("wcat", [P, 4 * C], F32)
        bias2 = sb("bias2", [C, 4 * C], F16)
        bn_sum = sb("bn_sum", [P, 2, C], F32)
        bn_part = yred[:, 1, 0:2 * C].rearrange("p (t c) -> p t c", t=2)
        bnv = sb("bnv", [C, 8], F32)
        gb = sb("gb", [C, 2], F32)
        w3s = yred[0:C, 1, 2 * C:3 * C]
        wfin = yred[0:D, 1, 3 * C:4 * C]
        b3row = yred[0:1, 1, 4 * C:5 * C]
        e_last = yred[0:1, 0, 2 * C:2 * C + D]
        a12 = scr[0:C, 0:2]
        g_rz = scr[:, 128:256]
        g_n = scr[:, 256:384]
        bih = scr[0:C, 384:384 + 3 * C]
        bhh = scr[0:C, 576:576 + 3 * C]
        bsum = scr[0:C, 768:1024]
        bhi = scr[0:C, 1024:1152].bitcast(F16)
        blo = scr[0:C, 1152:1280].bitcast(F16)
        waT = scr[0:C, 1280:1280 + P]
        wa = scr[:, 1408:1408 + C + 2]
        wa_s = scr[:, 1480:1480 + C + 2]
        w1s = scr[:, 1552:1552 + C]
        fold = yred[0:C, 0, 0:D]
        fmat = mat[:, :, :, :, :].rearrange("p j i s c -> p (j i s c)").bitcast(F32)
        fin_v = [fmat[:, t * NB * D:(t + 1) * NB * D].rearrange("p (i c) -> p i c", c=D) for t in range(FIN)]
        fin_x = [fmat[:, FIN * NB * D + t * NB * C:FIN * NB * D + (t + 1) * NB * C]
                 .rearrange("p (i c) -> p i c", c=C) for t in range(FIN)]
        fin_vt = [scr[:, 0:512], scr[:, 512:1024]]
        fin_r = [scr[:, 1024:1280], scr[:, 1280:1536]]
        fin_y = [scr[:, 1536:1792], scr[:, 1792:2048]]
        t_elu = scr[:, 2816:2816 + CB * C].rearrange("p (i c) -> p i c", c=C)

        tp = ctx.enter_context(nc.psum_tensor("tp", [P, 2, 512], F32))
        acc = [ctx.enter_context(nc.psum_tensor(f"acc{i}", [P, 3, 512], F32)) for i in range(2)]

        def t_bank(c, wide):
            return (tp[:, 0, :], tp[:, 1, :], acc[0][:, 2, :], acc[1][:, 2, :])[c % (4 if wide else 2)]

        s_ps = acc[0][:, 0:2, :]
        y_ps = acc[0][:, 2, :]
        deg_ps = acc[1][:, 2, 0:NB]
        k_ps = [acc[1][:, i, :].bitcast(F16) for i in range(2)]
        wh_ps = acc[0][:, 0:2, :].rearrange("p a (i c) -> p (a i) c", c=C)
        mx_ps = acc[0][:, 2, 128:257]
        s1_ps = [tp[:, 0, :], tp[:, 1, :], acc[1][:, 2, :], tp[:, 0, :]]
        hT_ps = [[acc[0][:, i, :].bitcast(F16) for i in range(2)], [acc[i][:, 2, :].bitcast(F16) for i in range(2)]]
        s12_ps = acc[0][:, 2, 0:2 * NB].rearrange("p (i t) -> p i t", t=2)
        m_ps = acc[1][:, 1:3, :].rearrange("p a (i c) -> p (a i) c", c=C)
        gate_ps = [acc[i][:, 2, :].rearrange("p (i c) -> p i c", c=4 * C) for i in range(2)]

        w_in, set_pe, set_dve, set_pool = (sem(n) for n in ("w_in", "set_pe", "set_dve", "set_pool"))
        row_in = [sem(f"row_in{i}") for i in range(2)]
        col_in = [sem(f"col_in{i}") for i in range(2)]
        arow_in = [sem(f"arow_in{i}") for i in range(2)]
        x0_in, xr_in, x1_out, x1_in = (sem(n) for n in ("x0_in", "xr_in", "x1_out", "x1_in"))
        x3_out, v3_out = sem("x3_out"), sem("v3_out")
        w3_in, e_set = sem("w3_in"), sem("e_set")
        fin_in = [sem(f"fin_in{i}") for i in range(FIN)]
        fin_out = [sem(f"fin_out{i}") for i in range(FIN)]
        at_done, slog_done, sig_done, asum_done, kf_done, khi_done, klo_done, kup_t = (
            sem(n) for n in ("at_done", "slog_done", "sig_done", "asum_done", "kf_done", "khi_done",
                             "klo_done", "kup_t"))
        kup_done = [sem(f"kup_done{i}") for i in range(2)]
        deg_done, deg_read, dh_done, v0_hi, v0_done, y_done, y_read, x1_done = (
            sem(n) for n in ("deg_done", "deg_read", "dh_done", "v0_hi", "v0_done", "y_done", "y_read", "x1_done"))
        ln0_step, h0_ready, deg_step, y_step, v_step, f_step = (
            sem(n) for n in ("ln0_step", "h0_ready", "deg_step", "y_step", "v_step", "f_step"))
        a2t_done, ahi_done, alo_done = (sem(n) for n in ("a2t_done", "ahi_done", "alo_done"))
        h_ready, ht_t, ht_cp, wh_mm, s1_mm, s1_cp, mx_in, mx_t, mx_r, mx_b = (sem(n) for n in (
            "h_ready", "ht_t", "ht_cp", "wh_mm", "s1_mm", "s1_cp", "mx_in", "mx_t", "mx_r", "mx_b"))
        nb_done, wh_read, hatt_ready, hs_hi, hs_lo, p_step = (sem(n) for n in (
            "nb_done", "wh_read", "hatt_ready", "hs_hi", "hs_lo", "p_step"))
        sq_done, v3_step = sem("sq_done"), sem("v3_step")
        coef_in, coef_done, bw_ready, bw_hi, b_ready, g1_done, g2_pool, g2_dve, pos_done, g_used = (sem(n) for n in (
            "coef_in", "coef_done", "bw_ready", "bw_hi", "b_ready", "g1_done", "g2_pool", "g2_dve", "pos_done", "g_used"))
        acc_done, acc_read, elu_in, elu_exp, m1_mm, m1_cp, m_mm, m_sum, v_hi, v_ready = (sem(n) for n in (
            "acc_done", "acc_read", "elu_in", "elu_exp", "m1_mm", "m1_cp", "m_mm", "m_sum", "v_hi", "v_ready"))
        msg_in, msg_done, cat_t, cat_cp, gate_mm, rz_done, pre_done, n_done, gru_done = (sem(n) for n in (
            "msg_in", "msg_done", "cat_t", "cat_cp", "gate_mm", "rz_done", "pre_done", "n_done", "gru_done"))
        x3_ready, m3_in, v3_done = sem("x3_ready"), sem("m3_in"), sem("v3_done")
        f_mm, f_vt, f_vtcp, f_out, f_relu, f_y, f_add = (sem(n) for n in (
            "f_mm", "f_vt", "f_vtcp", "f_out", "f_relu", "f_y", "f_add"))

        def known(b, k):
            return isinstance(b, int) and b * NCH + k <= 0

        def pool_g2(g):
            return g - g // 2

        POOL_G2 = pool_g2(TCH)
        PREP_AT = (6, 12, 20, 28, 34)
        HT_AT = 12

        block = ctx.enter_context(nc.Block())

        W_DMAS = 19
        SET_POOL, SET_IDENT, SET_WAT, SET_WA, SET_DVE = 10, 1, 16, 27, 29
        DEG_STEPS, V_STEPS = 3 + RSQRT_STEPS, 124
        F_SUMS, F_FOLD, F_ALL = 1, 21, 22

        @block.sync
        def _(sp):
            sp.dma_start(tmp[:, :, 0:R], U.rearrange("(i p) r -> p i r", p=P)).then_inc(w_in, 16)
            sp.dma_start(wsc[:, :], w_scale.partition_broadcast(P)).then_inc(w_in, 16)
            for o in (0, C):
                sp.dma_start(wa[o:o + C, 0:C], L1W).then_inc(w_in, 16)
                sp.dma_start(w1s[o:o + C, :], W1).then_inc(w_in, 16)
            for t in range(2):
                sp.dma_start(a12[:, t:t + 1], L1a[C * t:C * t + C, :]).then_inc(w_in, 16)
            sp.dma_start(w2s[:, :], W2).then_inc(w_in, 16)
            sp.dma_start(b1s[:, :], b1.rearrange("(c o) -> c o", o=1)).then_inc(w_in, 16)
            sp.dma_start(b2s[:, :], b2.partition_broadcast(P)).then_inc(w_in, 16)
            sp.dma_start(g_rz[:, 0:C], W_ih[0:2 * C, :]).then_inc(w_in, 16)
            sp.dma_start(g_rz[:, C:2 * C], W_hh[0:2 * C, :]).then_inc(w_in, 16)
            sp.wait_ge(set_pool, 1)
            sp.dma_start(g_n[0:C, 0:C], W_ih[2 * C:3 * C, :]).then_inc(w_in, 16)
            sp.dma_start(g_n[C:2 * C, C:2 * C], W_hh[2 * C:3 * C, :]).then_inc(w_in, 16)
            sp.dma_start(bih, b_ih.partition_broadcast(C)).then_inc(w_in, 16)
            sp.dma_start(bhh, b_hh.partition_broadcast(C)).then_inc(w_in, 16)
            sp.dma_start(gb[:, 0:1], gamma.rearrange("(c o) -> c o", o=1)).then_inc(w_in, 16)
            sp.dma_start(gb[:, 1:2], beta.rearrange("(c o) -> c o", o=1)).then_inc(w_in, 16)

            def load_step(b, n, first):
                s = n % 2
                if not (first and n < 2):
                    back = first_chunk[n - 1] if n >= 2 else first_chunk[NB - 1] - NCH if n == 0 else 0
                    sp.wait_ge(asum_done, b * NCH + back)
                sp.dma_start(rows[:, s, 0:(n + 1) * P], adj_rows[b, n, :, 0:(n + 1) * P]).then_inc(row_in[s], 16)
                if n > 0:
                    if first and n == 1:
                        sp.wait_ge(set_dve, SET_DVE)
                    sp.dma_start(cols[:, s, 0:n, :], adj_cols[b, :, 0:n, n * P:(n + 1) * P]).then_inc(col_in[s], 16)

            def load_residual(b):
                sp.dma_start(xt[:, :, :], xv[b]).then_inc(xr_in, 16)

            def store_x1(b):
                sp.wait_ge(x1_done, b * NQ + NQ)
                sp.dma_start(xs[b], xt[:, :, :]).then_inc(x1_out, 16)
                sp.wait_ge(x1_out, b * 16 + 16)

            sp.dma_start(h, xv[0]).then_inc(x0_in, 16)
            for n in range(NB):
                load_step(0, n, True)
            load_residual(0)
            with sp.Fori(1, B) as b:
                for n in range(NB):
                    load_step(b, n, False)
                    if n == 1:
                        sp.wait_ge(v0_done, b)
                        sp.dma_start(h, xv[b]).then_inc(x0_in, 16)
                store_x1(b - 1)
                load_residual(b)

            def load_row(b, i, first):
                s = i % 2
                if first and i < 2:
                    sp.wait_ge(asum_done, B * NCH)
                else:
                    sp.wait_ge(a2t_done, b * TCH + NQ * (i - 1))
                sp.dma_start(rows[:, s, :], adj_rows[b, i]).then_inc(arow_in[s], 16)

            def store_x3(b):
                sp.wait_ge(gru_done, b * NQ + NQ)
                sp.dma_start(xs[b], xt[:, :, :]).then_inc(x3_out, 16)

            def store_v(b):
                sp.wait_ge(v3_done, b * NQ + NQ)
                sp.dma_start(vs[b], vout).then_inc(v3_out, 16)

            for i in range(NB):
                load_row(0, i, True)
            store_x1(B - 1)
            sp.dma_start(xt[:, :, :], xs[0]).then_inc(x1_in, 16)
            with sp.Fori(0, B - 1) as b:
                store_x3(b)
                load_row(b + 1, 0, False)
                load_row(b + 1, 1, False)
                sp.wait_ge(x3_out, b * 16 + 16)
                sp.wait_ge(x3_ready, b * 2 + 2)
                sp.dma_start(xt[:, :, :], xs[b + 1]).then_inc(x1_in, 16)
                for i in range(2, NB):
                    load_row(b + 1, i, False)
                store_v(b)
            store_x3(B - 1)
            sp.dma_start(w3s, L3W).then_inc(w3_in, 16)
            sp.dma_start(b3row, L3b.rearrange("(o c) -> o c", o=1)).then_inc(w3_in, 16)
            store_v(B - 1)
            sp.wait_ge(x3_out, B * 16)
            sp.wait_ge(v3_out, B * 16 + 16)

            def load_final(t, s):
                sp.dma_start(fin_v[s], vs[t * FIN + s]).then_inc(fin_in[s], 16)
                sp.dma_start(fin_x[s], xs[t * FIN + s]).then_inc(fin_in[s], 16)

            def store_final(t, s):
                sp.wait_ge(f_add, t * (FIN * NQ) + (s + 1) * NQ)
                sp.dma_start(outv[t * FIN + s], fin_x[s]).then_inc(fin_out[s], 16)

            for s in range(FIN):
                load_final(0, s)
            with sp.Fori(0, B // FIN - 1) as t:
                for s in range(FIN + 1):
                    if s < FIN:
                        store_final(t, s)
                    if s >= 1:
                        sp.wait_ge(fin_out[s - 1], t * 16 + 16)
                        load_final(t + 1, s - 1)
            for s in range(FIN):
                store_final(B // FIN - 1, s)
            for s in range(FIN):
                sp.wait_ge(fin_out[s], 16 * (B // FIN))

        USES = NB // 2

        def row_landed(eng, b, n):
            eng.wait_ge(row_in[n % 2], b * (16 * USES) + 16 * (n // 2 + 1))

        def col_landed(eng, b, n):
            uses, use = (USES - 1, n // 2) if n % 2 == 0 else (USES, n // 2 + 1)
            eng.wait_ge(col_in[n % 2], b * (16 * uses) + 16 * use)

        @block.tensor
        def _(pe):
            pe.wait_ge(set_pool, SET_POOL)
            pe.wait_ge(w_in, 16 * W_DMAS)
            pe.wait_ge(set_dve, SET_IDENT)
            pe.transpose(tp[0:C, 0, 0:P], wa[:, 0:C], ident[:, :])
            pe.transpose(tp[:, 0, P:2 * P], g_rz, ident[:, :])
            pe.transpose(tp[:, 0, 2 * P:3 * P], g_n, ident[:, :]).then_inc(set_pe, 1)
            pe.wait_ge(set_dve, SET_WAT)
            pe.matmul(tp[:, 1, 0:2], waT, a12, start=True, stop=True).then_inc(set_pe, 1)
            pe.wait_ge(set_dve, SET_WA)
            for o in range(2):
                for i in range(NB):
                    ins = pe.transpose(acc[o][0:UK, i // 8, :].bitcast(F16)[:, (i % 8) * P:(i % 8 + 1) * P],
                                       u_nat[:, o, i, :], ident16[:, :])
            ins.then_inc(set_pe, 1)
            pe.wait_ge(set_dve, SET_DVE)

            def k_step(b, n, late, beside=None):
                for k in range(n // CB + 1):
                    ck = first_chunk[n] + k
                    m0, m1 = CB * k, min(CB * k + CB, n + 1)
                    if k == 0:
                        row_landed(pe, b, n)
                        if n > 0:
                            col_landed(pe, b, n)
                    if not known(b, ck - 1):
                        pe.wait_ge(asum_done, b * NCH + (ck - 1))
                        pe.wait_ge(sig_done, b * NCH + (ck - 1))
                    for m in range(m0, m1):
                        src = cols[:, n % 2, m, :] if m < n else rows[:, n % 2, n * P:(n + 1) * P]
                        ins = pe.transpose(tp[:, ck % 2, (m - m0) * P:(m - m0 + 1) * P], src, ident[:, :])
                    ins.then_inc(at_done, 1)
                    pe.matmul(s_ps[:, ck % 2, 0:(m1 - m0) * P], u_st[:, n * P:(n + 1) * P],
                              u_mv[:, m0 * P:m1 * P], start=True, stop=True).then_inc(slog_done, 1)
                    if beside is not None:
                        beside(ck)
                    late.append(ck)
                    if len(late) > LATE:
                        upper(b, late.pop(0))

            def upper(b, ck):
                n, k = chunks[ck]
                off, u = off_diag[ck], up_index[ck]
                if off <= 0:
                    return
                pe.wait_ge(klo_done, b * NCH + (ck + 1))
                if u == 0:
                    if not known(b, 0):
                        pe.wait_ge(deg_read, b)
                    pe.matmul(deg_ps, zeros16[:, :], zeros16[:, 0:NB], start=True, stop=False,
                              skip_group_check=True)
                if not (isinstance(b, int) and b == 0 and u < 2):
                    pe.wait_ge(kup_done[u % 2], b * UPS[u % 2] + u // 2)
                for m in range(CB * k, CB * k + off):
                    for part in range(2):
                        pe.matmul(deg_ps[:, m:m + 1], mat[:, n, m, part, :], ones16[:, 0:1],
                                  start=False, stop=False, skip_group_check=True)
                        c = (m - CB * k) * 2 + part
                        ins = pe.transpose(k_ps[u % 2][:, c * P:(c + 1) * P], mat[:, n, m, part, :], ident16[:, :])
                ins.then_inc(kup_t, 1)

            def finish_k(b, late):
                while late:
                    upper(b, late.pop(0))
                pe.matmul(deg_ps, zeros16[:, :], zeros16[:, 0:NB], start=False, stop=True,
                          skip_group_check=True).then_inc(deg_done, 1)

            def y_block(b, i, part=None):
                if part is not None and part > 0:
                    pass
                elif i == 0:
                    pe.wait_ge(v0_done, b + 1)
                    for o in range(2):
                        pe.wait_ge(kup_done[o], b * UPS[o] + UPS[o])
                elif i % CB == 0:
                    pe.wait_ge(y_read, b * NQ + i // CB)
                o = (i % CB) * P
                for j in range(NB) if part is None else range(CB * part, CB * part + CB):
                    pe.matmul(y_ps[:, o:o + P], mat[:, j, i, 0, :], vec[:, j, 0:2 * C],
                              start=(j == 0), stop=False, skip_group_check=True)
                    ins = pe.matmul(y_ps[:, o:o + C], mat[:, j, i, 1, :], vec[:, j, 0:C],
                                    start=False, stop=(j == NB - 1), skip_group_check=True)
                if part in (None, NQ - 1):
                    ins.then_inc(y_done, 1)

            late = []
            for n in range(NB):
                k_step(0, n, late)
            finish_k(0, late)
            with pe.Fori(1, B) as b:
                def products(ck):
                    for i in range(NB):
                        if ck == min(first_chunk[i] + LEAD - 1, NCH - 1):
                            y_block(b - 1, i)

                for n in range(NB):
                    k_step(b, n, late, products)
                finish_k(b, late)

            def a_step(b, i, wide, beside=None):
                pe.wait_ge(arow_in[i % 2], b * (16 * USES) + 16 * (i // 2 + 1))
                for k in range(NQ):
                    c = i * NQ + k
                    ring = 4 if wide else 2
                    if c >= ring:
                        pe.wait_ge(alo_done, b * TCH + (c - ring + 1))
                    for j in range(CB):
                        ins = pe.transpose(t_bank(c, wide)[:, j * P:(j + 1) * P],
                                           rows[:, i % 2, (CB * k + j) * P:(CB * k + j + 1) * P], ident[:, :])
                    ins.then_inc(a2t_done, 1)
                    if beside is not None:
                        beside(k)

            y_block(B - 1, 0)
            for n in range(NB):
                a_step(0, n, False, (lambda k: y_block(B - 1, n + 1, k)) if n + 1 < NB else None)

            def vec_part(a, o, i, js):
                for j in js:
                    pe.matmul(a[:, o:o + 2 * D], mat[:, j, i, 0, :], vec[:, j, :],
                              start=(j == 0), stop=False, skip_group_check=True)
                    ins = pe.matmul(a[:, o:o + D], mat[:, j, i, 1, :], vec[:, j, 0:D],
                                    start=False, stop=(j == NB - 1), skip_group_check=True)
                return ins

            def h_transposed(b, layer):
                use = b * 2 + (layer - 1)
                for half in range(2):
                    pe.wait_ge(hs_lo, use * 2 + (half + 1))
                    for i in range(8):
                        ins = pe.transpose(hT_ps[layer - 1][half][:, i * P:(i + 1) * P], hs[:, 8 * half + i, :], ident16[:, :])
                    ins.then_inc(ht_t, 1)

            def stay_warm(bank, n):
                for _ in range(n):
                    pe.matmul(bank, zeros16[:, :], hT[:, 0:512], start=True, stop=True)

            def split_product(dst, hT_part, w_hi, w_lo, h_stationary):
                for part, w, rows_ in ((0, w_hi, P), (1, w_lo, C)):
                    a, v = (hT_part, w) if h_stationary else (w, hT_part)
                    ins = pe.matmul(dst, a[0:rows_], v[0:rows_], start=(part == 0), stop=(part == 1))
                return ins

            def layer1(b):
                pe.wait_ge(alo_done, b * TCH + TCH)
                pe.wait_ge(ht_cp, b * 4 + 2)
                for i in range(NB):
                    nodes = hT[:, i * P:(i + 1) * P]
                    split_product(wh_ps[:, i, :], nodes, wa_hi[:, 0:C], wa_lo[:, 0:C], True)
                    ins = split_product(s12_ps[:, i, :], nodes, wa_hi[:, C:C + 2], wa_lo[:, C:C + 2], True)
                ins.then_inc(wh_mm, 1)
                for c in range(NQ):
                    if c == 3:
                        pe.wait_ge(s1_cp, b * NQ + 1)
                    split_product(s1_ps[c], hT[:, c * 512:(c + 1) * 512], wa1_hi, wa1_lo, False).then_inc(s1_mm, 1)
                    if c == 0:
                        pe.wait_ge(mx_in, b + 1)
                        pe.transpose(mx_ps[0:1, 0:P], small[:, 0:1], ident[:, :]).then_inc(mx_t, 1)
                    if c == 2:
                        pe.wait_ge(mx_r, b + 1)
                        pe.matmul(mx_ps[:, P:P + 1], onesf[0:1, :], small[0:1, 1:2], start=True, stop=True) \
                            .then_inc(mx_b, 1)
                pe.wait_ge(s1_cp, b * NQ + NQ)
                stay_warm(tp[:, 0, :], WARM[2])
                pe.wait_ge(b_ready, b * 2 + 1)
                pe.wait_ge(wh_read, b + 1)
                for q in range(NQ):
                    a = acc[q % 2]
                    if q >= 2:
                        pe.wait_ge(acc_read, b * (3 * NQ) + (q - 1))
                    for bank in range(3):
                        pe.matmul(a[:, bank, 0:3 * 2 * D], zeros16[:, :],
                                  vec[:, 0:3, :].rearrange("p i c -> p (i c)"),
                                  start=True, stop=False, skip_group_check=True)
                    for j in range(NB):
                        g = q * NB + j
                        if g == NB // 2:
                            pe.wait_ge(b_ready, b * 2 + 2)
                        if g % 2 < 1:
                            pe.wait_ge(g2_pool, b * POOL_G2 + pool_g2(g + 1))
                        else:
                            pe.wait_ge(g2_dve, b * (TCH - POOL_G2) + (g + 1 - pool_g2(g + 1)))
                        for s in range(2 * CB):
                            m = (pos_b, neg_b)[s // CB][:, g % RING, (s % CB) * P:(s % CB + 1) * P]
                            ins = pe.matmul(a[:, s // 3, (s % 3) * 2 * D:(s % 3 + 1) * 2 * D], m,
                                            (vec, vec_d)[s // CB][:, j, :], start=False,
                                            stop=(j == NB - 1), skip_group_check=True)
                        ins.then_inc(g_used, 1)
                    pe.matmul(a[:, 2, 2 * 2 * D:3 * 2 * D], zeros16[:, :], vec[:, 0, :], start=False, stop=True,
                              skip_group_check=True).then_inc(acc_done, 1)

            def layer2(b):
                pe.wait_ge(acc_read, b * (3 * NQ) + (NQ - 1))
                stay_warm(acc[0][:, 0, :], WARM[0])
                h_transposed(b, 2)
                for c in range(NQ):
                    pe.wait_ge(ht_cp, b * 4 + 2 + (c // 2 + 1))
                    split_product(acc[0][0:C, c, :] if c < 2 else acc[1][0:C, 0, :] if c == 2 else tp[0:C, 0, :],
                                  hT[:, c * 512:(c + 1) * 512], w1_hi, w1_lo, False).then_inc(m1_mm, 1)
                for c in range(NQ):
                    pe.wait_ge(m1_cp, b * NQ + (c + 1))
                    for i in range(CB * c, CB * c + CB):
                        ins = pe.matmul(m_ps[:, i, :], m1T[0:C, i * P:(i + 1) * P], w2s[:, :], start=True, stop=True)
                    if c % 2 == 1:
                        ins.then_inc(m_mm, 1)
                pe.wait_ge(v_ready, b * 4 + 2)
                for q in range(NQ):
                    if q >= 2:
                        pe.wait_ge(acc_read, b * (3 * NQ) + NQ + (q - 1))
                    for i in range(CB):
                        ins = vec_part(acc[q % 2][:, i // 2, :], (i % 2) * 2 * D, CB * q + i, range(NB))
                        if i == CB - 1:
                            ins.then_inc(acc_done, 1)
                        if q >= 1 and i == 1:
                            cat_transposed(b, q - 1)
                        if q >= 1 and i == 2:
                            gates(b, q - 1)
                cat_transposed(b, NQ - 1)
                gates(b, NQ - 1)

            def cat_transposed(b, q):
                pe.wait_ge(msg_done, b * NQ + (q + 1))
                for i in range(CB):
                    ins = pe.transpose(tp[:, q % 2, i * P:(i + 1) * P], cat[:, CB * q + i, 0:2 * C], ident[:, :])
                ins.then_inc(cat_t, 1)

            def gates(b, q):
                pe.wait_ge(cat_cp, b * NQ + (q + 1))
                if q >= 1:
                    pe.wait_ge(pre_done, b * NQ + q)
                for i in range(CB):
                    g = gate_ps[i // 2][:, i % 2, :]
                    pe.matmul(g, catT[:, i * P:(i + 1) * P], wcat[:, :], start=True, stop=False)
                    ins = pe.matmul(g, ones16[0:C, :], bias2[:, :], start=False, stop=True)
                ins.then_inc(gate_mm, 1)

            def layer3(b, follow):
                pe.wait_ge(acc_read, b * (3 * NQ) + NQ + (NQ - 1))
                stay_warm(acc[0][:, 0, :], WARM[1])
                pe.wait_ge(v_ready, b * 4 + 4)

                def block_part(i, k):
                    q = i // CB
                    if q >= 2 and i % CB == 0 and k == 0:
                        pe.wait_ge(acc_read, b * (3 * NQ) + 2 * NQ + (q - 1))
                    ins = vec_part(acc[q % 2][:, (i % CB) // 2, :], (i % 2) * 2 * D, i, range(CB * k, CB * k + CB))
                    if i % CB == CB - 1 and k == NQ - 1:
                        ins.then_inc(acc_done, 1)

                for k in range(NQ):
                    block_part(0, k)
                for i in range(NB):
                    if follow and i == HT_AT:
                        pe.wait_ge(acc_read, b * (3 * NQ) + 2 * NQ + 3)
                        h_transposed(b + 1, 1)
                    if follow:
                        a_step(b + 1, i, True, (lambda k: block_part(i + 1, k)) if i + 1 < NB else None)
                    elif i + 1 < NB:
                        for k in range(NQ):
                            block_part(i + 1, k)

            pe.wait_ge(sig_done, B * NCH)
            h_transposed(0, 1)
            with pe.Fori(0, B - 1) as b:
                layer1(b)
                layer2(b)
                layer3(b, True)
            layer1(B - 1)
            layer2(B - 1)
            layer3(B - 1, False)

            pe.wait_ge(f_step, F_SUMS)
            pe.matmul(tp[0:C, 0, 0:1], bn_sum[:, 0, :], onesf[:, 0:1], start=True, stop=True)
            pe.matmul(tp[0:C, 0, 1:2], bn_sum[:, 1, :], onesf[:, 0:1], start=True, stop=True).then_inc(f_mm, 1)
            pe.wait_ge(f_step, F_FOLD)
            pe.wait_ge(w3_in, 32)
            pe.wait_ge(e_set, 2)
            pe.matmul(tp[0:D, 1, 0:C], fold, w3s, start=True, stop=False)
            pe.matmul(tp[0:D, 1, 0:C], e_last, b3row, start=False, stop=True).then_inc(f_mm, 1)
            pe.wait_ge(f_step, F_ALL)
            def final_transposed(t, c):
                s, q = c // NQ, c % NQ
                if q == 0:
                    pe.wait_ge(fin_in[s], t * 32 + 32)
                for i in range(CB):
                    ins = pe.transpose(tp[0:D, c % 2, i * P:(i + 1) * P], fin_v[s][:, CB * q + i, :], ident[:, :])
                ins.then_inc(f_vt, 1)

            stay_warm(acc[0][:, 0, :], WARM[3])
            with pe.Fori(0, B // FIN) as t:
                final_transposed(t, 0)
                for c in range(FIN * NQ):
                    if c + 1 < FIN * NQ:
                        final_transposed(t, c + 1)
                    pe.wait_ge(f_vtcp, t * (FIN * NQ) + (c + 1))
                    if c >= 2:
                        pe.wait_ge(f_y, t * (FIN * NQ) + (c - 1))
                    for i in range(CB):
                        ins = pe.matmul(acc[c % 2][:, 0, i * C:(i + 1) * C], fin_vt[c % 2][0:D, i * P:(i + 1) * P],
                                        wfin, start=True, stop=True)
                    ins.then_inc(f_out, 1)
                pe.wait_ge(f_y, t * (FIN * NQ) + FIN * NQ)

        @block.scalar
        def _(act):
            def k_sig(b, ck):
                w = (min(CB, chunks[ck][0] + 1 - CB * chunks[ck][1])) * P
                act.wait_ge(slog_done, b * NCH + (ck + 1))
                if not known(b, ck - 1):
                    act.wait_ge(kf_done, b * NCH + (ck - 1))
                act.activation(s_sig_b[:, ck % 2, 0:w], s_ps[:, ck % 2, 0:w], ACT.Sigmoid,
                               scale=1.0 / (U_SCALE * U_SCALE)).then_inc(sig_done, 1)

            def k_hi(b, ck):
                n, k = chunks[ck]
                m0, m1 = CB * k, min(CB * k + CB, n + 1)
                act.wait_ge(kf_done, b * NCH + (ck + 1))
                if not isinstance(b, int):
                    act.wait_ge(y_done, (b - 1) * NB + (n + 1))
                act.activation(mat[:, n, m0:m1, 0, :],
                               k_f32_b[:, ck % 2, 0:(m1 - m0) * P].rearrange("p (i c) -> p i c", c=P),
                               ACT.Copy).then_inc(khi_done, 1)

            def k_up(b, ck):
                n, k = chunks[ck]
                off, u = off_diag[ck], up_index[ck]
                if off <= 0 or u % 2 == 1:
                    return
                act.wait_ge(kup_t, b * NUP + (u + 1))
                act.activation(mat[:, CB * k:CB * k + off, n, :, :],
                               k_ps[u % 2][:, 0:off * 2 * P].rearrange("p (m s c) -> p m s c", s=2, c=P),
                               ACT.Copy).then_inc(kup_done[0], 1)

            def k_batch(b):
                for ck in range(NCH + LATE + 1):
                    if ck < NCH:
                        k_sig(b, ck)
                    if ck >= LATE + 1:
                        k_up(b, ck - LATE - 1)
                    if 1 <= ck <= NCH:
                        k_hi(b, ck - 1)
                for half in range(2):
                    s = slice(8 * half, 8 * half + 8)
                    act.wait_ge(dh_done, b * 2 + (half + 1))
                    act.activation(vec[:, s, 0:C], tmp[:, s, 0:C], ACT.Copy, scale=VEC_SCALE).then_inc(v0_hi, 1)

            k_batch(0)
            with act.Fori(1, B) as b:
                k_batch(b)

            def a_hi(b, c, wide):
                i, k = c // NQ, c % NQ
                act.wait_ge(a2t_done, b * TCH + (c + 1))
                act.activation(mat[:, CB * k:CB * k + CB, i, 0, :],
                               t_bank(c, wide).rearrange("p (j c) -> p j c", c=P), ACT.Copy,
                               scale=MAT_SCALE).then_inc(ahi_done, 1)

            for c in range(TCH):
                a_hi(0, c, False)

            def h_parts(b, layer, half):
                src, ready = (h_att, hatt_ready) if layer == 1 else (h, h_ready)
                act.wait_ge(ready, b * 2 + (half + 1))
                s = slice(8 * half, 8 * half + 8)
                act.activation(hs[:, s, 0:C], src[:, s, :], ACT.Copy).then_inc(hs_hi, 1)

            def h_copy(b, layer):
                for half in range(2):
                    act.wait_ge(ht_t, (b * 2 + (layer - 1)) * 2 + (half + 1))
                    act.activation(hT[:, half * 8 * P:(half + 1) * 8 * P], hT_ps[layer - 1][half], ACT.Copy).then_inc(ht_cp, 1)

            def layer1(b):
                for c in range(NQ):
                    act.wait_ge(s1_mm, b * NQ + (c + 1))
                    act.activation(s1row[:, c * 512:(c + 1) * 512], s1_ps[c], ACT.Copy,
                                   scale=1.0 / W_SCALE).then_inc(s1_cp, 1)
                act.wait_ge(coef_in, b + 1)
                act.activation(coef[:, :, :], coef[:, :, :], ACT.Exp, scale=1.0 / W_SCALE).then_inc(coef_done, 1)
                for half in range(2):
                    for t in range(2):
                        act.wait_ge(bw_ready, b * 4 + (2 * half + t + 1))
                        if half == 0 and t == 1:
                            act.wait_ge(v3_out, b * 16 + 16)
                        act.activation((vec, vec_d)[t][:, 8 * half:8 * half + 8, 0:D], tmp[:, 8 * t:8 * t + 8, :],
                                       ACT.Copy).then_inc(bw_hi, 1)
                for g in range(TCH):
                    q, j = g // NB, g % NB
                    if g >= RING:
                        act.wait_ge(g_used, b * TCH + (g - RING + 1))
                    act.activation(large_b[:, g % RING, :], s1row[:, q * 512:(q + 1) * 512], ACT.Relu,
                                   bias=s2st[:, j:j + 1], scale=STEEP).then_inc(pos_done, 1)
                    if q >= 1 and j == 5:
                        elu(b, q - 1)
                elu(b, NQ - 1)

            def elu(b, q):
                act.wait_ge(elu_in, b * NQ + (q + 1))
                act.activation(t_elu, t_elu, ACT.Exp).then_inc(elu_exp, 1)

            def layer2(b):
                for half in range(2):
                    h_parts(b, 2, half)
                h_copy(b, 2)
                for c in range(NQ):
                    act.wait_ge(m1_mm, b * NQ + (c + 1))
                    src = acc[0][0:C, c, :] if c < 2 else acc[1][0:C, 0, :] if c == 2 else tp[0:C, 0, :]
                    act.activation(m1T[0:C, c * 512:(c + 1) * 512], src, ACT.Relu, bias=b1s[:, 0:1],
                                   scale=1.0 / W_SCALE).then_inc(m1_cp, 1)
                for half in range(2):
                    s = slice(8 * half, 8 * half + 8)
                    act.wait_ge(m_sum, b * 2 + (half + 1))
                    act.activation(vec[:, s, 0:C], tmp[:, s, 0:C], ACT.Relu, scale=VEC_SCALE).then_inc(v_hi, 1)

                def gate_copies(q):
                    act.wait_ge(cat_t, b * NQ + (q + 1))
                    if q >= 1:
                        act.wait_ge(gate_mm, b * NQ + q)
                    act.activation(catT, tp[:, q % 2, :], ACT.Copy).then_inc(cat_cp, 1)
                    act.wait_ge(gate_mm, b * NQ + (q + 1))
                    if q >= 1:
                        act.wait_ge(gru_done, b * NQ + q)
                    for i in range(2):
                        ins = act.activation(t_rz[:, 2 * i:2 * i + 2, :], gate_ps[i][:, :, 0:2 * C], ACT.Tanh, scale=0.5)
                    ins.then_inc(rz_done, 1)

                def n_gate(q):
                    act.wait_ge(pre_done, b * NQ + (q + 1))
                    act.activation(t_n, t_pre, ACT.Tanh).then_inc(n_done, 1)

                for q in range(NQ):
                    if q >= 1:
                        gate_copies(q - 1)
                    act.wait_ge(msg_in, b * NQ + (q + 1))
                    act.activation(cat[:, CB * q:CB * q + CB, 0:C], msum[:, :, 0:C], ACT.Relu,
                                   scale=UNSCALE).then_inc(msg_done, 1)
                    if q >= 1:
                        n_gate(q - 1)
                gate_copies(NQ - 1)
                n_gate(NQ - 1)

            def layer3(b, follow):
                for half in range(2):
                    s = slice(8 * half, 8 * half + 8)
                    act.wait_ge(m3_in, b * 2 + (half + 1))
                    act.activation(vec[:, s, 0:D], tmp[:, s, :], ACT.Copy, scale=VEC_SCALE).then_inc(v_hi, 1)
                if follow:
                    for c in range(TCH):
                        a_hi(b + 1, c, True)
                        if c == PREP_AT[3] + 3:
                            for half in range(2):
                                h_parts(b + 1, 1, half)
                        if c == HT_AT * NQ:
                            h_copy(b + 1, 1)

            for half in range(2):
                h_parts(0, 1, half)
            h_copy(0, 1)
            with act.Fori(0, B - 1) as b:
                layer1(b)
                layer2(b)
                layer3(b, True)
            layer1(B - 1)
            layer2(B - 1)
            layer3(B - 1, False)

            def final_copy(t, c):
                act.wait_ge(f_vt, t * (FIN * NQ) + (c + 1))
                act.activation(fin_vt[c % 2][0:D, :], tp[0:D, c % 2, :], ACT.Copy).then_inc(f_vtcp, 1)

            with act.Fori(0, B // FIN) as t:
                final_copy(t, 0)
                for c in range(FIN * NQ):
                    if c + 1 < FIN * NQ:
                        final_copy(t, c + 1)
                    act.wait_ge(f_out, t * (FIN * NQ) + (c + 1))
                    if c >= 2:
                        act.wait_ge(f_y, t * (FIN * NQ) + (c - 1))
                    act.activation(fin_r[c % 2], acc[c % 2][:, 0, 0:CB * C], ACT.Relu, scale=0.99).then_inc(f_relu, 1)

        @block.gpsimd
        def _(pool):
            pool.memset(g_n, 0.0).then_inc(set_pool, 1)
            pool.memset(ident[:, :], 0.0).then_inc(set_pool, 1)
            pool.wait_ge(set_pool, 2)
            pool.affine_select(out=ident[:, :], in_=ident[:, :], compare_op=ALU.not_equal, fill=1.0, base=0,
                               pattern=[[-1, P]], channel_multiplier=1).then_inc(set_pool, 1)
            pool.memset(onesf[:, :], 1.0).then_inc(set_pool, 1)
            pool.memset(zeros16[:, :], 0.0).then_inc(set_pool, 1)
            pool.memset(ones16[:, :], 1.0).then_inc(set_pool, 1)
            pool.memset(bn_sum[:, :, :], 0.0).then_inc(set_pool, 1)
            pool.memset(bias2[:, :], 0.0).then_inc(set_pool, 1)
            pool.memset(cat[:, :, 2 * C:2 * C + 1], 1.0).then_inc(set_pool, 1)
            pool.memset(rsum[:, :, :], 0.0).then_inc(set_pool, 1)
            pool.memset(small[:, 3:4], 0.0).then_inc(v3_out, 16)

            with pool.Fori(0, B) as b:
                for ck, (n, k) in enumerate(chunks):
                    m0, m1 = CB * k, min(CB * k + CB, n + 1)
                    pool.wait_ge(khi_done, b * NCH + (ck + 1))
                    pool.tensor_tensor(mat[:, n, m0:m1, 1, :],
                                       k_f32_b[:, ck % 2, 0:(m1 - m0) * P].rearrange("p (i c) -> p i c", c=P),
                                       mat[:, n, m0:m1, 0, :], ALU.subtract).then_inc(klo_done, 1)
            with pool.Fori(0, B) as b:
                for g in range(TCH):
                    if g % 2 < 1:
                        pool.wait_ge(g1_done, b * TCH + (g + 1))
                        pool.tensor_tensor(neg_b[:, g % RING, :], neg_b[:, g % RING, :], pos_b[:, g % RING, :],
                                           ALU.subtract).then_inc(g2_pool, 1)
                pool.wait_ge(x3_ready, b * 2 + 2)
                pool.tensor_tensor(h_sq, h, h, ALU.mult).then_inc(sq_done, 1)
                for q in range(NQ):
                    pool.wait_ge(acc_read, b * (3 * NQ) + 2 * NQ + (q + 1))
                    pool.tensor_tensor(msum, msum, sqd[:, CB * q:CB * q + CB].unsqueeze(2).to_broadcast([P, CB, D]),
                                       ALU.mult).then_inc(v3_step, 1)
                    pool.wait_ge(v3_step, b * NQ + (q + 1))
                    pool.tensor_tensor(vout[:, CB * q:CB * q + CB, :], msum, h1[:, CB * q:CB * q + CB, :],
                                       ALU.add).then_inc(v3_done, 1)
            pool.wait_ge(x3_ready, 2 * B)
            pool.memset(e_last[:, 0:C], 0.0).then_inc(e_set, 1)
            pool.memset(e_last[:, C:D], 1.0).then_inc(e_set, 1)

        @block.vector
        def _(dve):
            def centred(ch, src, dst, blocks):
                s = slice(*blocks)
                wide = [P, blocks[1] - blocks[0], C]
                src, sq, xc = src[:, s, :], dst[:, s, :], tmp[:, s, 0:C]
                mean, var = st[:, 0, s], st[:, 1, s]
                ch.link(dve.tensor_reduce(mean, src, AX, ALU.add))
                ch.link(dve.tensor_scalar(mean, mean, -1.0 / C, None, ALU.mult))
                ch.link(dve.tensor_tensor(xc, src, mean.unsqueeze(2).to_broadcast(wide), ALU.add))
                ch.link(dve.tensor_tensor(sq, xc, xc, ALU.mult))
                ch.link(dve.tensor_reduce(var, sq, AX, ALU.add))
                ch.link(dve.tensor_scalar(var, var, 1.0 / C, LN_EPS, ALU.mult, ALU.add))

            def scaled(dst, ready, blocks):
                s = slice(*blocks)
                wide = [P, blocks[1] - blocks[0], C]
                dve.scalar_tensor_tensor(out=dst[:, s, :], in0=tmp[:, s, 0:C], scalar=0.0,
                                         in1=rstd[:, s].unsqueeze(2).to_broadcast(wide),
                                         op0=ALU.max, op1=ALU.mult).then_inc(ready, 1)

            def layer_norm(ch, src, dst, ready, blocks=(0, NB)):
                s = slice(*blocks)
                centred(ch, src, dst, blocks)
                rsqrt(ch, dve, rstd[:, s], var[:, s], tn[:, s])
                scaled(dst, ready, blocks)

            dve.wait_ge(set_pool, SET_POOL)
            dve.wait_ge(w_in, 16 * W_DMAS)
            ch = Chain(dve, set_dve, 0)
            u16 = tmp[:, :, R:2 * R]
            ch.link(dve.tensor_copy(ident16[:, :], ident[:, :]))
            assert ch.n == SET_IDENT
            ch.link(dve.tensor_scalar(u16, tmp[:, :, 0:R], U_SCALE, None, ALU.mult))
            ch.link(dve.tensor_copy(u_nat[:, 0, :, 0:R], u16))
            ch.link(dve.tensor_tensor(u_nat[:, 0, :, 2 * R:3 * R], u16, u_nat[:, 0, :, 0:R], ALU.subtract))
            ch.do(dve.tensor_copy(u_nat[:, 0, :, R:2 * R], u_nat[:, 0, :, 0:R]))
            ch.do(dve.tensor_copy(u_nat[:, 1, :, 0:R], u_nat[:, 0, :, 0:R]))
            ch.do(dve.tensor_copy(u_nat[:, 1, :, R:2 * R], u_nat[:, 0, :, 2 * R:3 * R]))
            ch.do(dve.tensor_copy(u_nat[:, 1, :, 2 * R:3 * R], u_nat[:, 0, :, 0:R]))
            ch.do(dve.tensor_tensor(bsum[:, 0:2 * C], bih[:, 0:2 * C], bhh[:, 0:2 * C], ALU.add))
            ch.do(dve.tensor_copy(bsum[:, 2 * C:3 * C], bih[:, 2 * C:3 * C]))
            ch.link(dve.tensor_copy(bsum[:, 3 * C:4 * C], bhh[:, 2 * C:3 * C]))
            ch.link(dve.tensor_copy(bhi, bsum))
            ch.link(dve.tensor_tensor(blo, bsum, bhi, ALU.subtract))
            ch.do(dve.tensor_copy(bias2[0:1, :], bhi[0:1, :]))
            ch.do(dve.tensor_copy(bias2[32:33, :], blo[32:33, :]))
            dve.wait_ge(set_pe, 1)
            ch.do(dve.tensor_copy(waT, tp[0:C, 0, 0:P]))
            assert ch.n == SET_WAT, ch.n
            ch.do(dve.tensor_copy(wcat[:, 0:P], tp[:, 0, P:2 * P]))
            ch.do(dve.tensor_copy(wcat[:, P:2 * P], tp[:, 0, 2 * P:3 * P]))
            dve.wait_ge(set_pe, 2)
            ch.link(dve.tensor_copy(wa[:, C:C + 2], tp[:, 1, 0:2]))
            ch.link(dve.tensor_scalar(wa_s, wa, W_SCALE, None, ALU.mult))
            ch.link(dve.tensor_copy(wa_hi[:, :], wa_s))
            ch.do(dve.tensor_tensor(wa_lo[:, :], wa_s, wa_hi[:, :], ALU.subtract))
            ch.link(dve.tensor_scalar(w1s, w1s, W_SCALE, None, ALU.mult))
            ch.link(dve.tensor_copy(w1_hi[:, :], w1s))
            ch.do(dve.tensor_tensor(w1_lo[:, :], w1s, w1_hi[:, :], ALU.subtract))
            ch.do(dve.tensor_copy(wa1_hi[:, :], wa_hi[:, C:C + 1].to_broadcast([P, P])))
            ch.link(dve.tensor_copy(wa1_lo[:, :], wa_lo[:, C:C + 1].to_broadcast([P, P])))
            assert ch.n == SET_WA, ch.n
            dve.wait_ge(set_pe, 3)
            for o, dst in enumerate((u_st, u_mv)):
                ch.do(dve.tensor_copy(dst.rearrange("p (a c) -> p a c", a=2),
                                      acc[o][0:UK, 0:2, :].bitcast(F16)))
            assert ch.n == SET_DVE, ch.n
            ch.settle()

            def k_sum(b, ck):
                n, k = chunks[ck]
                w = min(CB, n + 1 - CB * k) * P
                if k == 0:
                    row_landed(dve, b, n)
                dve.wait_ge(at_done, b * NCH + (ck + 1))
                if not known(b, ck - 1):
                    dve.wait_ge(kf_done, b * NCH + (ck - 1))
                dve.tensor_tensor(a_sum_b[:, ck % 2, 0:w], rows[:, n % 2, CB * k * P:CB * k * P + w],
                                  tp[:, ck % 2, 0:w], ALU.add).then_inc(asum_done, 1)

            def k_mul(b, ck):
                n, k = chunks[ck]
                w = min(CB, n + 1 - CB * k) * P
                dve.wait_ge(sig_done, b * NCH + (ck + 1))
                dve.wait_ge(asum_done, b * NCH + (ck + 1))
                if not known(b, ck - 1):
                    dve.wait_ge(klo_done, b * NCH + (ck - 1))
                dve.scalar_tensor_tensor(out=k_f32_b[:, ck % 2, 0:w], in0=a_sum_b[:, ck % 2, 0:w],
                                         scalar=0.5 * MAT_SCALE, in1=s_sig_b[:, ck % 2, 0:w], op0=ALU.mult,
                                         op1=ALU.mult, accum_out=rsum[:, n, k:k + 1]).then_inc(kf_done, 1)

            def k_up(b, ck):
                n, k = chunks[ck]
                off, u = off_diag[ck], up_index[ck]
                if off <= 0 or u % 2 == 0:
                    return
                dve.wait_ge(kup_t, b * NUP + (u + 1))
                dve.tensor_copy(mat[:, CB * k:CB * k + off, n, :, :],
                                k_ps[u % 2][:, 0:off * 2 * P].rearrange("p (m s c) -> p m s c", s=2, c=P)) \
                    .then_inc(kup_done[1], 1)

            def y_post(b, q):
                dve.wait_ge(y_done, b * NB + CB * (q + 1))
                if q == 0:
                    dve.wait_ge(xr_in, b * 16 + 16)
                dve.tensor_reduce(yq[:, :, :], y_ps.rearrange("p (i s c) -> p i c s", s=2, c=C), AX,
                                  ALU.add).then_inc(y_read, 1)
                dve.wait_ge(y_read, b * NQ + (q + 1))
                dve.tensor_tensor(yq[:, :, :], yq[:, :, :],
                                  dscale[:, CB * q:CB * q + CB].unsqueeze(2).to_broadcast([P, CB, C]),
                                  ALU.mult).then_inc(y_step, 1)
                dve.wait_ge(y_step, b * NQ + (q + 1))
                dve.tensor_tensor(xt[:, CB * q:CB * q + CB, :], xt[:, CB * q:CB * q + CB, :], yq[:, :, :],
                                  ALU.add).then_inc(x1_done, 1)
                dve.wait_ge(x1_done, b * NQ + (q + 1))

            def k_batch(b, last):
                ln = Chain(dve, ln0_step, b * (6 + LN_STEPS))
                for ck in range(NCH + LATE + 1):
                    n = chunks[ck][0] if ck < NCH else NB
                    if last is not None and n % CB == 0 and n > 0 and (ck == NCH or n < NB and chunks[ck][1] == 0):
                        y_post(last, n // CB - 1)
                    if ck < NCH:
                        k_sum(b, ck)
                    if 1 <= ck <= NCH:
                        k_mul(b, ck - 1)
                    if ck >= LATE + 1:
                        k_up(b, ck - LATE - 1)
                    if ck < NCH and chunks[ck][1] == 0:
                        if n == 9:
                            dve.wait_ge(x0_in, b * 16 + 16)
                            centred(ln, h, h, (0, 8))
                        if n == 10:
                            centred(ln, h, h, (8, NB))
                        if n == 11:
                            rsqrt(ln, dve, rstd, var, tn)
                        if n == 12:
                            scaled(h, h0_ready, (0, 8))
                            scaled(h, h0_ready, (8, NB))
                assert ln.n == 6 + LN_STEPS, ln.n
                ch = Chain(dve, deg_step, b * DEG_STEPS)
                dve.wait_ge(kf_done, b * NCH + NCH)
                ch.link(dve.tensor_reduce(deg, rsum[:, :, :], AX, ALU.add))
                dve.wait_ge(deg_done, b + 1)
                dve.tensor_tensor(deg, deg, deg_ps, ALU.add).then_inc(deg_read, 1)
                dve.wait_ge(deg_read, b + 1)
                dve.wait_ge(h0_ready, b * 2 + 2)
                ch.link(dve.tensor_scalar(deg, deg, 1.0 / MAT_SCALE, DEG_EPS, ALU.mult, ALU.max))
                rsqrt(ch, dve, dinv, deg, tn)
                ch.do(dve.tensor_scalar(dscale, dinv, wsc[:, 0:1], UNSCALE, ALU.mult, ALU.mult))
                for s in (slice(0, 8), slice(8, NB)):
                    dve.tensor_tensor(tmp[:, s, 0:C], h[:, s, :], dinv[:, s].unsqueeze(2).to_broadcast([P, 8, C]),
                                      ALU.mult).then_inc(dh_done, 1)
                for half in range(2):
                    s = slice(8 * half, 8 * half + 8)
                    dve.wait_ge(v0_hi, b * 2 + (half + 1))
                    ins = dve.scalar_tensor_tensor(out=vec[:, s, C:2 * C], in0=tmp[:, s, 0:C], scalar=VEC_SCALE,
                                                   in1=vec[:, s, 0:C], op0=ALU.mult, op1=ALU.subtract)
                ins.then_inc(v0_done, 1)
                assert ch.n == DEG_STEPS, ch.n

            k_batch(0, None)
            with dve.Fori(1, B) as b:
                k_batch(b, b - 1)

            def a_lo(b, c, wide):
                i, k = c // NQ, c % NQ
                dve.wait_ge(ahi_done, b * TCH + (c + 1))
                dve.scalar_tensor_tensor(out=mat[:, CB * k:CB * k + CB, i, 1, :],
                                         in0=t_bank(c, wide).rearrange("p (j c) -> p j c", c=P), scalar=MAT_SCALE,
                                         in1=mat[:, CB * k:CB * k + CB, i, 0, :], op0=ALU.mult,
                                         op1=ALU.subtract).then_inc(alo_done, 1)

            for c in range(TCH):
                if c % (NQ * CB) == NQ * (CB - 1):
                    y_post(B - 1, c // (NQ * CB))
                a_lo(0, c, False)

            def wide(v, q=None):
                if q is None:
                    return v.unsqueeze(2).to_broadcast([P, NB, C])
                return v[:, CB * q:CB * q + CB].unsqueeze(2).to_broadcast([P, CB, C])

            def low_part(b, layer, half):
                src = h_att if layer == 1 else h
                s = slice(8 * half, 8 * half + 8)
                dve.wait_ge(hs_hi, (b * 2 + (layer - 1)) * 2 + (half + 1))
                dve.tensor_tensor(hs[:, s, C:2 * C], src[:, s, :], hs[:, s, 0:C], ALU.subtract).then_inc(hs_lo, 1)

            def prepare(b, part, ch):
                if part == 0:
                    dve.wait_ge(x1_in, b * 16 + 16)
                if part < 2:
                    centred(ch, xt, h_att, (8 * part, 8 * part + 8))
                if part == 2:
                    rsqrt(ch, dve, rstd, var, tn)
                if part == 3:
                    for half in range(2):
                        scaled(h_att, hatt_ready, (8 * half, 8 * half + 8))
                if part == 4:
                    for half in range(2):
                        low_part(b, 1, half)
                    assert ch.n == 6 + LN_STEPS

            def layer1(b, ch):
                s1, s2 = s12_ps[:, :, 0], s12_ps[:, :, 1]
                dve.wait_ge(wh_mm, b + 1)
                dve.tensor_reduce(small[:, 0:1], s2, AX, ALU.max).then_inc(mx_in, 1)
                dve.wait_ge(mx_t, b + 1)
                dve.tensor_reduce(small[0:1, 1:2], mx_ps[0:1, 0:P], AX, ALU.max).then_inc(mx_r, 1)
                dve.wait_ge(mx_b, b + 1)
                ch.link(dve.tensor_copy(small[:, 2:3], mx_ps[:, P:P + 1]))
                top = small[:, 2:3]
                ch.link(dve.tensor_scalar(var, s1, top, None, ALU.add))
                ch.link(dve.scalar_tensor_tensor(out=tn, in0=var, scalar=0.2, in1=var, op0=ALU.mult, op1=ALU.max))
                ch.do(dve.tensor_tensor(coef[:, 0, :], var, tn, ALU.subtract))
                ch.do(dve.scalar_tensor_tensor(out=coef[:, 1, :], in0=var, scalar=0.2, in1=tn, op0=ALU.mult,
                                               op1=ALU.subtract))
                ch.do(dve.tensor_scalar(coef[:, 2, :], s2, top, None, ALU.subtract))
                ch.do(dve.tensor_scalar(s2st[:, :], s2, STEEP / W_SCALE, None, ALU.mult))
                ch.settle(1)
                dve.tensor_scalar(coef[:, 3, :], coef[:, 2, :], 0.2, None, ALU.mult).then_inc(coef_in, 1)
                dve.wait_ge(coef_done, b + 1)
                ch.link(dve.tensor_scalar(coef[:, 2:4, :], coef[:, 2:4, :], ATT_SCALE / W_SCALE, None, ALU.mult))
                for half in range(2):
                    s = slice(8 * half, 8 * half + 8)
                    for t in range(2):
                        w, part = coef[:, 2 + t, s], tmp[:, 8 * t:8 * t + 8, :]
                        if half == 1:
                            dve.wait_ge(b_ready, b * 2 + 1)
                        ins = dve.tensor_tensor(part[:, :, 0:C], wh_ps[:, s, :],
                                                w.unsqueeze(2).to_broadcast([P, 8, C]), ALU.mult)
                        if half == 1 and t == 1:
                            ins.then_inc(wh_read, 1)
                        dve.tensor_scalar(part[:, :, C:D], w.unsqueeze(2), W_SCALE, None, ALU.mult).then_inc(bw_ready, 1)
                    for t in range(2):
                        v = (vec, vec_d)[t]
                        dve.wait_ge(bw_hi, b * 4 + (2 * half + t + 1))
                        ins = dve.tensor_tensor(v[:, s, D:2 * D], tmp[:, 8 * t:8 * t + 8, :], v[:, s, 0:D], ALU.subtract)
                    ins.then_inc(b_ready, 1)
                dve.wait_ge(s1_cp, b * NQ + NQ)

                def neighbours(g):
                    q, j = g // NB, g % NB
                    if g >= RING:
                        dve.wait_ge(g_used, b * TCH + (g - RING + 1))
                    dve.tensor_scalar(neg_b[:, g % RING, :].rearrange("p (i c) -> p i c", c=P),
                                      mat[:, j, CB * q:CB * q + CB, 0, :], 0.0, None, ALU.is_gt).then_inc(nb_done, 1)

                def positive(g):
                    dve.wait_ge(nb_done, b * TCH + (g + 1))
                    dve.wait_ge(pos_done, b * TCH + (g + 1))
                    dve.tensor_tensor(pos_b[:, g % RING, :], neg_b[:, g % RING, :], large_b[:, g % RING, :],
                                      ALU.min).then_inc(g1_done, 1)

                def negative(g):
                    if g % 2 == 1:
                        dve.wait_ge(g1_done, b * TCH + (g + 1))
                        dve.tensor_tensor(neg_b[:, g % RING, :], neg_b[:, g % RING, :], pos_b[:, g % RING, :],
                                          ALU.subtract).then_inc(g2_dve, 1)

                def post(q):
                    a = acc[q % 2]
                    dve.wait_ge(acc_done, b * (3 * NQ) + (q + 1))
                    for bank in range(3):
                        k = min(3, 2 * CB - 3 * bank)
                        ins = dve.tensor_reduce(nsum[:, 3 * bank:3 * bank + k, :],
                                                a[:, bank, 0:k * 2 * D].rearrange("p (i s c) -> p i c s", s=2, c=D),
                                                AX, ALU.add)
                    ins.then_inc(acc_read, 1)
                    dve.wait_ge(acc_read, b * (3 * NQ) + (q + 1))
                    for t in range(2):
                        ch.do(dve.tensor_tensor(nwt[:, CB * t:CB * t + CB, :], nsum[:, CB * t:CB * t + CB, :],
                                                coef[:, t, CB * q:CB * q + CB].unsqueeze(2).to_broadcast([P, CB, D]),
                                                ALU.mult))
                    ch.settle()
                    ch.link(dve.tensor_tensor(nsum[:, 0:CB, :], nwt[:, 0:CB, :], nwt[:, CB:2 * CB, :], ALU.add))
                    den = tn[:, 0:CB]
                    ch.link(dve.reciprocal(den.unsqueeze(2), nsum[:, 0:CB, C:D]))
                    ch.link(dve.tensor_tensor(yq[:, :, :], nsum[:, 0:CB, 0:C],
                                              den.unsqueeze(2).to_broadcast([P, CB, C]), ALU.mult))
                    dve.tensor_scalar(t_elu, yq[:, :, :], 0.0, None, ALU.min).then_inc(elu_in, 1)
                    return q

                def post_end(q):
                    dve.wait_ge(elu_exp, b * NQ + (q + 1))
                    ch.link(dve.scalar_tensor_tensor(out=yq[:, :, :], in0=yq[:, :, :], scalar=0.0, in1=t_elu,
                                                     op0=ALU.max, op1=ALU.add))
                    x_q = xt[:, CB * q:CB * q + CB, :]
                    ch.link(dve.scalar_tensor_tensor(out=x_q, in0=yq[:, :, :], scalar=-1.0, in1=x_q,
                                                     op0=ALU.add, op1=ALU.add))

                for g in range(TCH + 2):
                    if g < TCH:
                        neighbours(g)
                    if 1 <= g <= TCH:
                        positive(g - 1)
                    if g >= 2:
                        negative(g - 2)
                    if NB <= g < TCH and g % NB == 4:
                        post(g // NB - 1)
                    if NB <= g < TCH and g % NB == 8:
                        post_end(g // NB - 1)
                centred(ch, xt, h, (0, 8))
                post(NQ - 1)
                post_end(NQ - 1)

            def values(b, ch, half):
                s = slice(8 * half, 8 * half + 8)
                ch.do(dve.tensor_tensor(tmp[:, s, 0:C], h[:, s, :], dinv[:, s].unsqueeze(2).to_broadcast([P, 8, C]),
                                        ALU.mult))
                dve.tensor_copy(tmp[:, s, C:D], dinv[:, s].unsqueeze(2)).then_inc(m3_in, 1)

            def layer2(b, ch):
                centred(ch, xt, h, (8, NB))
                rsqrt(ch, dve, rstd, var, tn)
                for half in range(2):
                    scaled(h, h_ready, (8 * half, 8 * half + 8))
                for half in range(2):
                    low_part(b, 2, half)
                ch.do(dve.memset(vec[:, :, C:D], VEC_SCALE))
                ch.do(dve.memset(vec[:, :, 2 * D - 1:2 * D], 0.0))
                for half in range(2):
                    s = slice(8 * half, 8 * half + 8)
                    dve.wait_ge(m_mm, b * 2 + (half + 1))
                    dve.tensor_tensor(tmp[:, s, 0:C], m_ps[:, s, :], b2s[:, :].unsqueeze(1).to_broadcast([P, 8, C]),
                                      ALU.add).then_inc(m_sum, 1)
                for half in range(2):
                    s = slice(8 * half, 8 * half + 8)
                    dve.wait_ge(v_hi, b * 4 + (half + 1))
                    ch.link(dve.tensor_scalar(tmp[:, s, 0:C], tmp[:, s, 0:C], 0.0, VEC_SCALE, ALU.max, ALU.mult))
                    dve.tensor_tensor(vec[:, s, D:D + C], tmp[:, s, 0:C], vec[:, s, 0:C],
                                      ALU.subtract).then_inc(v_ready, 1)

                def message(q):
                    dve.wait_ge(acc_done, b * (3 * NQ) + NQ + (q + 1))
                    if q >= 1:
                        dve.wait_ge(msg_done, b * NQ + q)
                    for k in range(2):
                        ins = dve.tensor_reduce(msum[:, 2 * k:2 * k + 2, :],
                                                acc[q % 2][:, k, 0:4 * D].rearrange("p (i s c) -> p i c s", s=2, c=D),
                                                AX, ALU.add)
                    ins.then_inc(acc_read, 1)
                    dve.wait_ge(acc_read, b * (3 * NQ) + NQ + (q + 1))
                    dve.tensor_scalar(deg[:, CB * q:CB * q + CB].unsqueeze(2), msum[:, :, C:D], UNSCALE, None,
                                      ALU.mult).then_inc(msg_in, 1)

                def gru(q):
                    dve.wait_ge(rz_done, b * NQ + (q + 1))
                    for k in range(2):
                        s = slice(2 * k, 2 * k + 2)
                        ch.do(dve.scalar_tensor_tensor(out=t_w[:, s, :], in0=t_rz[:, s, 0:C], scalar=1.0,
                                                       in1=gate_ps[k][:, :, 3 * C:4 * C], op0=ALU.add, op1=ALU.mult))
                    ch.settle()
                    for k in range(2):
                        s = slice(2 * k, 2 * k + 2)
                        ins = dve.scalar_tensor_tensor(out=t_pre[:, s, :], in0=t_w[:, s, :], scalar=0.5,
                                                       in1=gate_ps[k][:, :, 2 * C:3 * C], op0=ALU.mult, op1=ALU.add)
                    ins.then_inc(pre_done, 1)

                def gru_end(q):
                    hq, xq = h[:, CB * q:CB * q + CB, :], xt[:, CB * q:CB * q + CB, :]
                    dve.wait_ge(n_done, b * NQ + (q + 1))
                    ch.link(dve.tensor_tensor(t_w, hq, t_n, ALU.subtract))
                    ch.link(dve.scalar_tensor_tensor(out=t_w, in0=t_rz[:, :, C:2 * C], scalar=1.0, in1=t_w,
                                                     op0=ALU.add, op1=ALU.mult))
                    ch.link(dve.scalar_tensor_tensor(out=t_w, in0=t_w, scalar=0.5, in1=t_n, op0=ALU.mult, op1=ALU.add))
                    dve.tensor_tensor(xq, xq, t_w, ALU.add).then_inc(gru_done, 1)

                for q in range(NQ):
                    if q >= 1:
                        gru(q - 1)
                    message(q)
                    if q >= 1:
                        gru_end(q - 1)
                    if q == 2:
                        dve.wait_ge(gru_done, b * NQ + 2)
                        centred(ch, xt, h, (0, 8))
                rsqrt(ch, dve, roots, var_deg, root_tmp)
                scaled(h, x3_ready, (0, 8))
                dve.wait_ge(x3_ready, b * 2 + 1)
                values(b, ch, 0)
                gru(NQ - 1)
                gru_end(NQ - 1)
                dve.wait_ge(gru_done, b * NQ + NQ)

            def layer3(b, ch, follow):
                def values_low(half):
                    s = slice(8 * half, 8 * half + 8)
                    dve.wait_ge(v_hi, b * 4 + 2 + (half + 1))
                    dve.scalar_tensor_tensor(out=vec[:, s, D:2 * D], in0=tmp[:, s, :], scalar=VEC_SCALE,
                                             in1=vec[:, s, 0:D], op0=ALU.mult, op1=ALU.subtract).then_inc(v_ready, 1)

                layer_norm(ch, xt, h, x3_ready, (8, NB))
                dve.wait_ge(x3_ready, b * 2 + 2)
                values(b, ch, 1)
                values_low(0)
                ch.link(dve.tensor_tensor(sqd, deg, dinv, ALU.mult))
                ch.link(dve.tensor_scalar(sqd, sqd, -UNSCALE, None, ALU.mult))
                values_low(1)
                dve.wait_ge(v_ready, b * 4 + 4)
                dve.wait_ge(sq_done, b + 1)
                ch.do(dve.tensor_reduce(bn_part[:, 0, :], h.rearrange("p i c -> p c i"), AX, ALU.add))
                ch.link(dve.tensor_reduce(bn_part[:, 1, :], h_sq.rearrange("p i c -> p c i"), AX, ALU.add))
                ch.link(dve.tensor_tensor(bn_sum[:, :, :], bn_sum[:, :, :], bn_part[:, :, :], ALU.add))

                def post(q):
                    dve.wait_ge(acc_done, b * (3 * NQ) + 2 * NQ + (q + 1))
                    if q >= 1:
                        dve.wait_ge(v3_done, b * NQ + q)
                    for k in range(2):
                        ins = dve.tensor_reduce(msum[:, 2 * k:2 * k + 2, :],
                                                acc[q % 2][:, k, 0:4 * D].rearrange("p (i s c) -> p i c s", s=2, c=D),
                                                AX, ALU.add)
                    ins.then_inc(acc_read, 1)

                if follow:
                    prep = Chain(dve, p_step, (b + 1) * (6 + LN_STEPS))
                    for c in range(TCH):
                        a_lo(b + 1, c, True)
                        if c in PREP_AT:
                            prepare(b + 1, PREP_AT.index(c), prep)
                        if c % (NQ * CB) == NQ * (CB - 1) + 1:
                            post(c // (NQ * CB))
                else:
                    for q in range(NQ):
                        post(q)

            def layers(b, follow):
                ch = Chain(dve, v_step, b * V_STEPS)
                layer1(b, ch)
                layer2(b, ch)
                layer3(b, ch, follow)
                assert ch.n == V_STEPS, ch.n

            ch = Chain(dve, p_step, 0)
            for part in range(5):
                prepare(0, part, ch)
            with dve.Fori(0, B - 1) as b:
                layers(b, True)
            layers(B - 1, False)

            ch = Chain(dve, f_step, 0)
            ch.link(dve.tensor_copy(small[:, 3:4], bn_sum[:, 0, 0:1]))
            assert ch.n == F_SUMS
            dve.wait_ge(f_mm, 1)
            mu, ex2, vr, rs, t1, sc, sh = (bnv[:, i:i + 1] for i in range(7))
            ch.link(dve.tensor_scalar(bnv[:, 0:2], tp[0:C, 0, 0:2], 1.0 / (B * N), None, ALU.mult))
            ch.link(dve.tensor_tensor(vr, mu, mu, ALU.mult))
            ch.link(dve.tensor_tensor(vr, ex2, vr, ALU.subtract))
            ch.link(dve.tensor_scalar(vr, vr, BN_EPS, None, ALU.add))
            rsqrt(ch, dve, rs, vr, t1)
            ch.link(dve.tensor_tensor(sc, gb[:, 0:1], rs, ALU.mult))
            ch.link(dve.tensor_tensor(t1, mu, sc, ALU.mult))
            ch.link(dve.tensor_tensor(sh, gb[:, 1:2], t1, ALU.subtract))
            ch.do(dve.tensor_scalar(fold[:, 0:C], ident[0:C, 0:C], sc, None, ALU.mult))
            ch.link(dve.tensor_copy(fold[:, C:D], sh))
            assert ch.n == F_FOLD, ch.n
            dve.wait_ge(f_mm, 2)
            ch.link(dve.tensor_copy(wfin, tp[0:D, 1, 0:C]))
            assert ch.n == F_ALL, ch.n
            with dve.Fori(0, B // FIN) as t:
                for s in range(FIN):
                    dve.wait_ge(fin_in[s], t * 32 + 32)
                    for q in range(NQ):
                        c = s * NQ + q
                        dve.wait_ge(f_relu, t * (FIN * NQ) + (c + 1))
                        dve.scalar_tensor_tensor(out=fin_y[c % 2], in0=acc[c % 2][:, 0, 0:CB * C], scalar=0.01,
                                                 in1=fin_r[c % 2], op0=ALU.mult, op1=ALU.add).then_inc(f_y, 1)
                        dve.wait_ge(f_y, t * (FIN * NQ) + (c + 1))
                        xq = fin_x[s][:, CB * q:CB * q + CB, :]
                        dve.tensor_tensor(xq, xq, fin_y[c % 2].rearrange("p (i c) -> p i c", c=C), ALU.add) \
                            .then_inc(f_add, 1)


_INS = ['x', 'adj', 'L0_gnn_U', 'L0_gnn_w_scale', 'L1_gnn_W', 'L1_gnn_a', 'L2_gnn_W1', 'L2_gnn_b1', 'L2_gnn_W2',
        'L2_gnn_b2', 'L2_gnn_W_ih', 'L2_gnn_b_ih', 'L2_gnn_W_hh', 'L2_gnn_b_hh', 'L3_gnn_gamma', 'L3_gnn_beta',
        'L3_gnn_W', 'L3_gnn_b']


def kernel(**inputs):
    import numpy as _np
    import concourse.bacc as _bacc
    from concourse import mybir as _mybir
    from concourse.bass_utils import run_bass_kernel_spmd as _run

    nc = _bacc.Bacc("TRN2", target_bir_lowering=False, num_devices=1)
    arrays, args = {}, []
    for name in _INS:
        a = _np.ascontiguousarray(inputs[name])
        arrays[f"in_{name}_dram"] = a
        args.append(nc.dram_tensor(f"in_{name}_dram", a.shape, _mybir.dt.from_np(a.dtype), kind="ExternalInput").ap())
    b, n, c = inputs["x"].shape
    out = nc.dram_tensor("out_0_dram", (b, n, c), _mybir.dt.float32, kind="ExternalOutput").ap()
    xs = nc.dram_tensor("x_scratch", (b, P, n // P, c), _mybir.dt.float32, kind="Internal").ap()
    vs = nc.dram_tensor("v_scratch", (b, P, n // P, c + 1), _mybir.dt.float32, kind="Internal").ap()
    gnn_kernel(nc, *args, out, xs, vs)
    r = _run(nc, [arrays], core_ids=[0])
    return r.results[0]["out_0_dram"]
```
